# Optimizing a Trainium2 kernel written in Bass

```python
import numpy as np
import jax
import jax.numpy as jnp

def _softmax(x, axis=-1):
    return jax.nn.softmax(x, axis=axis)

def _gelu(x):
    return jax.nn.gelu(x, approximate=True)

def _silu(x):
    return jax.nn.silu(x)

def _sigmoid(x):
    return jax.nn.sigmoid(x)

def _layernorm(x, axis=-1, eps=1e-05):
    m = jnp.mean(x, axis=axis, keepdims=True)
    v = jnp.var(x, axis=axis, keepdims=True)
    return (x - m) / jnp.sqrt(v + eps)

def _scatter_add(tgt, idx, src, axis=0):
    return tgt.at[idx].add(src)

def _segment_sum(src, seg, n):
    return jax.ops.segment_sum(src, seg, n)
kernel_name = 'mk_prb_d1_jaxref_r4_b81d77'

def setup_inputs(seed: int=0):
    np.random.seed(seed)
    _w = jnp.asarray

    def _L0_attn_setup():
        import jax, jax.numpy as jnp
        import numpy as np
        EPS = 1e-12
        HEADS = 16
        DIM_KEYS = 16
        DIM_VALUES = 64

        def l2norm(t):
            n = jnp.linalg.norm(t, axis=-1, keepdims=True)
            return t / jnp.maximum(n, EPS)

        def tanh_norm(t):
            n = jnp.linalg.norm(t, axis=-1, keepdims=True)
            return jnp.tanh(n) * (t / jnp.maximum(n, EPS))

        def split_heads(x, h):
            b, n, hd = x.shape
            return x.reshape(b, n, h, hd // h).transpose(0, 2, 1, 3)
        key = jax.random.key(seed)
        k1, k2, k3, k4 = jax.random.split(key, 4)
        b, n, dim = (4, 512, 256)
        dim_inner = (DIM_KEYS + DIM_VALUES) * HEADS
        tokens = jax.random.normal(k1, (b, n, dim), dtype=jnp.float32)
        Wqg = jax.random.normal(k2, (dim, dim_inner), dtype=jnp.float32) * dim ** (-0.5)
        Wkv = jax.random.normal(k3, (dim, dim_inner), dtype=jnp.float32) * dim ** (-0.5)
        Wout = jax.random.normal(k4, (DIM_VALUES * HEADS, dim), dtype=jnp.float32) * (DIM_VALUES * HEADS) ** (-0.5)
        return {'tokens': tokens, 'Wqg': Wqg, 'Wkv': Wkv, 'Wout': Wout}
    _L0_attn_in = _L0_attn_setup()

    def _L0_ffn_setup():
        import jax, jax.numpy as jnp
        import numpy as np
        B, S, H = (1, 512, 256)
        E, K = (16, 4)
        G, TG = (4, 2)
        I_MOE = 128
        N_SH = 2
        SCALE = 2.5

        def _mlp(x, gw, uw, dw):
            return jax.nn.silu(x @ gw.T) * (x @ uw.T) @ dw.T

        def _route(x2d, router_weight, e_bias):
            T = x2d.shape[0]
            scores = jax.nn.sigmoid(x2d @ router_weight.T)
            sc = scores + e_bias[None, :]
            group_scores = jnp.sum(jax.lax.top_k(sc.reshape(T, G, E // G), 2)[0], axis=-1)
            _, gidx = jax.lax.top_k(group_scores, TG)
            gmask = jnp.zeros((T, G), sc.dtype).at[jnp.arange(T)[:, None], gidx].set(1.0)
            smask = jnp.repeat(gmask, E // G, axis=1)
            masked = jnp.where(smask > 0, sc, 0.0)
            _, tidx = jax.lax.top_k(masked, K)
            tw = jnp.take_along_axis(scores, tidx, axis=1)
            tw = tw / (jnp.sum(tw, axis=-1, keepdims=True) + 1e-20)
            tw = tw * SCALE
            return (tidx, tw)

        def _moe_forward(hidden_states, router_weight, e_bias, gate_w, up_w, down_w, sh_gate_w, sh_up_w, sh_down_w):
            orig_shape = hidden_states.shape
            x = hidden_states.reshape(-1, H)
            T = x.shape[0]
            tidx, tw = _route(x, router_weight, e_bias)
            g = jnp.einsum('th,eih->tei', x, gate_w)
            u = jnp.einsum('th,eih->tei', x, up_w)
            h = jax.nn.silu(g) * u
            yo = jnp.einsum('tei,ehi->teh', h, down_w)
            combine = jnp.zeros((T, E), tw.dtype).at[jnp.arange(T)[:, None], tidx].add(tw)
            routed = jnp.einsum('te,teh->th', combine, yo)
            shared = _mlp(hidden_states.reshape(-1, H), sh_gate_w, sh_up_w, sh_down_w)
            return (routed + shared).reshape(orig_shape)
        key = jax.random.key(seed)
        ks = jax.random.split(key, 9)
        s = 0.02
        return {'hidden_states': jax.random.normal(ks[0], (B, S, H), jnp.float32), 'router_weight': jax.random.normal(ks[1], (E, H), jnp.float32) * s, 'e_bias': jnp.zeros((E,), jnp.float32), 'gate_w': jax.random.normal(ks[2], (E, I_MOE, H), jnp.float32) * s, 'up_w': jax.random.normal(ks[3], (E, I_MOE, H), jnp.float32) * s, 'down_w': jax.random.normal(ks[4], (E, H, I_MOE), jnp.float32) * s, 'sh_gate_w': jax.random.normal(ks[5], (N_SH * I_MOE, H), jnp.float32) * s, 'sh_up_w': jax.random.normal(ks[6], (N_SH * I_MOE, H), jnp.float32) * s, 'sh_down_w': jax.random.normal(ks[7], (H, N_SH * I_MOE), jnp.float32) * s}
    _L0_ffn_in = _L0_ffn_setup()
    _d = {'L0_attn_tokens': _L0_attn_in['tokens'], 'L0_attn_Wqg': _L0_attn_in['Wqg'], 'L0_attn_Wkv': _L0_attn_in['Wkv'], 'L0_attn_Wout': _L0_attn_in['Wout'], 'L0_ffn_router_weight': _L0_ffn_in['router_weight'], 'L0_ffn_e_bias': _L0_ffn_in['e_bias'], 'L0_ffn_gate_w': _L0_ffn_in['gate_w'], 'L0_ffn_up_w': _L0_ffn_in['up_w'], 'L0_ffn_down_w': _L0_ffn_in['down_w'], 'L0_ffn_sh_gate_w': _L0_ffn_in['sh_gate_w'], 'L0_ffn_sh_up_w': _L0_ffn_in['sh_up_w'], 'L0_ffn_sh_down_w': _L0_ffn_in['sh_down_w']}
    _x0 = _d['L0_attn_tokens']
    _d['L0_attn_tokens'] = jax.random.normal(jax.random.fold_in(jax.random.key(seed), 1), (16, 512, 256), dtype=_x0.dtype)
    del _x0
    return _d

def reference(L0_attn_tokens, L0_attn_Wqg, L0_attn_Wkv, L0_attn_Wout, L0_ffn_router_weight, L0_ffn_e_bias, L0_ffn_gate_w, L0_ffn_up_w, L0_ffn_down_w, L0_ffn_sh_gate_w, L0_ffn_sh_up_w, L0_ffn_sh_down_w):

    def _L0_attn_ref(tokens, Wqg, Wkv, Wout):
        import jax, jax.numpy as jnp
        import numpy as np
        EPS = 1e-12
        HEADS = 16
        DIM_KEYS = 16
        DIM_VALUES = 64

        def l2norm(t):
            n = jnp.linalg.norm(t, axis=-1, keepdims=True)
            return t / jnp.maximum(n, EPS)

        def tanh_norm(t):
            n = jnp.linalg.norm(t, axis=-1, keepdims=True)
            return jnp.tanh(n) * (t / jnp.maximum(n, EPS))

        def split_heads(x, h):
            b, n, hd = x.shape
            return x.reshape(b, n, h, hd // h).transpose(0, 2, 1, 3)
        qg = split_heads(tokens @ Wqg, HEADS)
        kv = split_heads(tokens @ Wkv, HEADS)
        queries, gates = (qg[..., :DIM_KEYS], qg[..., DIM_KEYS:])
        keys, values = (kv[..., :DIM_KEYS], kv[..., DIM_KEYS:])
        queries, keys, values = (l2norm(queries), l2norm(keys), l2norm(values))
        sim = jnp.einsum('bhid,bhjd->bhij', queries, keys)
        attn = jnp.square(jax.nn.relu(sim))
        aggr = jnp.einsum('bhij,bhjd->bhid', attn, values)
        out = tanh_norm(aggr) * jnp.tanh(jax.nn.silu(gates))
        b, h, n, d = out.shape
        out = out.transpose(0, 2, 1, 3).reshape(b, n, h * d)
        return out @ Wout

    def _L0_ffn_ref(hidden_states, router_weight, e_bias, gate_w, up_w, down_w, sh_gate_w, sh_up_w, sh_down_w):
        import jax, jax.numpy as jnp
        import numpy as np
        B, S, H = (1, 512, 256)
        E, K = (16, 4)
        G, TG = (4, 2)
        I_MOE = 128
        N_SH = 2
        SCALE = 2.5

        def _mlp(x, gw, uw, dw):
            return jax.nn.silu(x @ gw.T) * (x @ uw.T) @ dw.T

        def _route(x2d, router_weight, e_bias):
            T = x2d.shape[0]
            scores = jax.nn.sigmoid(x2d @ router_weight.T)
            sc = scores + e_bias[None, :]
            group_scores = jnp.sum(jax.lax.top_k(sc.reshape(T, G, E // G), 2)[0], axis=-1)
            _, gidx = jax.lax.top_k(group_scores, TG)
            gmask = jnp.zeros((T, G), sc.dtype).at[jnp.arange(T)[:, None], gidx].set(1.0)
            smask = jnp.repeat(gmask, E // G, axis=1)
            masked = jnp.where(smask > 0, sc, 0.0)
            _, tidx = jax.lax.top_k(masked, K)
            tw = jnp.take_along_axis(scores, tidx, axis=1)
            tw = tw / (jnp.sum(tw, axis=-1, keepdims=True) + 1e-20)
            tw = tw * SCALE
            return (tidx, tw)

        def _moe_forward(hidden_states, router_weight, e_bias, gate_w, up_w, down_w, sh_gate_w, sh_up_w, sh_down_w):
            orig_shape = hidden_states.shape
            x = hidden_states.reshape(-1, H)
            T = x.shape[0]
            tidx, tw = _route(x, router_weight, e_bias)
            g = jnp.einsum('th,eih->tei', x, gate_w)
            u = jnp.einsum('th,eih->tei', x, up_w)
            h = jax.nn.silu(g) * u
            yo = jnp.einsum('tei,ehi->teh', h, down_w)
            combine = jnp.zeros((T, E), tw.dtype).at[jnp.arange(T)[:, None], tidx].add(tw)
            routed = jnp.einsum('te,teh->th', combine, yo)
            shared = _mlp(hidden_states.reshape(-1, H), sh_gate_w, sh_up_w, sh_down_w)
            return (routed + shared).reshape(orig_shape)
        return _moe_forward(hidden_states, router_weight, e_bias, gate_w, up_w, down_w, sh_gate_w, sh_up_w, sh_down_w)
    x = L0_attn_tokens
    xn = _layernorm(x, axis=-1)
    x = x + _L0_attn_ref(xn, L0_attn_Wqg, L0_attn_Wkv, L0_attn_Wout) + _L0_ffn_ref(xn, L0_ffn_router_weight, L0_ffn_e_bias, L0_ffn_gate_w, L0_ffn_up_w, L0_ffn_down_w, L0_ffn_sh_gate_w, L0_ffn_sh_up_w, L0_ffn_sh_down_w)
    return x

_drawn_inputs = setup_inputs


def setup_inputs(seed=0):
    import zlib

    import numpy as np

    out = dict(_drawn_inputs(seed))
    spreads = {'L0_ffn_e_bias': (0.0, 0.479)}
    factors = {'L0_ffn_router_weight': 7.678,
     'L0_ffn_gate_w': 3.799,
     'L0_ffn_up_w': 3.745,
     'L0_ffn_down_w': 3.76,
     'L0_ffn_sh_gate_w': 3.388,
     'L0_ffn_sh_up_w': 3.351,
     'L0_ffn_sh_down_w': 3.352}
    for name, (base, spread) in spreads.items():
        noise = np.random.default_rng([zlib.crc32(name.encode()), seed]).standard_normal(out[name].shape)
        drawn = base * np.exp(spread * noise) if base else spread * noise
        out[name] = jnp.asarray(drawn.astype(out[name].dtype))
    for name, factor in factors.items():
        out[name] = (out[name] * factor).astype(out[name].dtype)
    return out
```

```python
from contextlib import ExitStack

import concourse.bass as bass
from concourse import mybir

F32 = mybir.dt.float32
F16 = mybir.dt.float16
I32 = mybir.dt.int32
ALU = mybir.AluOpType
ACT = mybir.ActivationFunctionType
AX = mybir.AxisListType

P = 128
B, T, D = 16, 512, 256
H, DK, DV = 16, 16, 64
E, NG, GE = 16, 4, 4
ES = 2
EA = E + ES
NB = T // P
KD = D // P
NP_ = H // 2
QK_W = 2 * H * DK
V_AT = QK_W
G_AT = V_AT + H * DV
WA_W = G_AT + H * DV
RSQRT_MAGIC = 0x5F3759DF

W_EXP = 9
QK_SCALE = 2.0 ** 7
S_SCALE = 2.0 ** -7
P_SCALE = 2.0 ** 14
V_SCALE = 2.0 ** 8
C_SCALE = 2.0 ** 8
AG_UNSCALE = 1.0 / (P_SCALE * V_SCALE)
EPS_L2 = 1e-12
EPS_LN = 1e-5
EPS_TW = 1e-20
ROUTE_SCALE = 2.5

STEPS = NP_ * NB
ORDER = list(range(E, EA)) + list(range(E))
ROUTED = [e for e in ORDER if e < E]
CT_STEP = 2


def expert_items():
    items = []
    for n, e in enumerate(ORDER):
        if e < E:
            items.append(("c", e))
        items += [("g", e), ("u", e)]
        if n >= 2:
            items.append(("d", ORDER[n - 2]))
    return items + [("d", ORDER[-2]), ("d", ORDER[-1])]


def plan_steps():
    cost = {"c": 1, "g": 6, "u": 6, "d": 6}
    items = expert_items()
    total = sum(cost[k] for k, _ in items)
    steps, done, at = [], 0, 0
    for s in range(STEPS):
        mine = []
        while at < len(items) and done + cost[items[at][0]] / 2 <= total * (s + 1) / STEPS:
            mine.append(items[at])
            done += cost[items[at][0]]
            at += 1
        steps.append(mine)
    steps[-1] += items[at:]
    return steps


PLAN = plan_steps()


def work_order():
    order = [("R", 0)] + [("QK", k) for k in range(NB)] + [("V", n) for n in range(2 * NB)]
    order += [("T", n) for n in range(4 * NB)]
    for s in range(STEPS):
        if s == CT_STEP:
            order.append(("CT", 0))
        if s % NB == 1 and s > NB:
            order.append(("N", s // NB - 1))
        order += [it for it in PLAN[s] if it[0] != "d"]
    order += [("N", NP_ - 1), ("G", 0), ("G", 1), ("WT", 0), ("WB", 0)]
    for t in range(NP_):
        if t + 2 < NP_:
            order.append(("G", t + 2))
        if t + 1 < NP_:
            order.append(("WB", t + 1))
    return order + [("X", k) for k in range(NB)]


ORDERED = work_order()
WORK = {key: n for n, key in enumerate(ORDERED)}
NW = 3
PER = len(WORK)
FIRST = NB
assert PER % NW == 0
RSQRT_STEPS = 11
ROUTE_STEPS = 34
HEAD_STEPS = 1 + RSQRT_STEPS + 4


def build_layer(nc, x, x_t, wa, w_gate, w_up, w_down, w_out, w_router, bias, ident, ident_h, sel, tri, out_t):
    with ExitStack() as ctx:
        def sb(name, shape, dt=F32):
            return ctx.enter_context(nc.sbuf_tensor(name, shape, dt))

        def sem(name):
            return ctx.enter_context(nc.semaphore(name))

        wa_h, wa_l = sb("wa_h", [P, KD, WA_W], F16), sb("wa_l", [P, KD, WA_W], F16)
        gate_h, gate_l = sb("gate_h", [P, KD, EA * P], F16), sb("gate_l", [P, KD, EA * P], F16)
        up_h, up_l = sb("up_h", [P, KD, EA * P], F16), sb("up_l", [P, KD, EA * P], F16)
        down_h, down_l = sb("down_h", [P, EA, D], F16), sb("down_l", [P, EA, D], F16)
        wo_h, wo_l = sb("wo_h", [P, NP_, D], F16), sb("wo_l", [P, NP_, D], F16)
        wr = sb("wr", [P, KD, E])
        bias_sb = sb("bias_sb", [P, E])
        id32, id16 = sb("id32", [P, P]), sb("id16", [P, P], F16)
        sel16 = sb("sel16", [2 * H, H * DV], F16)
        pair_sel = sb("pair_sel", [P, 2])
        tri_sb = sb("tri_sb", [P, NG * NG])
        eps_qkv = sb("eps_qkv", [P, 1])
        inv_a, inv_m = sb("inv_a", [P, 1]), sb("inv_m", [P, 1])
        up_routed, up_shared = sb("up_routed", [P, 1]), sb("up_shared", [P, 1])
        attn_scale, out_scale = sb("attn_scale", [P, 1]), sb("out_scale", [P, 1])

        split_weights(nc, x, wa, w_gate, w_up, w_down, w_out, w_router, bias, ident, ident_h, sel, tri,
                      dict(wa=(wa_h, wa_l), gate=(gate_h, gate_l), up=(up_h, up_l), down=(down_h, down_l),
                           wo=(wo_h, wo_l)),
                      wr, bias_sb, id32, id16, sel16, pair_sel, tri_sb, eps_qkv, inv_a, inv_m, up_routed,
                      up_shared, attn_scale, out_scale)

        x_sb = sb("x_sb", [P, NB, D])
        y_sb = sb("y_sb", [P, KD, T])
        xf = sb("xf", [P, KD, T])
        xh, xl = sb("xh", [P, KD, T], F16), sb("xl", [P, KD, T], F16)
        NR_, NH_ = 4, 4
        ring = sb("ring", [P, NR_, T])
        qk_raw = ring[:, :, :]
        ph, pl = sb("ph", [P, NH_, T], F16), sb("pl", [P, NH_, T], F16)
        wide = sb("wide", [P, NP_, T])
        v_raw = wide[:, :, :].rearrange("p (k a) t -> p k (a t)", k=NB)
        agg = wide
        qst, kst = sb("qst", [P, 2, 2 * T], F16), sb("kst", [P, 2, 2 * T], F16)
        qt, kt = sb("qt", [P, NP_, T], F16), sb("kt", [P, NP_, T], F16)
        vh, vl = sb("vh", [P, NB, H * DV], F16), sb("vl", [P, NB, H * DV], F16)
        sq = sb("sq", [P, 2, T])
        cb = sb("cb", [P, T])
        sg = sb("sg", [P, 2, T])
        gate_sb = sg
        hf = sb("hf", [P, 2, T])
        hh, hl = sb("hh", [P, 2, T], F16), sb("hl", [P, 2, T], F16)
        ah, al = sb("ah", [P, 2, T], F16), sb("al", [P, 2, T], F16)
        ct, wt = sb("ct", [2 * E, T], F16), sb("wt", [2 * H, T], F16)
        cst, wst = sb("cst", [P, NB, 2 * E], F16), sb("wst", [P, NB, 2 * H], F16)
        stats = sb("stats", [P, NB, 6])
        ln_m, ln_mean = sb("ln_m", [P, NB]), sb("ln_mean", [P, NB])
        ln_a, ln_y, ln_t = sb("ln_a", [P, NB]), sb("ln_y", [P, NB]), sb("ln_t", [P, NB])
        qn_a, qn_y, qn_t = (sb(f"qn_{c}", [P, NB, 2 * H]) for c in "ayt")
        vn_a, vn_y, vn_t = (sb(f"vn_{c}", [P, NB, H]) for c in "ayt")
        an_a, an_y, an_t = (sb(f"an_{c}", [P, NB, H]) for c in "ayt")
        th = sb("th", [P, NB, H])
        sc_s, sc_b, sc_m = (sb(f"sc_{c}", [P, NB, E]) for c in "sbm")
        pmax, pmin = sb("pmax", [P, NB * NG, 2]), sb("pmin", [P, NB * NG, 2])
        g_a, g_b, g_c, g_s = (sb(f"g_{c}", [P, NB * NG]) for c in "abcs")
        g_gt, g_eq = sb("g_gt", [P, NB * NG, NG]), sb("g_eq", [P, NB * NG, NG])
        top8 = sb("top8", [P, NB, 8])
        PAD = 8
        pre = [sb(f"pre{n}", [P, NB, PAD + E]) for n in range(2)]
        more, cnt = sb("more", [P, NB, E]), sb("cnt", [P, NB])

        sim = [ctx.enter_context(nc.psum_tensor(f"sim{n}", [P, T], F32)) for n in range(2)]
        av = ctx.enter_context(nc.psum_tensor("av", [P, T], F32))
        acc = [ctx.enter_context(nc.psum_tensor(f"acc{n}", [P, T], F32)) for n in range(KD)]
        wk = [ctx.enter_context(nc.psum_tensor(f"wk{n}", [P, T], F32)) for n in range(NW)]

        x_loaded, res_loaded, stored = sem("x_loaded"), sem("res_loaded"), sem("stored")
        work_full = sem("work_full")
        sim_full, relu_done, square_done = sem("sim_full"), sem("relu_done"), sem("square_done")
        ph_done, pl_done, av_step = sem("ph_done"), sem("pl_done"), sem("av_step")
        agg_done, agg_sq_done = sem("agg_done"), sem("agg_sq_done")
        down_done, y_done = sem("down_done"), sem("y_done")
        ln_step, xn_done, xf_done = sem("ln_step"), sem("xn_done"), sem("xf_done")
        xh_done, xl_done = sem("xh_done"), sem("xl_done")
        raw_done, rawsq_done, norm_done = sem("raw_done"), sem("rawsq_done"), sem("norm_done")
        qn_step, vn_step, an_step = sem("qn_step"), sem("vn_step"), sem("an_step")
        qkn_done, vn_done = sem("qkn_done"), sem("vn_done")
        qk_hi, qk_lo, qk_turned = sem("qk_hi"), sem("qk_lo"), sem("qk_turned")
        v_hi, v_lo = sem("v_hi"), sem("v_lo")
        score_done, route_step, ct_done = sem("score_done"), sem("route_step"), sem("ct_done")
        cb_done, silu_done, sgc_done = sem("cb_done"), sem("silu_done"), sem("sgc_done")
        hf_done, h_hi, h_lo = sem("hf_done"), sem("h_hi"), sem("h_lo")
        n_done, th_done, wt_done = sem("n_done"), sem("th_done"), sem("wt_done")
        gsilu_done, gate_done, gw_done = sem("gsilu_done"), sem("gate_done"), sem("gw_done")
        a_done, a_hi, a_lo = sem("a_done"), sem("a_hi"), sem("a_lo")
        out_mm = sem("out_mm")

        def upto(b, per, c):
            return max(b * per + c, 0) if isinstance(b, int) else b * per + c

        def filled(b, key):
            if key[0] == "X":
                return upto(b, PER, key[1] + 1)
            return upto(b, PER, FIRST + WORK[key] + 1)

        def bank(key):
            return wk[(FIRST + WORK[key]) % NW]

        def bank16(key):
            return bank(key)[:, :].bitcast(F16)

        def read(b, key):
            kind, n = key
            s, per, count = {
                "R": (score_done, 1, 1),
                "QK": (raw_done, 3 * NB, n + 1),
                "V": (raw_done, 3 * NB, NB + n + 1),
                "T": (qk_turned, 4 * NB, n + 1),
                "CT": (ct_done, 1, 1),
                "c": (cb_done, E, ROUTED.index(n) + 1 if n in ROUTED else 0),
                "g": (silu_done, EA, ORDER.index(n) + 1),
                "u": (hf_done, EA, ORDER.index(n) + 1),
                "N": (n_done, NP_, n + 1),
                "G": (gsilu_done, NP_, n + 1),
                "WT": (wt_done, 1, 1),
                "WB": (gw_done, NP_, n + 1),
                "X": (xf_done, NB, n + 1),
            }[kind]
            return s, upto(b, per, count)

        def bank_read(b, key):
            if key[0] == "X":
                if key[1] >= NW:
                    return read(b, ("X", key[1] - NW))
                return read(b - 1, ORDERED[WORK[key] - NW])
            if WORK[key] >= NW:
                return read(b, ORDERED[WORK[key] - NW])
            return read(b, ("X", WORK[key] + NB - NW))

        def rounds(eng, body):
            body(0, False)
            with eng.Fori(1, B - 1) as b:
                body(b, False)
            body(B - 1, True)

        block = ctx.enter_context(nc.Block())

        @block.sync
        def _(sp):
            def load_x(b):
                sp.wait_ge(work_full, filled(b - 1, ("X", NB - 1)))
                sp.dma_start(x_sb[:, :, :], x[b].rearrange("(k p) d -> p k d", p=P)).then_inc(x_loaded, 16)

            load_x(0)

            def body(b, last):
                if not last:
                    load_x(b + 1)
                sp.wait_ge(stored, upto(b, 16, 0))
                sp.dma_start(y_sb[:, :, :], x_t[b].rearrange("(m p) t -> p m t", p=P)).then_inc(res_loaded, 16)
                sp.wait_ge(y_done, upto(b, KD, KD))
                sp.dma_start(out_t[b].rearrange("(m p) t -> p m t", p=P), y_sb[:, :, :]).then_inc(stored, 16)

            rounds(sp, body)
            sp.wait_ge(stored, 16 * B)

        @block.vector
        def _(dve):
            v = nc.vector

            class Chain:

                def __init__(self, s, b, per):
                    self.s, self.b, self.per, self.n = s, b, per, 0

                def __call__(self, ins):
                    ins.then_inc(self.s, 1)
                    self.n += 1
                    dve.wait_ge(self.s, self.b * self.per + self.n)

                def end(self):
                    assert self.n == self.per, (self.n, self.per)

            def rsqrt(link, a, y, t):
                ai, yi = a.bitcast(I32), y.bitcast(I32)
                link(v.tensor_scalar(yi, ai, 1, None, ALU.logical_shift_right))
                link(v.tensor_scalar(yi, yi, -1.0, float(RSQRT_MAGIC), ALU.mult, ALU.add))
                for _ in range(3):
                    link(v.tensor_tensor(t, y, y, ALU.mult))
                    link(v.scalar_tensor_tensor(out=t, in0=a, scalar=-0.5, in1=t, op0=ALU.mult, op1=ALU.mult))
                    link(v.scalar_tensor_tensor(out=y, in0=t, scalar=1.5, in1=y, op0=ALU.add, op1=ALU.mult))

            def layernorm(b):
                link = Chain(ln_step, b, 4 + RSQRT_STEPS)
                dve.wait_ge(x_loaded, upto(b, 16, 16))
                dve.wait_ge(xn_done, upto(b, NB, 0))
                for k in range(NB):
                    ins = v.bn_stats(stats[:, k, :], x_sb[:, k, :])
                link(ins)
                v.tensor_tensor(ln_m[:, :], stats[:, :, 1], stats[:, :, 4], ALU.add)
                v.tensor_tensor(ln_a[:, :], stats[:, :, 2], stats[:, :, 5], ALU.add)
                link(v.tensor_tensor(ln_t[:, :], stats[:, :, 1], stats[:, :, 4], ALU.subtract))
                v.tensor_scalar(ln_mean[:, :], ln_m[:, :], 0.5, None, ALU.mult)
                v.tensor_scalar(ln_a[:, :], ln_a[:, :], 1.0 / D, EPS_LN, ALU.mult, ALU.add)
                link(v.scalar_tensor_tensor(out=ln_y[:, :], in0=ln_t[:, :], scalar=0.25, in1=ln_t[:, :],
                                            op0=ALU.mult, op1=ALU.mult))
                link(v.tensor_tensor(ln_a[:, :], ln_a[:, :], ln_y[:, :], ALU.add))
                rsqrt(link, ln_a[:, :], ln_y[:, :], ln_t[:, :])
                for k in range(NB):
                    v.tensor_scalar(x_sb[:, k, :], x_sb[:, k, :], ln_mean[:, k:k + 1], ln_y[:, k:k + 1],
                                    ALU.subtract, ALU.mult).then_inc(xn_done, 1)
                link.end()

            def tokens_lo(b):
                dve.wait_ge(xf_done, upto(b, NB, NB))
                dve.wait_ge(xh_done, upto(b, 1, 1))
                dve.wait_ge(work_full, filled(b - 1, ("G", NP_ - 1)))
                v.tensor_tensor(xl[:, :, :], xf[:, :, :], xh[:, :, :], ALU.subtract).then_inc(xl_done, 1)

            def sums(b, n):
                dve.wait_ge(rawsq_done, upto(b, 3 * NB, n + 1))
                if n < NB:
                    v.tensor_reduce(qn_a[:, n, :], sq[:, n % 2, :].rearrange("p (h d) -> p h d", d=DK), AX.X,
                                    ALU.add).then_inc(norm_done, 1)
                else:
                    k, half = (n - NB) // 2, (n - NB) % 2
                    v.tensor_reduce(vn_a[:, k, half * 8:half * 8 + 8],
                                    sq[:, n % 2, :].rearrange("p (h d) -> p h d", d=DV), AX.X,
                                    ALU.add).then_inc(norm_done, 1)

            def norms(b, which):
                s, a, y, t = (qn_step, qn_a, qn_y, qn_t) if which == "qk" else (vn_step, vn_a, vn_y, vn_t)
                dve.wait_ge(norm_done, upto(b, 3 * NB, NB if which == "qk" else 3 * NB))
                if which == "qk":
                    dve.wait_ge(qkn_done, upto(b, NB, 0))
                else:
                    dve.wait_ge(vn_done, upto(b, 2 * NB, 0))
                link = Chain(s, b, 1 + RSQRT_STEPS)
                link(v.tensor_scalar(a[:, :, :], a[:, :, :], eps_qkv[:, 0:1], None, ALU.max))
                rsqrt(link, a[:, :, :], y[:, :, :], t[:, :, :])
                link.end()

            def unit_qk(b, k):
                dve.wait_ge(raw_done, upto(b, 3 * NB, k + 1))
                blk = qk_raw[:, k, :].rearrange("p (h d) -> p h d", d=DK)
                v.scalar_tensor_tensor(out=blk, in0=blk, scalar=QK_SCALE,
                                       in1=qn_y[:, k, :].unsqueeze(2).to_broadcast([P, 2 * H, DK]),
                                       op0=ALU.mult, op1=ALU.mult).then_inc(qkn_done, 1)

            def unit_v(b, n):
                k, half = n // 2, n % 2
                dve.wait_ge(raw_done, upto(b, 3 * NB, NB + n + 1))
                blk = v_raw[:, k, half * T:half * T + T].rearrange("p (h d) -> p h d", d=DV)
                v.scalar_tensor_tensor(out=blk, in0=blk, scalar=V_SCALE,
                                       in1=vn_y[:, k, half * 8:half * 8 + 8].unsqueeze(2).to_broadcast([P, 8, DV]),
                                       op0=ALU.mult, op1=ALU.mult).then_inc(vn_done, 1)

            def turned(b, n):
                k, c = n // 4, n % 4
                dve.wait_ge(work_full, filled(b, ("T", n)))
                dve.wait_ge(sim_full, upto(b, 2 * STEPS, 0))
                dst = (qt if c < 2 else kt)[:, 4 * (c % 2):4 * (c % 2) + 4, k * P:(k + 1) * P]
                ins = v.tensor_copy(dst, bank16(("T", n))[:, 0:T].rearrange("p (m t) -> p m t", m=4))
                ins.then_inc(qk_turned, 1)

            def route(b):
                link = Chain(route_step, b, ROUTE_STEPS)
                tt = v.tensor_tensor
                dve.wait_ge(score_done, upto(b, 1, 1))
                link(tt(sc_b[:, :, :], sc_s[:, :, :], bias_sb[:, :].unsqueeze(1).to_broadcast([P, NB, E]), ALU.add))
                two = sc_b[:, :, :].rearrange("p k (g a c) -> p (k g) a c", a=2, c=2)
                link(tt(pmax[:, :, :], two[:, :, :, 0], two[:, :, :, 1], ALU.max))
                link(tt(pmin[:, :, :], two[:, :, :, 0], two[:, :, :, 1], ALU.min))
                link(tt(g_a[:, :], pmax[:, :, 0], pmax[:, :, 1], ALU.max))
                link(tt(g_b[:, :], pmax[:, :, 0], pmax[:, :, 1], ALU.min))
                link(tt(g_c[:, :], pmin[:, :, 0], pmin[:, :, 1], ALU.max))
                link(tt(g_b[:, :], g_b[:, :], g_c[:, :], ALU.max))
                link(tt(g_s[:, :], g_a[:, :], g_b[:, :], ALU.add))
                other = g_s[:, :].rearrange("p (k j) -> p k j", j=NG).unsqueeze(2).to_broadcast([P, NB, NG, NG])
                mine = g_s[:, :].rearrange("p (k g) -> p k g", g=NG).unsqueeze(3).to_broadcast([P, NB, NG, NG])
                tt(g_gt[:, :, :].rearrange("p (k g) j -> p k g j", k=NB), other, mine, ALU.is_gt)
                link(tt(g_eq[:, :, :].rearrange("p (k g) j -> p k g j", k=NB), other, mine, ALU.is_equal))
                eq = g_eq[:, :, :].rearrange("p (k g) j -> p k (g j)", k=NB)
                link(tt(eq, eq, tri_sb[:, :].unsqueeze(1).to_broadcast([P, NB, NG * NG]), ALU.mult))
                link(tt(g_gt[:, :, :], g_gt[:, :, :], g_eq[:, :, :], ALU.add))
                link(v.tensor_reduce(g_a[:, :], g_gt[:, :, :], AX.X, ALU.add))
                link(v.tensor_scalar(g_a[:, :], g_a[:, :], 1.5, None, ALU.is_lt))
                per_group = sc_m[:, :, :].rearrange("p k (g c) -> p (k g) c", c=GE)
                link(tt(per_group, sc_b[:, :, :].rearrange("p k (g c) -> p (k g) c", c=GE),
                        g_a[:, :].unsqueeze(2).to_broadcast([P, NB * NG, GE]), ALU.mult))
                link(v.tensor_scalar(sc_m[:, :, :], sc_m[:, :, :], 0.0, None, ALU.add))
                for n in range(2):
                    v.memset(pre[n][:, :, 0:PAD], 0.0)
                for k in range(NB):
                    ins = v.max(top8[:, k, :], sc_m[:, k, :])
                link(ins)
                fourth = top8[:, :, 3:4].to_broadcast([P, NB, E])
                link(tt(more[:, :, :], sc_m[:, :, :], fourth, ALU.is_gt))
                link(tt(pre[0][:, :, PAD:], sc_m[:, :, :], fourth, ALU.is_equal))
                link(v.tensor_copy(sc_b[:, :, :], pre[0][:, :, PAD:]))
                link(v.tensor_reduce(cnt[:, :], more[:, :, :], AX.X, ALU.add))
                for n, d in enumerate((1, 2, 4, 8)):
                    src, dst = pre[n % 2], pre[(n + 1) % 2]
                    link(tt(dst[:, :, PAD:], src[:, :, PAD:], src[:, :, PAD - d:PAD + E - d], ALU.add))
                link(tt(pre[0][:, :, PAD:], pre[0][:, :, PAD:], cnt[:, :].unsqueeze(2).to_broadcast([P, NB, E]),
                        ALU.add))
                link(v.scalar_tensor_tensor(out=sc_b[:, :, :], in0=pre[0][:, :, PAD:], scalar=4.5,
                                            in1=sc_b[:, :, :], op0=ALU.is_lt, op1=ALU.mult))
                link(tt(more[:, :, :], more[:, :, :], sc_b[:, :, :], ALU.add))
                link(tt(sc_s[:, :, :], sc_s[:, :, :], more[:, :, :], ALU.mult))
                link(v.tensor_reduce(cnt[:, :], sc_s[:, :, :], AX.X, ALU.add))
                link(v.tensor_scalar(cnt[:, :], cnt[:, :], EPS_TW, None, ALU.add))
                link(v.reciprocal(cnt[:, :], cnt[:, :]))
                link(v.scalar_tensor_tensor(out=sc_m[:, :, :], in0=sc_s[:, :, :], scalar=ROUTE_SCALE * C_SCALE,
                                            in1=cnt[:, :].unsqueeze(2).to_broadcast([P, NB, E]),
                                            op0=ALU.mult, op1=ALU.mult))
                dve.wait_ge(work_full, filled(b - 1, ("CT", 0)))
                link(v.tensor_copy(cst[:, :, 0:E], sc_m[:, :, :]))
                link(tt(cst[:, :, E:2 * E], sc_m[:, :, :], cst[:, :, 0:E], ALU.subtract))
                link.end()

            def probs(b, n):
                dve.wait_ge(square_done, upto(b, 2 * STEPS, n + 1))
                dve.wait_ge(av_step, upto(b, STEPS, n // 2 - 1))
                v.tensor_copy(ph[:, n % NH_, :], ring[:, n % NR_, :]).then_inc(ph_done, 1)

            def probs_lo(b, n):
                dve.wait_ge(ph_done, upto(b, 2 * STEPS, n + 1))
                v.tensor_tensor(pl[:, n % NH_, :], ring[:, n % NR_, :], ph[:, n % NH_, :],
                                ALU.subtract).then_inc(pl_done, 1)

            def hidden(b, e):
                n = ORDER.index(e)
                dve.wait_ge(silu_done, upto(b, EA, n + 1))
                if e < E:
                    dve.wait_ge(sgc_done, upto(b, E, ROUTED.index(e) + 1))
                dve.wait_ge(work_full, filled(b, ("u", e)))
                dve.wait_ge(h_lo, upto(b, EA, n - 1))
                dve.wait_ge(h_hi, upto(b, EA, n - 1))
                ins = v.scalar_tensor_tensor(out=hf[:, n % 2, :], in0=bank(("u", e))[:, :],
                                             scalar=(up_routed if e < E else up_shared)[:, 0:1],
                                             in1=sg[:, n % 2, :], op0=ALU.mult, op1=ALU.mult)
                ins.then_inc(hf_done, 1)

            def head_norms(b, t):
                dve.wait_ge(work_full, filled(b, ("N", t)))
                ins = v.tensor_copy(an_a[:, :, 2 * t:2 * t + 2],
                                    bank(("N", t))[:, 0:2 * NB].rearrange("p (k h) -> p k h", h=2))
                ins.then_inc(n_done, 1)

            def head_scales(b):
                link = Chain(an_step, b, HEAD_STEPS)
                dve.wait_ge(n_done, upto(b, NP_, NP_))
                link(v.tensor_scalar(an_a[:, :, :], an_a[:, :, :], EPS_L2 ** 2, None, ALU.max))
                rsqrt(link, an_a[:, :, :], an_y[:, :, :], an_t[:, :, :])
                link(v.tensor_tensor(an_t[:, :, :], an_a[:, :, :], an_y[:, :, :], ALU.mult))
                dve.wait_ge(th_done, upto(b, 1, 1))
                link(v.scalar_tensor_tensor(out=an_a[:, :, :], in0=th[:, :, :], scalar=C_SCALE, in1=an_y[:, :, :],
                                            op0=ALU.mult, op1=ALU.mult))
                link(v.tensor_copy(wst[:, :, 0:H], an_a[:, :, :]))
                link(v.tensor_tensor(wst[:, :, H:2 * H], an_a[:, :, :], wst[:, :, 0:H], ALU.subtract))
                link.end()

            def gated(b, t):
                dve.wait_ge(work_full, filled(b, ("WB", t)))
                dve.wait_ge(gate_done, upto(b, NP_, t + 1))
                ins = v.tensor_tensor(gate_sb[:, t % 2, :], gate_sb[:, t % 2, :], bank(("WB", t))[:, :], ALU.mult)
                ins.then_inc(gw_done, 1)

            def gated2(b, t):
                dve.wait_ge(gw_done, upto(b, NP_, t + 1))
                dve.wait_ge(agg_done, upto(b, NP_, t + 1))
                v.scalar_tensor_tensor(out=agg[:, t, :], in0=agg[:, t, :], scalar=attn_scale[:, 0:1],
                                       in1=gate_sb[:, t % 2, :], op0=ALU.mult, op1=ALU.mult).then_inc(a_done, 1)

            def finish(b):
                dve.wait_ge(out_mm, upto(b, NP_, NP_))
                dve.wait_ge(res_loaded, upto(b, 16, 16))
                for m in range(KD):
                    v.scalar_tensor_tensor(out=y_sb[:, m, :], in0=acc[m][:, :], scalar=out_scale[:, 0:1],
                                           in1=y_sb[:, m, :], op0=ALU.mult, op1=ALU.add).then_inc(y_done, 1)

            layernorm(0)

            def body(b, last):
                tokens_lo(b)
                for n in range(NB):
                    sums(b, n)
                norms(b, "qk")
                for k in range(NB):
                    unit_qk(b, k)
                for n in range(NB, 3 * NB):
                    sums(b, n)
                for n in range(4 * NB):
                    turned(b, n)
                norms(b, "v")
                for n in range(2 * NB):
                    unit_v(b, n)
                route(b)
                for s in range(STEPS):
                    for n in (2 * s, 2 * s + 1):
                        probs(b, n)
                    for n in (2 * s, 2 * s + 1):
                        probs_lo(b, n)
                    if s % NB == 1 and s > NB:
                        head_norms(b, s // NB - 1)
                    for kind, e in PLAN[s]:
                        if kind == "u":
                            hidden(b, e)
                head_norms(b, NP_ - 1)
                head_scales(b)
                if not last:
                    layernorm(b + 1)
                for t in range(NP_):
                    gated(b, t)
                    gated2(b, t)
                finish(b)

            rounds(dve, body)

        @block.scalar
        def _(act):
            a = nc.scalar.activation

            def turn_tokens(b, k):
                act.wait_ge(work_full, filled(b, ("X", k)))
                act.wait_ge(work_full, filled(b - 1, ("R", 0)))
                act.wait_ge(xh_done, upto(b, 1, 0))
                act.wait_ge(xl_done, upto(b, 1, 0))
                ins = a(xf[:, :, k * P:(k + 1) * P],
                        wk[k % NW][:, 0:KD * P].rearrange("p (m t) -> p m t", m=KD), ACT.Copy)
                ins.then_inc(xf_done, 1)

            for k in range(NB):
                turn_tokens(0, k)

            def raw(b):
                act.wait_ge(xf_done, upto(b, NB, NB))
                act.wait_ge(work_full, filled(b - 1, ("G", NP_ - 1)))
                a(xh[:, :, :], xf[:, :, :], ACT.Copy).then_inc(xh_done, 1)
                act.wait_ge(work_full, filled(b, ("R", 0)))
                act.wait_ge(route_step, upto(b, ROUTE_STEPS, 0))
                a(sc_s[:, :, :], bank(("R", 0))[:, 0:NB * E].rearrange("p (k e) -> p k e", e=E),
                  ACT.Sigmoid).then_inc(score_done, 1)
                act.wait_ge(a_hi, upto(b, NP_, 0))
                act.wait_ge(a_lo, upto(b, NP_, 0))
                act.wait_ge(pl_done, upto(b, 2 * STEPS, 0))
                for n in range(3 * NB):
                    key = ("QK", n) if n < NB else ("V", n - NB)
                    act.wait_ge(work_full, filled(b, key))
                    act.wait_ge(norm_done, upto(b, 3 * NB, n - 1))
                    if n == 0:
                        act.wait_ge(work_full, filled(b - 1, ("N", NP_ - 1)))
                    a(sq[:, n % 2, :], bank(key)[:, :], ACT.Square).then_inc(rawsq_done, 1)
                    if n < NB:
                        dst = qk_raw[:, n, :]
                    else:
                        k, half = (n - NB) // 2, (n - NB) % 2
                        dst = v_raw[:, k, half * T:half * T + T]
                    a(dst, bank(key)[:, :], ACT.Copy).then_inc(raw_done, 1)

            def split_hi_qk(b, k):
                act.wait_ge(qkn_done, upto(b, NB, k + 1))
                if k >= 2:
                    act.wait_ge(work_full, filled(b, ("T", 4 * k - 5)))
                else:
                    act.wait_ge(work_full, filled(b - 1, ("T", 4 * k + 11)))
                blk = qk_raw[:, k, :]
                for c, dst, dims in ((0, qst, 0), (1, kst, 1)):
                    src = blk[:, c * H * DK:(c + 1) * H * DK].rearrange("p (h d) -> p h d", d=DK)
                    src = src.unsqueeze(2).to_broadcast([P, H, 2, DK])
                    to = dst[:, k % 2, :].rearrange("p (h a c d) -> p h a c d", a=2, c=2, d=DK)
                    to = to[:, :, 0, :, :] if c == 0 else to[:, :, :, 0, :]
                    a(to, src, ACT.Copy).then_inc(qk_hi, 1)

            def split_hi_v(b, n):
                k, half = n // 2, n % 2
                act.wait_ge(vn_done, upto(b, 2 * NB, n + 1))
                act.wait_ge(av_step, upto(b, STEPS, 0))
                a(vh[:, k, half * T:half * T + T], v_raw[:, k, half * T:half * T + T], ACT.Copy).then_inc(v_hi, 1)

            def relu(b, n):
                act.wait_ge(sim_full, upto(b, 2 * STEPS, n + 1))
                act.wait_ge(pl_done, upto(b, 2 * STEPS, n - NR_ + 1))
                if n < NR_:
                    act.wait_ge(qk_lo, upto(b, 2 * NB, 2 * NB))
                a(ring[:, n % NR_, :], sim[n % 2][:, :], ACT.Relu, scale=S_SCALE).then_inc(relu_done, 1)

            def square(b, n):
                act.wait_ge(relu_done, upto(b, 2 * STEPS, n + 1))
                a(ring[:, n % NR_, :], ring[:, n % NR_, :], ACT.Square).then_inc(square_done, 1)

            def weigh(b, e):
                n = ROUTED.index(e)
                act.wait_ge(work_full, filled(b, ("c", e)))
                act.wait_ge(sgc_done, upto(b, E, n))
                a(cb[:, :], bank(("c", e))[:, :], ACT.Copy).then_inc(cb_done, 1)

            def silu(b, e):
                n = ORDER.index(e)
                act.wait_ge(work_full, filled(b, ("g", e)))
                act.wait_ge(hf_done, upto(b, EA, n - 1))
                act.wait_ge(a_done, upto(b, NP_, 0))
                ins = a(sg[:, n % 2, :], bank(("g", e))[:, :], ACT.Silu, scale=inv_m[:, 0:1])
                ins.then_inc(silu_done, 1)

            def hidden_hi(b, n):
                act.wait_ge(hf_done, upto(b, EA, n + 1))
                act.wait_ge(down_done, upto(b, EA, n - 1))
                a(hh[:, n % 2, :], hf[:, n % 2, :], ACT.Copy).then_inc(h_hi, 1)

            def take_heads(b, t):
                act.wait_ge(av_step, upto(b, STEPS, NB * (t + 1)))
                if t >= 2:
                    act.wait_ge(work_full, filled(b, ("N", t - 2)))
                else:
                    act.wait_ge(norm_done, upto(b, 3 * NB, 3 * NB))
                a(sq[:, t % 2, :], av[:, :], ACT.Square, scale=AG_UNSCALE).then_inc(agg_sq_done, 1)
                act.wait_ge(v_lo, upto(b, 2 * NB, 2 * NB))
                act.wait_ge(v_hi, upto(b, 2 * NB, 2 * NB))
                a(agg[:, t, :], av[:, :], ACT.Copy).then_inc(agg_done, 1)

            def gate(b, t):
                act.wait_ge(work_full, filled(b, ("G", t)))
                act.wait_ge(a_done, upto(b, NP_, t - 1))
                act.wait_ge(hf_done, upto(b, EA, EA))
                ins = a(gate_sb[:, t % 2, :], bank(("G", t))[:, :], ACT.Silu, scale=inv_a[:, 0:1])
                ins.then_inc(gsilu_done, 1)
                act.wait_ge(gsilu_done, upto(b, NP_, t + 1))
                a(gate_sb[:, t % 2, :], gate_sb[:, t % 2, :], ACT.Tanh).then_inc(gate_done, 1)

            def whole(b, last):
                raw(b)
                for k in range(NB):
                    split_hi_qk(b, k)
                for n in range(2 * NB):
                    split_hi_v(b, n)
                for s in range(STEPS):
                    if s == CT_STEP:
                        act.wait_ge(work_full, filled(b, ("CT", 0)))
                        a(ct[:, :], bank16(("CT", 0))[0:2 * E, 0:T], ACT.Copy).then_inc(ct_done, 1)
                    for n in (2 * s, 2 * s + 1):
                        relu(b, n)
                    for n in (2 * s, 2 * s + 1):
                        square(b, n)
                    for kind, e in PLAN[s]:
                        if kind == "c":
                            weigh(b, e)
                        if kind == "g":
                            silu(b, e)
                        if kind == "u" and ORDER.index(e) >= 1:
                            hidden_hi(b, ORDER.index(e) - 1)
                    if s % NB == 0 and s >= NB:
                        take_heads(b, s // NB - 1)
                hidden_hi(b, EA - 1)
                take_heads(b, NP_ - 1)
                gate(b, 0)
                gate(b, 1)
                act.wait_ge(an_step, upto(b, HEAD_STEPS, HEAD_STEPS - 3))
                a(th[:, :, :], an_t[:, :, :], ACT.Tanh).then_inc(th_done, 1)
                act.wait_ge(work_full, filled(b, ("WT", 0)))
                act.wait_ge(work_full, filled(b - 1, ("WB", NP_ - 1)))
                a(wt[:, :], bank16(("WT", 0))[0:2 * H, 0:T], ACT.Copy).then_inc(wt_done, 1)
                for t in range(NP_):
                    act.wait_ge(a_done, upto(b, NP_, t + 1))
                    act.wait_ge(out_mm, upto(b, NP_, t - 1))
                    a(ah[:, t % 2, :], agg[:, t, :], ACT.Copy).then_inc(a_hi, 1)
                    if t + 2 < NP_:
                        gate(b, t + 2)
                if not last:
                    for k in range(NB):
                        turn_tokens(b + 1, k)

            rounds(act, whole)

        @block.gpsimd
        def _(pool):
            tt = nc.gpsimd.tensor_tensor

            def split_lo_qk(b, k):
                for c, dst in ((0, qst), (1, kst)):
                    pool.wait_ge(qk_hi, upto(b, 2 * NB, 2 * k + c + 1))
                    src = qk_raw[:, k, c * H * DK:(c + 1) * H * DK].rearrange("p (h d) -> p h d", d=DK)
                    src = src.unsqueeze(2).to_broadcast([P, H, 2, DK])
                    to = dst[:, k % 2, :].rearrange("p (h a c d) -> p h a c d", a=2, c=2, d=DK)
                    hi, lo = ((to[:, :, 0, :, :], to[:, :, 1, :, :]) if c == 0
                              else (to[:, :, :, 0, :], to[:, :, :, 1, :]))
                    tt(lo, src, hi, ALU.subtract).then_inc(qk_lo, 1)

            def body(b, last):
                for k in range(NB):
                    split_lo_qk(b, k)
                for n in range(2 * NB):
                    k, half = n // 2, n % 2
                    pool.wait_ge(v_hi, upto(b, 2 * NB, n + 1))
                    pool.wait_ge(av_step, upto(b, STEPS, 0))
                    sl = slice(half * T, half * T + T)
                    tt(vl[:, k, sl], v_raw[:, k, sl], vh[:, k, sl], ALU.subtract).then_inc(v_lo, 1)

                def hidden_lo(n):
                    pool.wait_ge(h_hi, upto(b, EA, n + 1))
                    pool.wait_ge(down_done, upto(b, EA, n - 1))
                    tt(hl[:, n % 2, :], hf[:, n % 2, :], hh[:, n % 2, :], ALU.subtract).then_inc(h_lo, 1)

                for s in range(STEPS):
                    for kind, e in PLAN[s]:
                        n = ORDER.index(e)
                        if kind == "g" and e < E:
                            m = ROUTED.index(e)
                            pool.wait_ge(silu_done, upto(b, EA, n + 1))
                            pool.wait_ge(cb_done, upto(b, E, m + 1))
                            tt(sg[:, n % 2, :], sg[:, n % 2, :], cb[:, :], ALU.mult).then_inc(sgc_done, 1)
                        if kind == "u" and n >= 1:
                            hidden_lo(n - 1)
                hidden_lo(EA - 1)
                for t in range(NP_):
                    pool.wait_ge(a_hi, upto(b, NP_, t + 1))
                    pool.wait_ge(out_mm, upto(b, NP_, t - 1))
                    tt(al[:, t % 2, :], agg[:, t, :], ah[:, t % 2, :], ALU.subtract).then_inc(a_lo, 1)

            rounds(pool, body)

        @block.tensor
        def _(pe):
            mm, turn = nc.tensor.matmul, nc.tensor.transpose

            def products(dst, w_parts, x_parts, first=True, last=True):
                (w_h, w_l), (x_h, x_l) = w_parts, x_parts
                terms = [(w, x_h) for w in (w_h, w_l)] + [(w_h, x_l)]
                n = len(terms) * len(w_h)
                i = 0
                for w, xx in terms:
                    for k in range(len(w_h)):
                        ins = mm(dst, w[k], xx[k], start=first and i == 0, stop=last and i == n - 1)
                        i += 1
                return ins

            def turn_tokens(b, k):
                pe.wait_ge(xn_done, upto(b, NB, k + 1))
                pe.wait_ge(*bank_read(b, ("X", k)))
                for m in range(KD):
                    ins = turn(wk[k % NW][:, m * P:(m + 1) * P], x_sb[:, k, m * P:(m + 1) * P], id32[:, :])
                ins.then_inc(work_full, 1)

            def router(b):
                pe.wait_ge(xf_done, upto(b, NB, NB))
                pe.wait_ge(*bank_read(b, ("R", 0)))
                for k in range(NB):
                    for m in range(KD):
                        ins = mm(bank(("R", 0))[:, k * E:(k + 1) * E], xf[:, m, k * P:(k + 1) * P], wr[:, m, :],
                                 start=(m == 0), stop=(m == KD - 1))
                ins.then_inc(work_full, 1)

            def project(b, key, k, lo, width):
                pe.wait_ge(xh_done, upto(b, 1, 1))
                pe.wait_ge(xl_done, upto(b, 1, 1))
                pe.wait_ge(*bank_read(b, key))
                blk, cols = slice(k * P, (k + 1) * P), slice(lo, lo + width)
                ins = products(bank(key)[:, 0:width], ([xh[:, m, blk] for m in range(KD)],
                                                       [xl[:, m, blk] for m in range(KD)]),
                               ([wa_h[:, m, cols] for m in range(KD)], [wa_l[:, m, cols] for m in range(KD)]))
                ins.then_inc(work_full, 1)

            def turn_qk(b, n):
                k, c = n // 4, n % 4
                pe.wait_ge(qk_lo, upto(b, 2 * NB, 2 * k + (1 if c < 2 else 2)))
                pe.wait_ge(*bank_read(b, ("T", n)))
                src = (qst if c < 2 else kst)[:, k % 2, (c % 2) * T:(c % 2) * T + T]
                for m in range(4):
                    ins = turn(bank16(("T", n))[:, m * P:(m + 1) * P], src[:, m * P:(m + 1) * P], id16[:, :])
                ins.then_inc(work_full, 1)

            def turn_small(b, key, src):
                pe.wait_ge(*bank_read(b, key))
                for k in range(NB):
                    ins = turn(bank16(key)[0:2 * E, k * P:(k + 1) * P], src[:, k, :], id16[:, :])
                ins.then_inc(work_full, 1)

            def scores(b, s):
                pair, j = s // NB, s % NB
                if s == 0:
                    pe.wait_ge(qk_turned, upto(b, 4 * NB, 4 * NB))
                for half in range(2):
                    n = 2 * s + half
                    pe.wait_ge(relu_done, upto(b, 2 * STEPS, n - 1))
                    rows = slice(64 * half, 64 * half + 64)
                    mm(sim[half][:, :], kt[rows, pair, j * P:(j + 1) * P], qt[rows, pair, :], start=True,
                       stop=True).then_inc(sim_full, 1)

            def values(b, s):
                pair, j = s // NB, s % NB
                pe.wait_ge(pl_done, upto(b, 2 * STEPS, 2 * s + 2))
                if pair == 0:
                    pe.wait_ge(v_lo, upto(b, 2 * NB, 2 * (j + 1)))
                if j == 0:
                    pe.wait_ge(agg_done, upto(b, NP_, pair))
                for i, (vv, pp) in enumerate(((vh, ph), (vl, ph), (vh, pl))):
                    for half in range(2):
                        h = 2 * pair + half
                        ins = mm(av[64 * half:64 * half + 64, :], vv[:, j, h * DV:(h + 1) * DV],
                                 pp[:, (2 * s + half) % NH_, :], start=(j == 0 and i == 0),
                                 stop=(j == NB - 1 and i == 2))
                ins.then_inc(av_step, 1)

            def head_sums(b, t):
                pe.wait_ge(agg_sq_done, upto(b, NP_, t + 1))
                pe.wait_ge(*bank_read(b, ("N", t)))
                for k in range(NB):
                    ins = mm(bank(("N", t))[:, 2 * k:2 * k + 2], sq[:, t % 2, k * P:(k + 1) * P], pair_sel[:, :],
                             start=True, stop=True)
                ins.then_inc(work_full, 1)

            def item(b, kind, e):
                n = ORDER.index(e)
                cols = slice(e * P, (e + 1) * P)
                if kind == "c":
                    pe.wait_ge(ct_done, upto(b, 1, 1))
                    pe.wait_ge(*bank_read(b, (kind, e)))
                    for half in range(2):
                        ins = mm(bank((kind, e))[64 * half:64 * half + 64, :], sel16[:, e * DV:(e + 1) * DV], ct[:, :],
                                 start=True, stop=True)
                    ins.then_inc(work_full, 1)
                elif kind in "gu":
                    pe.wait_ge(*bank_read(b, (kind, e)))
                    wh, wl = (gate_h, gate_l) if kind == "g" else (up_h, up_l)
                    ins = products(bank((kind, e))[:, :], ([wh[:, m, cols] for m in range(KD)],
                                                           [wl[:, m, cols] for m in range(KD)]),
                                   ([xh[:, m, :] for m in range(KD)], [xl[:, m, :] for m in range(KD)]))
                    ins.then_inc(work_full, 1)
                else:
                    pe.wait_ge(h_hi, upto(b, EA, n + 1))
                    pe.wait_ge(h_lo, upto(b, EA, n + 1))
                    if n == 0:
                        pe.wait_ge(y_done, upto(b, KD, 0))
                    for m in range(KD):
                        mc = slice(m * P, (m + 1) * P)
                        ins = products(acc[m][:, :], ([down_h[:, e, mc]], [down_l[:, e, mc]]),
                                       ([hh[:, n % 2, :]], [hl[:, n % 2, :]]), first=(n == 0), last=False)
                    ins.then_inc(down_done, 1)

            def gates(b, t):
                pe.wait_ge(*bank_read(b, ("G", t)))
                cols = slice(G_AT + t * P, G_AT + (t + 1) * P)
                products(bank(("G", t))[:, :], ([wa_h[:, m, cols] for m in range(KD)],
                                                [wa_l[:, m, cols] for m in range(KD)]),
                         ([xh[:, m, :] for m in range(KD)], [xl[:, m, :] for m in range(KD)])).then_inc(work_full, 1)

            def spread(b, t):
                pe.wait_ge(wt_done, upto(b, 1, 1))
                pe.wait_ge(*bank_read(b, ("WB", t)))
                mm(bank(("WB", t))[:, :], sel16[:, t * P:(t + 1) * P], wt[:, :], start=True,
                   stop=True).then_inc(work_full, 1)

            def output(b, t):
                pe.wait_ge(a_lo, upto(b, NP_, t + 1))
                for m in range(KD):
                    mc = slice(m * P, (m + 1) * P)
                    ins = products(acc[m][:, :], ([wo_h[:, t, mc]], [wo_l[:, t, mc]]),
                                   ([ah[:, t % 2, :]], [al[:, t % 2, :]]), first=False, last=(t == NP_ - 1))
                ins.then_inc(out_mm, 1)

            for k in range(NB):
                turn_tokens(0, k)

            def body(b, last):
                router(b)
                for k in range(NB):
                    project(b, ("QK", k), k, 0, QK_W)
                for n in range(2 * NB):
                    project(b, ("V", n), n // 2, V_AT + (n % 2) * T, T)
                for n in range(4 * NB):
                    turn_qk(b, n)
                for s in range(STEPS):
                    if s == CT_STEP:
                        pe.wait_ge(route_step, upto(b, ROUTE_STEPS, ROUTE_STEPS))
                        turn_small(b, ("CT", 0), cst)
                    scores(b, s)
                    if s % NB == 1 and s > NB:
                        head_sums(b, s // NB - 1)
                    for kind, e in PLAN[s]:
                        item(b, kind, e)
                    if s >= 1:
                        values(b, s - 1)
                values(b, STEPS - 1)
                head_sums(b, NP_ - 1)
                gates(b, 0)
                gates(b, 1)
                pe.wait_ge(an_step, upto(b, HEAD_STEPS, HEAD_STEPS))
                turn_small(b, ("WT", 0), wst)
                spread(b, 0)
                for t in range(NP_):
                    if t + 2 < NP_:
                        gates(b, t + 2)
                    if t + 1 < NP_:
                        spread(b, t + 1)
                    if t == NP_ - 1 and not last:
                        for k in range(NB):
                            turn_tokens(b + 1, k)
                    output(b, t)

            rounds(pe, body)


def split_weights(nc, x, wa, w_gate, w_up, w_down, w_out, w_router, bias, ident, ident_h, sel, tri, parts,
                  wr, bias_sb, id32, id16, sel16, pair_sel, tri_sb, eps_qkv, inv_a, inv_m, up_routed, up_shared,
                  attn_scale, out_scale):
    with ExitStack() as ctx:
        def sb(name, shape, dt=F32):
            return ctx.enter_context(nc.sbuf_tensor(name, shape, dt))

        def sem(name):
            return ctx.enter_context(nc.semaphore(name))

        raw = {"wa": sb("raw_wa", [P, KD * WA_W]), "gate": sb("raw_gate", [P, KD * EA * P]),
               "up": sb("raw_up", [P, KD * EA * P]), "down": sb("raw_down", [P, EA * D]),
               "wo": sb("raw_wo", [P, NP_ * D])}
        source = {"wa": wa.rearrange("(m p) n -> p m n", p=P), "gate": w_gate.rearrange("(m p) n -> p m n", p=P),
                  "up": w_up.rearrange("(m p) n -> p m n", p=P), "down": w_down, "wo": w_out}
        split = {"wa": KD, "gate": KD, "up": KD, "down": EA, "wo": NP_}
        groups = [("wa",), ("gate", "up"), ("down", "wo")]
        floor = [2.0 ** -40, 2.0 ** -6, 2.0 ** -20]
        flat = {k: tuple(t[:, :, :].rearrange("p a n -> p (a n)") for t in v) for k, v in parts.items()}
        order = [k for g in groups for k in g]
        big = sb("big", [P, len(order)])
        top, every = sb("top", [P, 3]), sb("every", [P, 3])
        power, scale = sb("power", [P, 3]), sb("scale", [P, 3])
        sh = sb("sh", [P, 2])
        loaded = {k: sem(f"loaded_{k}") for k in order}
        small_loaded, big_done, top_done = sem("small_loaded"), sem("big_done"), sem("top_done")
        every_done, scale_step, hi_done, lo_done = (sem("every_done"), sem("scale_step"), sem("hi_done"),
                                                    sem("lo_done"))
        set_done = sem("set_done")
        SCALE_STEPS = 4
        CUT = 2560
        cuts = {k: [(a, min(a + CUT, raw[k].shape[1])) for a in range(0, raw[k].shape[1], CUT)] for k in order}
        pieces = [(k, a, z) for k in order for a, z in cuts[k]]

        block = ctx.enter_context(nc.Block())

        @block.sync
        def _(sp):
            for k in order:
                sp.dma_start(raw[k][:, :].rearrange("p (a n) -> p a n", a=split[k]), source[k]).then_inc(loaded[k], 16)
            sp.wait_ge(small_loaded, 16 * 6)

        @block.scalar
        def _(act):
            act.dma_start(wr[:, :, :], w_router.rearrange("(m p) e -> p m e", p=P)).then_inc(small_loaded, 16)
            act.dma_start(bias_sb[:, :], bias).then_inc(small_loaded, 16)
            act.dma_start(id32[:, :], ident).then_inc(small_loaded, 16)
            act.dma_start(id16[:, :], ident_h).then_inc(small_loaded, 16)
            act.dma_start(sel16[:, :], sel).then_inc(small_loaded, 16)
            act.dma_start(tri_sb[:, :], tri).then_inc(small_loaded, 16)
            for k, a, z in pieces:
                g = next(i for i, names in enumerate(groups) if k in names)
                act.wait_ge(scale_step, SCALE_STEPS * (g + 1))
                nc.scalar.activation(flat[k][0][:, a:z], raw[k][:, a:z], ACT.Copy,
                                     scale=scale[:, g:g + 1]).then_inc(hi_done, 1)

        @block.gpsimd
        def _(pool):
            for half in range(2):
                rows = slice(64 * half, 64 * half + 64)
                pool.memset(pair_sel[rows, half:half + 1], 1.0).then_inc(set_done, 1)
                pool.memset(pair_sel[rows, 1 - half:2 - half], 0.0).then_inc(set_done, 1)
            pool.wait_ge(set_done, 4)
            for g in range(3):
                pool.wait_ge(top_done, g + 1)
                pool.partition_all_reduce(every[:, g:g + 1], top[:, g:g + 1], P,
                                          bass.bass_isa.ReduceOp.max).then_inc(every_done, 1)

        @block.vector
        def _(dve):
            v = nc.vector
            steps = [0]

            def link(ins):
                steps[0] += 1
                ins.then_inc(scale_step, 1)
                dve.wait_ge(scale_step, steps[0])

            def largest(g):
                for k in groups[g]:
                    n = order.index(k)
                    dve.wait_ge(loaded[k], 16)
                    v.tensor_reduce(big[:, n:n + 1], raw[k][:, :], AX.X, ALU.max,
                                    apply_absolute_value=True).then_inc(big_done, 1)
                ns = [order.index(k) for k in groups[g]]
                dve.wait_ge(big_done, ns[-1] + 1)
                v.tensor_reduce(top[:, g:g + 1], big[:, ns[0]:ns[-1] + 1], AX.X, ALU.max).then_inc(top_done, 1)

            def scales(g):
                dve.wait_ge(every_done, g + 1)
                c = slice(g, g + 1)
                link(v.tensor_scalar(power[:, c], every[:, c], floor[g], None, ALU.max))
                link(v.tensor_scalar(power[:, c].bitcast(I32), power[:, c].bitcast(I32), 0x7F800000, None,
                                     ALU.bitwise_and))
                link(v.reciprocal(scale[:, c], power[:, c]))
                link(v.tensor_scalar(scale[:, c], scale[:, c], 2.0 ** W_EXP, None, ALU.mult))

            def low_parts(g):
                for n, (k, a, z) in enumerate(pieces):
                    if k in groups[g]:
                        dve.wait_ge(hi_done, n + 1)
                        v.scalar_tensor_tensor(out=flat[k][1][:, a:z], in0=raw[k][:, a:z], scalar=scale[:, g:g + 1],
                                               in1=flat[k][0][:, a:z], op0=ALU.mult,
                                               op1=ALU.subtract).then_inc(lo_done, 1)

            for g in range(3):
                largest(g)
                scales(g)
                low_parts(g)
            back = 2.0 ** -W_EXP
            mult = ALU.mult
            link(v.tensor_scalar(eps_qkv[:, :], scale[:, 0:1], scale[:, 0:1], EPS_L2 ** 2, mult, mult))
            link(v.tensor_scalar(inv_a[:, :], power[:, 0:1], back, None, mult))
            link(v.tensor_scalar(inv_m[:, :], power[:, 1:2], back, None, mult))
            link(v.reciprocal(sh[:, 0:1], power[:, 1:2]))
            link(v.tensor_scalar(up_shared[:, :], sh[:, 0:1], 2.0 ** (-5 - W_EXP), None, mult))
            link(v.tensor_scalar(up_routed[:, :], up_shared[:, :], 1.0 / C_SCALE, None, mult))
            link(v.tensor_scalar(sh[:, 1:2], sh[:, 0:1], sh[:, 0:1], 2.0 ** -5, mult, mult))
            link(v.tensor_scalar(attn_scale[:, :], sh[:, 1:2], AG_UNSCALE / C_SCALE, None, mult))
            link(v.reciprocal(sh[:, 0:1], sh[:, 1:2]))
            link(v.tensor_scalar(out_scale[:, :], power[:, 2:3], sh[:, 0:1], back, mult, mult))


_OUT = (B, D, T)


def kernel(L0_attn_tokens, L0_attn_Wqg, L0_attn_Wkv, L0_attn_Wout, L0_ffn_router_weight, L0_ffn_e_bias,
           L0_ffn_gate_w, L0_ffn_up_w, L0_ffn_down_w, L0_ffn_sh_gate_w, L0_ffn_sh_up_w, L0_ffn_sh_down_w):
    import numpy as np
    import concourse.bacc as bacc
    from concourse.bass_utils import run_bass_kernel_spmd

    asc = np.ascontiguousarray
    tokens = np.asarray(L0_attn_tokens)
    wqg = np.asarray(L0_attn_Wqg).reshape(D, H, DK + DV)
    wkv = np.asarray(L0_attn_Wkv).reshape(D, H, DK + DV)
    wa = np.concatenate([wqg[:, :, :DK].reshape(D, -1), wkv[:, :, :DK].reshape(D, -1),
                         wkv[:, :, DK:].reshape(D, -1), wqg[:, :, DK:].reshape(D, -1)], axis=1)

    def rows(routed, shared):
        return asc(np.concatenate([np.asarray(routed).reshape(E * P, D), np.asarray(shared)], axis=0).T)

    down = np.concatenate([np.asarray(L0_ffn_down_w).transpose(2, 0, 1),
                           np.asarray(L0_ffn_sh_down_w).reshape(D, ES, P).transpose(2, 1, 0)], axis=1)
    sel = np.zeros((2, H, H, DV), np.float16)
    for h in range(H):
        sel[:, h, h, :] = 1.0
    tri = np.tril(np.ones((NG, NG), np.float32), -1).reshape(1, -1)
    arrays = {
        "x": tokens,
        "x_t": asc(tokens.transpose(0, 2, 1)),
        "wa": asc(wa),
        "w_gate": rows(L0_ffn_gate_w, L0_ffn_sh_gate_w),
        "w_up": rows(L0_ffn_up_w, L0_ffn_sh_up_w),
        "w_down": asc(down),
        "w_out": asc(np.asarray(L0_attn_Wout).reshape(NP_, P, D).transpose(1, 0, 2)),
        "w_router": asc(np.asarray(L0_ffn_router_weight).T),
        "bias": asc(np.broadcast_to(np.asarray(L0_ffn_e_bias), (P, E))),
        "ident": np.eye(P, dtype=np.float32),
        "ident_h": np.eye(P, dtype=np.float16),
        "sel": sel.reshape(2 * H, H * DV),
        "tri": asc(np.broadcast_to(tri, (P, NG * NG))),
    }
    nc = bacc.Bacc("TRN2", target_bir_lowering=False, num_devices=1)
    args = [nc.dram_tensor(n, a.shape, mybir.dt.from_np(a.dtype), kind="ExternalInput").ap() for n, a in arrays.items()]
    out = nc.dram_tensor("out_t", _OUT, F32, kind="ExternalOutput").ap()
    build_layer(nc, *args, out)
    r = run_bass_kernel_spmd(nc, [arrays], core_ids=[0])
    return asc(r.results[0]["out_t"].transpose(0, 2, 1))
```

```python
from contextlib import ExitStack

import concourse.bass as bass
from concourse import mybir

F32 = mybir.dt.float32
F16 = mybir.dt.float16
I32 = mybir.dt.int32
ALU = mybir.AluOpType
ACT = mybir.ActivationFunctionType
AX = mybir.AxisListType

P = 128
B, T, D = 16, 512, 256
H, DK, DV = 16, 16, 64
E, NG, GE = 16, 4, 4
ES = 2
EA = E + ES
NB = T // P
KD = D // P
NP_ = H // 2
QK_W = 2 * H * DK
V_AT = QK_W
G_AT = V_AT + H * DV
WA_W = G_AT + H * DV
RSQRT_MAGIC = 0x5F3759DF

W_EXP = 9
QK_SCALE = 2.0 ** 7
S_SCALE = 2.0 ** -7
P_SCALE = 2.0 ** 14
V_SCALE = 2.0 ** 8
C_SCALE = 2.0 ** 8
AG_UNSCALE = 1.0 / (P_SCALE * V_SCALE)
EPS_L2 = 1e-12
EPS_LN = 1e-5
EPS_TW = 1e-20
ROUTE_SCALE = 2.5

STEPS = NP_ * NB
ORDER = list(range(E, EA)) + list(range(E))
ROUTED = [e for e in ORDER if e < E]


def expert_items():
    items = []
    for n, e in enumerate(ORDER):
        if e < E:
            items.append(("c", e))
        items += [("g", e), ("u", e)]
        if n == 1:
            items.append(("d", ORDER[0]))
        if n >= 3:
            items.append(("d", ORDER[n - 2]))
    return items + [("d", ORDER[-2]), ("d", ORDER[-1])]


COST = {"c": 1, "g": 6, "u": 6, "d": 6}
HEAD_ITEMS = 5
TAIL_ITEMS = 8
ITEMS = expert_items()


NORM_STEPS = range(1, 9)
ROUTE_FROM = 14
NEXT_AT = {9 + k: [("X", k)] for k in range(NB)} | {13: [("R", 0)]}


def plan_steps():
    items = ITEMS[HEAD_ITEMS:len(ITEMS) - TAIL_ITEMS]
    total = sum(COST[k] for k, _ in items)
    steps, due, done, at, held = [], [], 0, 0, False
    for s in range(STEPS):
        if s % NB == 2 and s > NB:
            due.append(("N", s // NB - 1))
        due += NEXT_AT.get(s, [])
        mine = []
        while True:
            if due and not held:
                mine.append(due.pop(0))
            elif at < len(items) and (done + COST[items[at][0]] / 2 <= total * (s + 1) / STEPS or s == STEPS - 1):
                kind = items[at][0]
                held = True if kind == "c" else False if kind == "u" else held
                mine.append(items[at])
                done += COST[kind]
                at += 1
            else:
                break
        steps.append(mine)
    assert at == len(items) and not due
    return steps


HEAD = ITEMS[:HEAD_ITEMS]
PLAN = plan_steps()
LATE = ITEMS[len(ITEMS) - TAIL_ITEMS:]
TAIL = ([("G", 0), LATE[0], ("AV", STEPS - 1), LATE[1], ("N", NP_ - 1), ("G", 1)] + LATE[2:4] + [("TH", 0)] + LATE[4:6]
        + [("WT", 0), LATE[6], ("G", 2), ("WB", 0), ("WB", 1), LATE[7]])
AHEAD = ("X", "R", "QK", "CT")


def pe_order():
    seq = [("V", n) for n in range(2 * NB)]
    for k in range(NB):
        seq += HEAD[k:k + 1] + [("T", 4 * k + c) for c in range(4)]
    seq += HEAD[NB:]
    for s in range(STEPS):
        seq.append(("S", s))
        seq += PLAN[s]
        if s >= 1:
            seq.append(("AV", s - 1))
    seq += TAIL
    for t in range(NP_):
        if t + 3 < NP_:
            seq.append(("G", t + 3))
        if t + 2 < NP_:
            seq.append(("WB", t + 2))
        if t >= NP_ - 2:
            seq.append(("QK", t - (NP_ - 2)))
        seq.append(("O", t))
    return seq + [("QK", 2), ("QK", 3), ("CT", 0)]


def work_order():
    return [key for key in pe_order() if key[0] not in ("S", "AV", "d", "TH", "O")]


ORDERED = work_order()
WORK = {key: n for n, key in enumerate(ORDERED)}
FIRST = [key for key in ORDERED if key[0] in AHEAD]
LAST = [key for key in ORDERED if key[0] not in AHEAD]
NW = 3
PER = len(WORK)
assert PER % NW == 0
RSQRT_STEPS = 11
ROUTE_STEPS = 34
HEAD_STEPS = 1 + RSQRT_STEPS + 4


def build_layer(nc, x, x_t, wa, w_gate, w_up, w_down, w_out, w_router, bias, ident, ident_h, sel, tri, out_t):
    with ExitStack() as ctx:
        def sb(name, shape, dt=F32):
            return ctx.enter_context(nc.sbuf_tensor(name, shape, dt))

        def sem(name):
            return ctx.enter_context(nc.semaphore(name))

        wa_h, wa_l = sb("wa_h", [P, KD, WA_W], F16), sb("wa_l", [P, KD, WA_W], F16)
        gate_h, gate_l = sb("gate_h", [P, KD, EA * P], F16), sb("gate_l", [P, KD, EA * P], F16)
        up_h, up_l = sb("up_h", [P, KD, EA * P], F16), sb("up_l", [P, KD, EA * P], F16)
        down_h, down_l = sb("down_h", [P, EA, D], F16), sb("down_l", [P, EA, D], F16)
        wo_h, wo_l = sb("wo_h", [P, NP_, D], F16), sb("wo_l", [P, NP_, D], F16)
        wr = sb("wr", [P, KD, E])
        bias_sb = sb("bias_sb", [P, E])
        id32, id16 = sb("id32", [P, P]), sb("id16", [P, P], F16)
        sel16 = sb("sel16", [2 * H, H * DV], F16)
        pair_sel = sb("pair_sel", [P, 2])
        tri_sb = sb("tri_sb", [P, NG * NG])
        eps_qkv = sb("eps_qkv", [P, 1])
        inv_a, inv_m = sb("inv_a", [P, 1]), sb("inv_m", [P, 1])
        up_routed, up_shared = sb("up_routed", [P, 1]), sb("up_shared", [P, 1])
        attn_scale, out_scale = sb("attn_scale", [P, 1]), sb("out_scale", [P, 1])

        split_weights(nc, x, wa, w_gate, w_up, w_down, w_out, w_router, bias, ident, ident_h, sel, tri,
                      dict(wa=(wa_h, wa_l), gate=(gate_h, gate_l), up=(up_h, up_l), down=(down_h, down_l),
                           wo=(wo_h, wo_l)),
                      wr, bias_sb, id32, id16, sel16, pair_sel, tri_sb, eps_qkv, inv_a, inv_m, up_routed,
                      up_shared, attn_scale, out_scale)

        x_sb = sb("x_sb", [P, NB, D])
        y_sb = sb("y_sb", [P, KD, T])
        xf = sb("xf", [P, KD, T])
        xh, xl = sb("xh", [P, KD, T], F16), sb("xl", [P, KD, T], F16)
        NR_, NH_ = 4, 4
        ring = sb("ring", [P, NR_, T])
        qk_raw = ring[:, :, :]
        ph, pl = sb("ph", [P, NH_, T], F16), sb("pl", [P, NH_, T], F16)
        wide = sb("wide", [P, NP_, T])
        v_raw = wide[:, :, :].rearrange("p (k a) t -> p k (a t)", k=NB)
        agg = wide
        qst, kst = sb("qst", [P, 2, 2 * T], F16), sb("kst", [P, 2, 2 * T], F16)
        qt, kt = sb("qt", [P, NP_, T], F16), sb("kt", [P, NP_, T], F16)
        vh, vl = sb("vh", [P, NB, H * DV], F16), sb("vl", [P, NB, H * DV], F16)
        sq = sb("sq", [P, 2, T])
        sg = sb("sg", [P, 2, T])
        gate_sb = sb("gate_sb", [P, 3, T])
        hf = sb("hf", [P, 2, T])
        hh, hl = sb("hh", [P, 2, T], F16), sb("hl", [P, 2, T], F16)
        ah, al = sb("ah", [P, 2, T], F16), sb("al", [P, 2, T], F16)
        ct, wt = sb("ct", [2 * E, T], F16), sb("wt", [2 * H, T], F16)
        cst, wst = sb("cst", [P, NB, 2 * E], F16), sb("wst", [P, NB, 2 * H], F16)
        stats = sb("stats", [P, NB, 6])
        ln_m, ln_mean = sb("ln_m", [P, NB]), sb("ln_mean", [P, NB])
        ln_a, ln_y, ln_t = sb("ln_a", [P, NB]), sb("ln_y", [P, NB]), sb("ln_t", [P, NB])
        qn_a, qn_y, qn_t = (sb(f"qn_{c}", [P, NB, 2 * H]) for c in "ayt")
        vn_a, vn_y, vn_t = (sb(f"vn_{c}", [P, NB, H]) for c in "ayt")
        an_a, an_y, an_t = sb("an_a", [P, NB, H]), sb("an_y", [P, NB, H]), vn_t
        th = an_t
        sc_s, sc_b, sc_m = (sb(f"sc_{c}", [P, NB, E]) for c in "sbm")
        pmax, pmin = sb("pmax", [P, NB * NG, 2]), sb("pmin", [P, NB * NG, 2])
        g_a, g_b, g_c, g_s = (sb(f"g_{c}", [P, NB * NG]) for c in "abcs")
        g_gt, g_eq = sb("g_gt", [P, NB * NG, NG]), sb("g_eq", [P, NB * NG, NG])
        top8 = sb("top8", [P, NB, 8])
        PAD = 8
        pre = [sb(f"pre{n}", [P, NB, PAD + E]) for n in range(2)]
        more, cnt = sb("more", [P, NB, E]), sb("cnt", [P, NB])

        sim = [ctx.enter_context(nc.psum_tensor(f"sim{n}", [P, T], F32)) for n in range(2)]
        av = ctx.enter_context(nc.psum_tensor("av", [P, T], F32))
        acc = [ctx.enter_context(nc.psum_tensor(f"acc{n}", [P, T], F32)) for n in range(KD)]
        wk = [ctx.enter_context(nc.psum_tensor(f"wk{n}", [P, T], F32)) for n in range(NW)]

        x_loaded, res_loaded, stored = sem("x_loaded"), sem("res_loaded"), sem("stored")
        work_full = sem("work_full")
        sim_full, relu_done, square_done = sem("sim_full"), sem("relu_done"), sem("square_done")
        ph_done, pl_done, av_step = sem("ph_done"), sem("pl_done"), sem("av_step")
        agg_done, agg_sq_done = sem("agg_done"), sem("agg_sq_done")
        down_done, y_done = sem("down_done"), sem("y_done")
        ln_step, xn_done, xf_done = sem("ln_step"), sem("xn_done"), sem("xf_done")
        xh_done, xl_done = sem("xh_done"), sem("xl_done")
        raw_done, rawsq_done, norm_done = sem("raw_done"), sem("rawsq_done"), sem("norm_done")
        qn_step, vn_step, an_step = sem("qn_step"), sem("vn_step"), sem("an_step")
        qkn_done, vn_done = sem("qkn_done"), sem("vn_done")
        qk_hi, qk_lo, qk_turned = sem("qk_hi"), sem("qk_lo"), sem("qk_turned")
        v_hi, v_lo = sem("v_hi"), sem("v_lo")
        score_done, route_step, ct_done = sem("score_done"), sem("route_step"), sem("ct_done")
        silu_done, sgc_done = sem("silu_done"), sem("sgc_done")
        hf_done, h_hi, h_lo = sem("hf_done"), sem("h_hi"), sem("h_lo")
        n_done, th_done, wt_done = sem("n_done"), sem("th_done"), sem("wt_done")
        gsilu_done, gate_done, gw_done = sem("gsilu_done"), sem("gate_done"), sem("gw_done")
        a_done, a_hi, a_lo = sem("a_done"), sem("a_hi"), sem("a_lo")
        out_mm = sem("out_mm")

        def upto(b, per, c):
            return max(b * per + c, 0) if isinstance(b, int) else b * per + c

        def place(b, key):
            if key[0] not in AHEAD and isinstance(b, int) and b == B - 1:
                return LAST.index(key)
            return WORK[key]

        def filled(b, key):
            if isinstance(b, int) and b < 0:
                return 0
            if key[0] in AHEAD:
                if isinstance(b, int) and b == 0:
                    return FIRST.index(key) + 1
                return upto(b - 1, PER, len(FIRST) + WORK[key] + 1)
            return upto(b, PER, len(FIRST) + place(b, key) + 1)

        def bank(b, key):
            if key[0] in AHEAD and isinstance(b, int) and b == 0:
                return wk[FIRST.index(key) % NW]
            return wk[(len(FIRST) + place(b, key)) % NW]

        def bank16(b, key):
            return bank(b, key)[:, :].bitcast(F16)

        def read(b, key):
            kind, n = key
            s, per, count = {
                "R": (score_done, 1, 1),
                "QK": (raw_done, 3 * NB, n + 1),
                "V": (raw_done, 3 * NB, NB + n + 1),
                "T": (qk_turned, 4 * NB, n + 1),
                "CT": (ct_done, 1, 1),
                "c": (sgc_done, E, ROUTED.index(n) + 1 if n in ROUTED else 0),
                "g": (silu_done, EA, ORDER.index(n) + 1),
                "u": (hf_done, EA, ORDER.index(n) + 1),
                "N": (n_done, NP_, n + 1),
                "G": (gsilu_done, NP_, n + 1),
                "WT": (wt_done, 1, 1),
                "WB": (gw_done, NP_, n + 1),
                "X": (xf_done, NB, n + 1),
            }[kind]
            return s, upto(b, per, count)

        def bank_read(b, key):
            if key[0] in AHEAD:
                b = b - 1
            if isinstance(b, int) and b < 0:
                n = FIRST.index(key) - NW
                return read(0, FIRST[n]) if n >= 0 else (xf_done, 0)
            n = place(b, key) - NW
            if n >= 0:
                before = (LAST if isinstance(b, int) and b == B - 1 else ORDERED)[n]
                return read(b + 1 if before[0] in AHEAD else b, before)
            if isinstance(b, int) and b == 0:
                return read(0, FIRST[n])
            return read(b if ORDERED[n][0] in AHEAD else b - 1, ORDERED[n])

        def rounds(eng, body):
            body(0, False)
            with eng.Fori(1, B - 1) as b:
                body(b, False)
            body(B - 1, True)

        block = ctx.enter_context(nc.Block())

        @block.sync
        def _(sp):
            def load_x(b):
                sp.wait_ge(work_full, filled(b - 1, ("X", NB - 1)))
                sp.dma_start(x_sb[:, :, :], x[b].rearrange("(k p) d -> p k d", p=P)).then_inc(x_loaded, 16)

            load_x(0)

            def body(b, last):
                if not last:
                    load_x(b + 1)
                sp.wait_ge(stored, upto(b, 16, 0))
                sp.dma_start(y_sb[:, :, :], x_t[b].rearrange("(m p) t -> p m t", p=P)).then_inc(res_loaded, 16)
                sp.wait_ge(y_done, upto(b, KD, KD))
                sp.dma_start(out_t[b].rearrange("(m p) t -> p m t", p=P), y_sb[:, :, :]).then_inc(stored, 16)

            rounds(sp, body)
            sp.wait_ge(stored, 16 * B)

        @block.vector
        def _(dve):
            v = nc.vector

            class Chain:

                def __init__(self, s, b, per):
                    self.s, self.b, self.per, self.n = s, b, per, 0

                def __call__(self, ins):
                    ins.then_inc(self.s, 1)
                    self.n += 1
                    dve.wait_ge(self.s, self.b * self.per + self.n)

                def end(self):
                    assert self.n == self.per, (self.n, self.per)

            def rsqrt_guess(link, a, y):
                link(v.tensor_scalar(y.bitcast(I32), a.bitcast(I32), 1, None, ALU.logical_shift_right))
                link(v.tensor_scalar(y.bitcast(I32), y.bitcast(I32), -1.0, float(RSQRT_MAGIC), ALU.mult, ALU.add))

            def newton(link, a, y, t):
                link(v.tensor_tensor(t, y, y, ALU.mult))
                link(v.scalar_tensor_tensor(out=t, in0=a, scalar=-0.5, in1=t, op0=ALU.mult, op1=ALU.mult))
                link(v.scalar_tensor_tensor(out=y, in0=t, scalar=1.5, in1=y, op0=ALU.add, op1=ALU.mult))

            def rsqrt(link, a, y, t):
                rsqrt_guess(link, a, y)
                for _ in range(3):
                    newton(link, a, y, t)

            def layernorm(b):
                link = Chain(ln_step, b, 4 + RSQRT_STEPS)
                a, y, t = ln_a[:, :], ln_y[:, :], ln_t[:, :]
                dve.wait_ge(x_loaded, upto(b, 16, 16))
                dve.wait_ge(xn_done, upto(b, NB, 0))
                for k in range(NB):
                    ins = v.bn_stats(stats[:, k, :], x_sb[:, k, :])
                    if k < NB - 1:
                        yield
                yield link(ins)
                v.tensor_tensor(ln_m[:, :], stats[:, :, 1], stats[:, :, 4], ALU.add)
                v.tensor_tensor(a, stats[:, :, 2], stats[:, :, 5], ALU.add)
                yield link(v.tensor_tensor(t, stats[:, :, 1], stats[:, :, 4], ALU.subtract))
                v.tensor_scalar(ln_mean[:, :], ln_m[:, :], 0.5, None, ALU.mult)
                v.tensor_scalar(a, a, 1.0 / D, EPS_LN, ALU.mult, ALU.add)
                yield link(v.scalar_tensor_tensor(out=y, in0=t, scalar=0.25, in1=t, op0=ALU.mult, op1=ALU.mult))
                yield link(v.tensor_tensor(a, a, y, ALU.add))
                yield rsqrt_guess(link, a, y)
                for _ in range(3):
                    yield newton(link, a, y, t)
                link.end()
                for k in range(NB):
                    v.tensor_scalar(x_sb[:, k, :], x_sb[:, k, :], ln_mean[:, k:k + 1], ln_y[:, k:k + 1],
                                    ALU.subtract, ALU.mult).then_inc(xn_done, 1)
                    yield

            def tokens_lo(b):
                dve.wait_ge(xf_done, upto(b, NB, NB))
                dve.wait_ge(xh_done, upto(b, 1, 1))
                dve.wait_ge(work_full, filled(b - 1, ("G", NP_ - 1)))
                v.tensor_tensor(xl[:, :, :], xf[:, :, :], xh[:, :, :], ALU.subtract).then_inc(xl_done, 1)

            def sums(b, n):
                dve.wait_ge(rawsq_done, upto(b, 3 * NB, n + 1))
                if n < NB:
                    v.tensor_reduce(qn_a[:, n, :], sq[:, n % 2, :].rearrange("p (h d) -> p h d", d=DK), AX.X,
                                    ALU.add).then_inc(norm_done, 1)
                else:
                    k, half = (n - NB) // 2, (n - NB) % 2
                    v.tensor_reduce(vn_a[:, k, half * 8:half * 8 + 8],
                                    sq[:, n % 2, :].rearrange("p (h d) -> p h d", d=DV), AX.X,
                                    ALU.add).then_inc(norm_done, 1)

            def norms_begin(b, which):
                if which == "qk":
                    dve.wait_ge(qkn_done, upto(b, NB, 0))
                    dve.wait_ge(norm_done, upto(b, 3 * NB, NB))
                    link, a, y = Chain(qn_step, b, 1 + RSQRT_STEPS), qn_a, qn_y
                else:
                    dve.wait_ge(vn_done, upto(b, 2 * NB, 0))
                    dve.wait_ge(norm_done, upto(b, 3 * NB, 3 * NB))
                    link, a, y = Chain(vn_step, b, 1 + RSQRT_STEPS), vn_a, vn_y
                link(v.tensor_scalar(a[:, :, :], a[:, :, :], eps_qkv[:, 0:1], None, ALU.max))
                rsqrt_guess(link, a[:, :, :], y[:, :, :])
                return link

            def norms_round(link, which):
                a, y, t = (qn_a, qn_y, qn_t) if which == "qk" else (vn_a, vn_y, vn_t)
                newton(link, a[:, :, :], y[:, :, :], t[:, :, :])

            def unit_qk(b, k):
                dve.wait_ge(raw_done, upto(b, 3 * NB, k + 1))
                blk = qk_raw[:, k, :].rearrange("p (h d) -> p h d", d=DK)
                v.scalar_tensor_tensor(out=blk, in0=blk, scalar=QK_SCALE,
                                       in1=qn_y[:, k, :].unsqueeze(2).to_broadcast([P, 2 * H, DK]),
                                       op0=ALU.mult, op1=ALU.mult).then_inc(qkn_done, 1)

            def unit_v(b, n):
                k, half = n // 2, n % 2
                dve.wait_ge(raw_done, upto(b, 3 * NB, NB + n + 1))
                blk = v_raw[:, k, half * T:half * T + T].rearrange("p (h d) -> p h d", d=DV)
                v.scalar_tensor_tensor(out=blk, in0=blk, scalar=V_SCALE,
                                       in1=vn_y[:, k, half * 8:half * 8 + 8].unsqueeze(2).to_broadcast([P, 8, DV]),
                                       op0=ALU.mult, op1=ALU.mult).then_inc(vn_done, 1)

            def turned(b, n):
                k, c = n // 4, n % 4
                dve.wait_ge(work_full, filled(b, ("T", n)))
                dve.wait_ge(sim_full, upto(b, 2 * STEPS, 0))
                dst = (qt if c < 2 else kt)[:, 4 * (c % 2):4 * (c % 2) + 4, k * P:(k + 1) * P]
                ins = v.tensor_copy(dst, bank16(b, ("T", n))[:, 0:T].rearrange("p (m t) -> p m t", m=4))
                ins.then_inc(qk_turned, 1)

            tt = v.tensor_tensor

            def route(b):
                link = Chain(route_step, b, ROUTE_STEPS)
                dve.wait_ge(score_done, upto(b, 1, 1))
                yield link(tt(sc_b[:, :, :], sc_s[:, :, :], bias_sb[:, :].unsqueeze(1).to_broadcast([P, NB, E]), ALU.add))
                two = sc_b[:, :, :].rearrange("p k (g a c) -> p (k g) a c", a=2, c=2)
                yield link(tt(pmax[:, :, :], two[:, :, :, 0], two[:, :, :, 1], ALU.max))
                yield link(tt(pmin[:, :, :], two[:, :, :, 0], two[:, :, :, 1], ALU.min))
                yield link(tt(g_a[:, :], pmax[:, :, 0], pmax[:, :, 1], ALU.max))
                yield link(tt(g_b[:, :], pmax[:, :, 0], pmax[:, :, 1], ALU.min))
                yield link(tt(g_c[:, :], pmin[:, :, 0], pmin[:, :, 1], ALU.max))
                yield link(tt(g_b[:, :], g_b[:, :], g_c[:, :], ALU.max))
                yield link(tt(g_s[:, :], g_a[:, :], g_b[:, :], ALU.add))
                other = g_s[:, :].rearrange("p (k j) -> p k j", j=NG).unsqueeze(2).to_broadcast([P, NB, NG, NG])
                mine = g_s[:, :].rearrange("p (k g) -> p k g", g=NG).unsqueeze(3).to_broadcast([P, NB, NG, NG])
                tt(g_gt[:, :, :].rearrange("p (k g) j -> p k g j", k=NB), other, mine, ALU.is_gt)
                yield link(tt(g_eq[:, :, :].rearrange("p (k g) j -> p k g j", k=NB), other, mine, ALU.is_equal))
                eq = g_eq[:, :, :].rearrange("p (k g) j -> p k (g j)", k=NB)
                yield link(tt(eq, eq, tri_sb[:, :].unsqueeze(1).to_broadcast([P, NB, NG * NG]), ALU.mult))
                yield link(tt(g_gt[:, :, :], g_gt[:, :, :], g_eq[:, :, :], ALU.add))
                yield link(v.tensor_reduce(g_a[:, :], g_gt[:, :, :], AX.X, ALU.add))
                yield link(v.tensor_scalar(g_a[:, :], g_a[:, :], 1.5, None, ALU.is_lt))
                per_group = sc_m[:, :, :].rearrange("p k (g c) -> p (k g) c", c=GE)
                yield link(tt(per_group, sc_b[:, :, :].rearrange("p k (g c) -> p (k g) c", c=GE),
                        g_a[:, :].unsqueeze(2).to_broadcast([P, NB * NG, GE]), ALU.mult))
                yield link(v.tensor_scalar(sc_m[:, :, :], sc_m[:, :, :], 0.0, None, ALU.add))
                for n in range(2):
                    v.memset(pre[n][:, :, 0:PAD], 0.0)
                for k in range(NB):
                    ins = v.max(top8[:, k, :], sc_m[:, k, :])
                yield link(ins)
                fourth = top8[:, :, 3:4].to_broadcast([P, NB, E])
                yield link(tt(more[:, :, :], sc_m[:, :, :], fourth, ALU.is_gt))
                yield link(tt(pre[0][:, :, PAD:], sc_m[:, :, :], fourth, ALU.is_equal))
                yield link(v.tensor_copy(sc_b[:, :, :], pre[0][:, :, PAD:]))
                yield link(v.tensor_reduce(cnt[:, :], more[:, :, :], AX.X, ALU.add))
                for n, d in enumerate((1, 2, 4, 8)):
                    src, dst = pre[n % 2], pre[(n + 1) % 2]
                    yield link(tt(dst[:, :, PAD:], src[:, :, PAD:], src[:, :, PAD - d:PAD + E - d], ALU.add))
                yield link(tt(pre[0][:, :, PAD:], pre[0][:, :, PAD:], cnt[:, :].unsqueeze(2).to_broadcast([P, NB, E]),
                        ALU.add))
                yield link(v.scalar_tensor_tensor(out=sc_b[:, :, :], in0=pre[0][:, :, PAD:], scalar=4.5,
                                            in1=sc_b[:, :, :], op0=ALU.is_lt, op1=ALU.mult))
                yield link(tt(more[:, :, :], more[:, :, :], sc_b[:, :, :], ALU.add))
                yield link(tt(sc_s[:, :, :], sc_s[:, :, :], more[:, :, :], ALU.mult))
                yield link(v.tensor_reduce(cnt[:, :], sc_s[:, :, :], AX.X, ALU.add))
                yield link(v.tensor_scalar(cnt[:, :], cnt[:, :], EPS_TW, None, ALU.add))
                yield link(v.reciprocal(cnt[:, :], cnt[:, :]))
                yield link(v.scalar_tensor_tensor(out=sc_m[:, :, :], in0=sc_s[:, :, :], scalar=ROUTE_SCALE * C_SCALE,
                                            in1=cnt[:, :].unsqueeze(2).to_broadcast([P, NB, E]),
                                            op0=ALU.mult, op1=ALU.mult))
                dve.wait_ge(work_full, filled(b - 1, ("CT", 0)))
                yield link(v.tensor_copy(cst[:, :, 0:E], sc_m[:, :, :]))
                yield link(tt(cst[:, :, E:2 * E], sc_m[:, :, :], cst[:, :, 0:E], ALU.subtract))
                link.end()

            def probs(b, n):
                dve.wait_ge(square_done, upto(b, 2 * STEPS, n + 1))
                dve.wait_ge(av_step, upto(b, STEPS, n // 2 - 1))
                v.tensor_copy(ph[:, n % NH_, :], ring[:, n % NR_, :]).then_inc(ph_done, 1)

            def probs_lo(b, n):
                dve.wait_ge(ph_done, upto(b, 2 * STEPS, n + 1))
                v.tensor_tensor(pl[:, n % NH_, :], ring[:, n % NR_, :], ph[:, n % NH_, :],
                                ALU.subtract).then_inc(pl_done, 1)

            def weigh(b, e):
                n = ORDER.index(e)
                dve.wait_ge(silu_done, upto(b, EA, n + 1))
                dve.wait_ge(work_full, filled(b, ("c", e)))
                v.tensor_tensor(sg[:, n % 2, :], sg[:, n % 2, :], bank(b, ("c", e))[:, :],
                                ALU.mult).then_inc(sgc_done, 1)

            def hidden(b, e):
                n = ORDER.index(e)
                dve.wait_ge(silu_done, upto(b, EA, n + 1))
                if e < E:
                    dve.wait_ge(sgc_done, upto(b, E, ROUTED.index(e) + 1))
                dve.wait_ge(work_full, filled(b, ("u", e)))
                dve.wait_ge(h_lo, upto(b, EA, n - 1))
                dve.wait_ge(h_hi, upto(b, EA, n - 1))
                ins = v.scalar_tensor_tensor(out=hf[:, n % 2, :], in0=bank(b, ("u", e))[:, :],
                                             scalar=(up_routed if e < E else up_shared)[:, 0:1],
                                             in1=sg[:, n % 2, :], op0=ALU.mult, op1=ALU.mult)
                ins.then_inc(hf_done, 1)

            def head_norms(b, t):
                dve.wait_ge(work_full, filled(b, ("N", t)))
                ins = v.tensor_copy(an_a[:, :, 2 * t:2 * t + 2],
                                    bank(b, ("N", t))[:, 0:2 * NB].rearrange("p (k h) -> p k h", h=2))
                ins.then_inc(n_done, 1)

            def head_scales_begin(b):
                link = Chain(an_step, b, HEAD_STEPS)
                dve.wait_ge(n_done, upto(b, NP_, NP_))
                link(v.tensor_scalar(an_a[:, :, :], an_a[:, :, :], EPS_L2 ** 2, None, ALU.max))
                rsqrt(link, an_a[:, :, :], an_y[:, :, :], an_t[:, :, :])
                link(v.tensor_tensor(an_t[:, :, :], an_a[:, :, :], an_y[:, :, :], ALU.mult))
                return link

            def head_scales_end(b, link):
                dve.wait_ge(th_done, upto(b, 1, 1))
                link(v.scalar_tensor_tensor(out=an_a[:, :, :], in0=th[:, :, :], scalar=C_SCALE, in1=an_y[:, :, :],
                                            op0=ALU.mult, op1=ALU.mult))
                link(v.tensor_copy(wst[:, :, 0:H], an_a[:, :, :]))
                link(v.tensor_tensor(wst[:, :, H:2 * H], an_a[:, :, :], wst[:, :, 0:H], ALU.subtract))
                link.end()

            def gated(b, t):
                dve.wait_ge(work_full, filled(b, ("WB", t)))
                dve.wait_ge(gate_done, upto(b, NP_, t + 1))
                ins = v.tensor_tensor(gate_sb[:, t % 3, :], gate_sb[:, t % 3, :], bank(b, ("WB", t))[:, :], ALU.mult)
                ins.then_inc(gw_done, 1)

            def gated2(b, t):
                dve.wait_ge(gw_done, upto(b, NP_, t + 1))
                dve.wait_ge(agg_done, upto(b, NP_, t + 1))
                v.scalar_tensor_tensor(out=agg[:, t, :], in0=agg[:, t, :], scalar=attn_scale[:, 0:1],
                                       in1=gate_sb[:, t % 3, :], op0=ALU.mult, op1=ALU.mult).then_inc(a_done, 1)

            def finish(b):
                dve.wait_ge(out_mm, upto(b, NP_, NP_))
                dve.wait_ge(res_loaded, upto(b, 16, 16))
                for m in range(KD):
                    v.scalar_tensor_tensor(out=y_sb[:, m, :], in0=acc[m][:, :], scalar=out_scale[:, 0:1],
                                           in1=y_sb[:, m, :], op0=ALU.mult, op1=ALU.add).then_inc(y_done, 1)

            def expert_item(b, kind, e):
                if kind == "g" and e < E:
                    weigh(b, e)
                if kind == "u":
                    hidden(b, e)
                if kind == "N":
                    head_norms(b, e)

            for _ in layernorm(0):
                pass
            tokens_lo(0)
            for _ in route(0):
                pass
            sums(0, 0)
            sums(0, 1)

            def body(b, last):
                for n in range(2, NB):
                    sums(b, n)
                link_qk = norms_begin(b, "qk")
                sums(b, 4)
                norms_round(link_qk, "qk")
                sums(b, 5)
                norms_round(link_qk, "qk")
                norms_round(link_qk, "qk")
                link_qk.end()
                for k in range(NB):
                    unit_qk(b, k)
                    sums(b, 6 + k)
                sums(b, 10)
                turned(b, 0)
                sums(b, 11)
                for n in range(1, 4):
                    turned(b, n)
                link_v = norms_begin(b, "v")
                for kind, e in HEAD[:2]:
                    expert_item(b, kind, e)
                for n in range(4, 8):
                    turned(b, n)
                for _ in range(3):
                    norms_round(link_v, "v")
                link_v.end()
                for n in range(8, 12):
                    turned(b, n)
                    if n < 10:
                        unit_v(b, n - 8)
                for kind, e in HEAD[2:]:
                    expert_item(b, kind, e)
                for n in range(12, 16):
                    turned(b, n)
                unit_v(b, 2)
                unit_v(b, 3)
                next_norm = layernorm(b + 1)
                next_route = route(b + 1)
                for s in range(STEPS):
                    for n in (2 * s, 2 * s + 1):
                        probs(b, n)
                    for n in (2 * s, 2 * s + 1):
                        probs_lo(b, n)
                    for kind, e in PLAN[s]:
                        expert_item(b, kind, e)
                    if s < 2:
                        unit_v(b, NB + 2 * s)
                        unit_v(b, NB + 2 * s + 1)
                    if not last:
                        for _ in range(2 if s in NORM_STEPS else 0):
                            next(next_norm, None)
                        for _ in range(2 if s >= ROUTE_FROM else 0):
                            next(next_route, None)
                for kind, n in TAIL:
                    expert_item(b, kind, n)
                    if (kind, n) == ("N", NP_ - 1):
                        link_heads = head_scales_begin(b)
                    if kind == "TH":
                        head_scales_end(b, link_heads)
                for t in range(NP_):
                    gated(b, t)
                    gated2(b, t)
                    if t == NP_ - 2 and not last:
                        tokens_lo(b + 1)
                    if t == NP_ - 1 and not last:
                        sums(b + 1, 0)
                        sums(b + 1, 1)
                finish(b)

            rounds(dve, body)

        @block.scalar
        def _(act):
            a = nc.scalar.activation

            def turn_tokens(b, k):
                act.wait_ge(work_full, filled(b, ("X", k)))
                act.wait_ge(work_full, filled(b - 1, ("R", 0)))
                act.wait_ge(xh_done, upto(b, 1, 0))
                act.wait_ge(xl_done, upto(b, 1, 0))
                ins = a(xf[:, :, k * P:(k + 1) * P],
                        bank(b, ("X", k))[:, 0:KD * P].rearrange("p (m t) -> p m t", m=KD), ACT.Copy)
                ins.then_inc(xf_done, 1)

            def tokens_hi(b):
                act.wait_ge(xf_done, upto(b, NB, NB))
                act.wait_ge(work_full, filled(b - 1, ("G", NP_ - 1)))
                a(xh[:, :, :], xf[:, :, :], ACT.Copy).then_inc(xh_done, 1)

            def router_scores(b):
                act.wait_ge(work_full, filled(b, ("R", 0)))
                act.wait_ge(route_step, upto(b, ROUTE_STEPS, 0))
                a(sc_s[:, :, :], bank(b, ("R", 0))[:, 0:NB * E].rearrange("p (k e) -> p k e", e=E),
                  ACT.Sigmoid).then_inc(score_done, 1)

            def raw(b, n):
                key = ("QK", n) if n < NB else ("V", n - NB)
                act.wait_ge(work_full, filled(b, key))
                if n < 2:
                    act.wait_ge(work_full, filled(b - 1, ("N", NP_ - 1)))
                act.wait_ge(norm_done, upto(b, 3 * NB, n - 1))
                a(sq[:, n % 2, :], bank(b, key)[:, :], ACT.Square).then_inc(rawsq_done, 1)
                if n < NB:
                    act.wait_ge(pl_done, upto(b, 2 * STEPS, 0))
                    dst = qk_raw[:, n, :]
                else:
                    k, half = (n - NB) // 2, (n - NB) % 2
                    act.wait_ge(a_hi, upto(b - 1, NP_, n - NB + 1))
                    act.wait_ge(a_lo, upto(b - 1, NP_, n - NB + 1))
                    dst = v_raw[:, k, half * T:half * T + T]
                a(dst, bank(b, key)[:, :], ACT.Copy).then_inc(raw_done, 1)

            for k in range(NB):
                turn_tokens(0, k)
            tokens_hi(0)
            router_scores(0)
            raw(0, 0)
            raw(0, 1)

            def split_hi_qk(b, k):
                act.wait_ge(qkn_done, upto(b, NB, k + 1))
                if k >= 2:
                    act.wait_ge(work_full, filled(b, ("T", 4 * k - 5)))
                else:
                    act.wait_ge(work_full, filled(b - 1, ("T", 4 * k + 11)))
                blk = qk_raw[:, k, :]
                for c, dst, dims in ((0, qst, 0), (1, kst, 1)):
                    src = blk[:, c * H * DK:(c + 1) * H * DK].rearrange("p (h d) -> p h d", d=DK)
                    src = src.unsqueeze(2).to_broadcast([P, H, 2, DK])
                    to = dst[:, k % 2, :].rearrange("p (h a c d) -> p h a c d", a=2, c=2, d=DK)
                    to = to[:, :, 0, :, :] if c == 0 else to[:, :, :, 0, :]
                    a(to, src, ACT.Copy).then_inc(qk_hi, 1)

            def split_hi_v(b, n):
                k, half = n // 2, n % 2
                act.wait_ge(vn_done, upto(b, 2 * NB, n + 1))
                act.wait_ge(av_step, upto(b, STEPS, 0))
                a(vh[:, k, half * T:half * T + T], v_raw[:, k, half * T:half * T + T], ACT.Copy).then_inc(v_hi, 1)

            def relu(b, n):
                act.wait_ge(sim_full, upto(b, 2 * STEPS, n + 1))
                act.wait_ge(pl_done, upto(b, 2 * STEPS, n - NR_ + 1))
                if n < NR_:
                    act.wait_ge(qk_lo, upto(b, 2 * NB, 2 * NB))
                a(ring[:, n % NR_, :], sim[n % 2][:, :], ACT.Relu, scale=S_SCALE).then_inc(relu_done, 1)

            def square(b, n):
                act.wait_ge(relu_done, upto(b, 2 * STEPS, n + 1))
                a(ring[:, n % NR_, :], ring[:, n % NR_, :], ACT.Square).then_inc(square_done, 1)

            def silu(b, e):
                n = ORDER.index(e)
                act.wait_ge(work_full, filled(b, ("g", e)))
                act.wait_ge(hf_done, upto(b, EA, n - 1))
                ins = a(sg[:, n % 2, :], bank(b, ("g", e))[:, :], ACT.Silu, scale=inv_m[:, 0:1])
                ins.then_inc(silu_done, 1)

            def hidden_hi(b, n):
                act.wait_ge(hf_done, upto(b, EA, n + 1))
                act.wait_ge(down_done, upto(b, EA, n - 1))
                a(hh[:, n % 2, :], hf[:, n % 2, :], ACT.Copy).then_inc(h_hi, 1)

            def square_heads(b, t, src=None):
                if t >= 2:
                    act.wait_ge(work_full, filled(b, ("N", t - 2)))
                else:
                    act.wait_ge(norm_done, upto(b, 3 * NB, 3 * NB))
                if src is None:
                    act.wait_ge(agg_done, upto(b, NP_, t + 1))
                    a(sq[:, t % 2, :], agg[:, t, :], ACT.Square, scale=AG_UNSCALE).then_inc(agg_sq_done, 1)
                else:
                    act.wait_ge(av_step, upto(b, STEPS, NB * (t + 1)))
                    a(sq[:, t % 2, :], src, ACT.Square, scale=AG_UNSCALE).then_inc(agg_sq_done, 1)

            def take_heads(b, t):
                act.wait_ge(av_step, upto(b, STEPS, NB * (t + 1)))
                act.wait_ge(v_lo, upto(b, 2 * NB, 2 * NB))
                act.wait_ge(v_hi, upto(b, 2 * NB, 2 * NB))
                a(agg[:, t, :], av[:, :], ACT.Copy).then_inc(agg_done, 1)

            def gate(b, t):
                act.wait_ge(work_full, filled(b, ("G", t)))
                act.wait_ge(a_done, upto(b, NP_, t - 2))
                ins = a(gate_sb[:, t % 3, :], bank(b, ("G", t))[:, :], ACT.Silu, scale=inv_a[:, 0:1])
                ins.then_inc(gsilu_done, 1)
                act.wait_ge(gsilu_done, upto(b, NP_, t + 1))
                a(gate_sb[:, t % 3, :], gate_sb[:, t % 3, :], ACT.Tanh).then_inc(gate_done, 1)

            def attention_hi(b, t):
                act.wait_ge(a_done, upto(b, NP_, t + 1))
                act.wait_ge(out_mm, upto(b, NP_, t - 1))
                a(ah[:, t % 2, :], agg[:, t, :], ACT.Copy).then_inc(a_hi, 1)

            def expert_item(b, kind, e):
                if kind == "g":
                    silu(b, e)
                if kind == "u" and ORDER.index(e) >= 1:
                    hidden_hi(b, ORDER.index(e) - 1)

            def whole(b, last):
                raw(b, 2)
                raw(b, 3)
                act.wait_ge(work_full, filled(b, ("CT", 0)))
                act.wait_ge(work_full, filled(b - 1, ("c", ROUTED[-1])))
                a(ct[:, :], bank16(b, ("CT", 0))[0:2 * E, 0:T], ACT.Copy).then_inc(ct_done, 1)
                for n in range(4, 8):
                    raw(b, n)
                split_hi_qk(b, 0)
                raw(b, 8)
                split_hi_qk(b, 1)
                for n in range(9, 3 * NB):
                    raw(b, n)
                expert_item(b, *HEAD[0])
                split_hi_qk(b, 2)
                expert_item(b, *HEAD[1])
                split_hi_qk(b, 3)
                expert_item(b, *HEAD[2])
                expert_item(b, *HEAD[3])
                split_hi_v(b, 0)
                split_hi_v(b, 1)
                for s in range(STEPS):
                    if s % NB == 1 and s > NB:
                        take_heads(b, s // NB - 1)
                    for n in (2 * s, 2 * s + 1):
                        relu(b, n)
                    for n in (2 * s, 2 * s + 1):
                        square(b, n)
                    for kind, e in PLAN[s]:
                        if kind == "X" and not last:
                            turn_tokens(b + 1, e)
                        elif kind == "R" and not last:
                            router_scores(b + 1)
                        else:
                            expert_item(b, kind, e)
                    if s < 3:
                        split_hi_v(b, 2 + 2 * s)
                        split_hi_v(b, 3 + 2 * s)
                    if s % NB == 1 and s > NB:
                        square_heads(b, s // NB - 1)
                for kind, n in TAIL:
                    if kind == "G":
                        gate(b, n)
                    elif kind == "AV":
                        square_heads(b, NP_ - 1, av[:, :])
                        take_heads(b, NP_ - 1)
                    elif kind == "TH":
                        act.wait_ge(an_step, upto(b, HEAD_STEPS, HEAD_STEPS - 3))
                        a(th[:, :, :], an_t[:, :, :], ACT.Tanh).then_inc(th_done, 1)
                    elif kind == "WT":
                        act.wait_ge(work_full, filled(b, ("WT", 0)))
                        act.wait_ge(work_full, filled(b - 1, ("WB", NP_ - 1)))
                        a(wt[:, :], bank16(b, ("WT", 0))[0:2 * H, 0:T], ACT.Copy).then_inc(wt_done, 1)
                    elif (kind, n) == ("d", ORDER[-2]):
                        hidden_hi(b, EA - 1)
                    else:
                        expert_item(b, kind, n)
                attention_hi(b, 0)
                for t in range(NP_):
                    if t + 1 < NP_:
                        attention_hi(b, t + 1)
                    if t + 3 < NP_:
                        gate(b, t + 3)
                    if t == NP_ - 4 and not last:
                        tokens_hi(b + 1)
                    if t > NP_ - 3 and not last:
                        raw(b + 1, t - (NP_ - 2))

            rounds(act, whole)

        @block.gpsimd
        def _(pool):
            tt = nc.gpsimd.tensor_tensor

            def split_lo_qk(b, k):
                for c, dst in ((0, qst), (1, kst)):
                    pool.wait_ge(qk_hi, upto(b, 2 * NB, 2 * k + c + 1))
                    src = qk_raw[:, k, c * H * DK:(c + 1) * H * DK].rearrange("p (h d) -> p h d", d=DK)
                    src = src.unsqueeze(2).to_broadcast([P, H, 2, DK])
                    to = dst[:, k % 2, :].rearrange("p (h a c d) -> p h a c d", a=2, c=2, d=DK)
                    hi, lo = ((to[:, :, 0, :, :], to[:, :, 1, :, :]) if c == 0
                              else (to[:, :, :, 0, :], to[:, :, :, 1, :]))
                    tt(lo, src, hi, ALU.subtract).then_inc(qk_lo, 1)

            def split_lo_v(b, n):
                k, half = n // 2, n % 2
                pool.wait_ge(v_hi, upto(b, 2 * NB, n + 1))
                pool.wait_ge(av_step, upto(b, STEPS, 0))
                sl = slice(half * T, half * T + T)
                tt(vl[:, k, sl], v_raw[:, k, sl], vh[:, k, sl], ALU.subtract).then_inc(v_lo, 1)

            def body(b, last):
                def hidden_lo(n):
                    pool.wait_ge(h_hi, upto(b, EA, n + 1))
                    pool.wait_ge(down_done, upto(b, EA, n - 1))
                    tt(hl[:, n % 2, :], hf[:, n % 2, :], hh[:, n % 2, :], ALU.subtract).then_inc(h_lo, 1)

                for k in range(NB):
                    split_lo_qk(b, k)
                hidden_lo(0)
                for n in range(2):
                    split_lo_v(b, n)
                for s in range(STEPS):
                    for kind, e in PLAN[s]:
                        if kind == "u":
                            hidden_lo(ORDER.index(e) - 1)
                    if s < 3:
                        split_lo_v(b, 2 + 2 * s)
                        split_lo_v(b, 3 + 2 * s)
                for kind, e in TAIL:
                    if kind == "u":
                        hidden_lo(ORDER.index(e) - 1)
                hidden_lo(EA - 1)
                for t in range(NP_):
                    pool.wait_ge(a_hi, upto(b, NP_, t + 1))
                    pool.wait_ge(out_mm, upto(b, NP_, t - 1))
                    tt(al[:, t % 2, :], agg[:, t, :], ah[:, t % 2, :], ALU.subtract).then_inc(a_lo, 1)

            rounds(pool, body)

        @block.tensor
        def _(pe):
            mm, turn = nc.tensor.matmul, nc.tensor.transpose

            def products(dst, w_parts, x_parts, first=True, last=True):
                (w_h, w_l), (x_h, x_l) = w_parts, x_parts
                terms = [(w, x_h) for w in (w_h, w_l)] + [(w_h, x_l)]
                n = len(terms) * len(w_h)
                i = 0
                for w, xx in terms:
                    for k in range(len(w_h)):
                        ins = mm(dst, w[k], xx[k], start=first and i == 0, stop=last and i == n - 1)
                        i += 1
                return ins

            def turn_tokens(b, k):
                pe.wait_ge(xn_done, upto(b, NB, k + 1))
                pe.wait_ge(*bank_read(b, ("X", k)))
                for m in range(KD):
                    ins = turn(bank(b, ("X", k))[:, m * P:(m + 1) * P], x_sb[:, k, m * P:(m + 1) * P], id32[:, :])
                ins.then_inc(work_full, 1)

            def router(b):
                pe.wait_ge(xf_done, upto(b, NB, NB))
                pe.wait_ge(*bank_read(b, ("R", 0)))
                for k in range(NB):
                    for m in range(KD):
                        ins = mm(bank(b, ("R", 0))[:, k * E:(k + 1) * E], xf[:, m, k * P:(k + 1) * P], wr[:, m, :],
                                 start=(m == 0), stop=(m == KD - 1))
                ins.then_inc(work_full, 1)

            def project(b, key, k, lo, width):
                pe.wait_ge(xh_done, upto(b, 1, 1))
                pe.wait_ge(xl_done, upto(b, 1, 1))
                pe.wait_ge(*bank_read(b, key))
                blk, cols = slice(k * P, (k + 1) * P), slice(lo, lo + width)
                ins = products(bank(b, key)[:, 0:width], ([xh[:, m, blk] for m in range(KD)],
                                                       [xl[:, m, blk] for m in range(KD)]),
                               ([wa_h[:, m, cols] for m in range(KD)], [wa_l[:, m, cols] for m in range(KD)]))
                ins.then_inc(work_full, 1)

            def turn_qk(b, n):
                k, c = n // 4, n % 4
                pe.wait_ge(qk_lo, upto(b, 2 * NB, 2 * k + (1 if c < 2 else 2)))
                pe.wait_ge(*bank_read(b, ("T", n)))
                src = (qst if c < 2 else kst)[:, k % 2, (c % 2) * T:(c % 2) * T + T]
                for m in range(4):
                    ins = turn(bank16(b, ("T", n))[:, m * P:(m + 1) * P], src[:, m * P:(m + 1) * P], id16[:, :])
                ins.then_inc(work_full, 1)

            def turn_small(b, key, src):
                pe.wait_ge(*bank_read(b, key))
                for k in range(NB):
                    ins = turn(bank16(b, key)[0:2 * E, k * P:(k + 1) * P], src[:, k, :], id16[:, :])
                ins.then_inc(work_full, 1)

            def scores(b, s):
                pair, j = s // NB, s % NB
                if s == 0:
                    pe.wait_ge(qk_turned, upto(b, 4 * NB, 4 * NB))
                for half in range(2):
                    n = 2 * s + half
                    pe.wait_ge(relu_done, upto(b, 2 * STEPS, n - 1))
                    rows = slice(64 * half, 64 * half + 64)
                    mm(sim[half][:, :], kt[rows, pair, j * P:(j + 1) * P], qt[rows, pair, :], start=True,
                       stop=True).then_inc(sim_full, 1)

            def values(b, s):
                pair, j = s // NB, s % NB
                pe.wait_ge(pl_done, upto(b, 2 * STEPS, 2 * s + 2))
                if pair == 0:
                    pe.wait_ge(v_lo, upto(b, 2 * NB, 2 * (j + 1)))
                if j == 0:
                    pe.wait_ge(agg_done, upto(b, NP_, pair))
                for i, (vv, pp) in enumerate(((vh, ph), (vl, ph), (vh, pl))):
                    for half in range(2):
                        h = 2 * pair + half
                        ins = mm(av[64 * half:64 * half + 64, :], vv[:, j, h * DV:(h + 1) * DV],
                                 pp[:, (2 * s + half) % NH_, :], start=(j == 0 and i == 0),
                                 stop=(j == NB - 1 and i == 2))
                ins.then_inc(av_step, 1)

            def head_sums(b, t):
                pe.wait_ge(agg_sq_done, upto(b, NP_, t + 1))
                pe.wait_ge(*bank_read(b, ("N", t)))
                for k in range(NB):
                    ins = mm(bank(b, ("N", t))[:, 2 * k:2 * k + 2], sq[:, t % 2, k * P:(k + 1) * P], pair_sel[:, :],
                             start=True, stop=True)
                ins.then_inc(work_full, 1)

            def item(b, kind, e):
                n = ORDER.index(e)
                cols = slice(e * P, (e + 1) * P)
                if kind == "c":
                    pe.wait_ge(ct_done, upto(b, 1, 1))
                    pe.wait_ge(*bank_read(b, (kind, e)))
                    for half in range(2):
                        ins = mm(bank(b, (kind, e))[64 * half:64 * half + 64, :], sel16[:, e * DV:(e + 1) * DV], ct[:, :],
                                 start=True, stop=True)
                    ins.then_inc(work_full, 1)
                elif kind in "gu":
                    pe.wait_ge(*bank_read(b, (kind, e)))
                    wh, wl = (gate_h, gate_l) if kind == "g" else (up_h, up_l)
                    ins = products(bank(b, (kind, e))[:, :], ([wh[:, m, cols] for m in range(KD)],
                                                           [wl[:, m, cols] for m in range(KD)]),
                                   ([xh[:, m, :] for m in range(KD)], [xl[:, m, :] for m in range(KD)]))
                    ins.then_inc(work_full, 1)
                else:
                    pe.wait_ge(h_hi, upto(b, EA, n + 1))
                    pe.wait_ge(h_lo, upto(b, EA, n + 1))
                    if n == 0:
                        pe.wait_ge(y_done, upto(b, KD, 0))
                    for m in range(KD):
                        mc = slice(m * P, (m + 1) * P)
                        ins = products(acc[m][:, :], ([down_h[:, e, mc]], [down_l[:, e, mc]]),
                                       ([hh[:, n % 2, :]], [hl[:, n % 2, :]]), first=(n == 0), last=False)
                    ins.then_inc(down_done, 1)

            def gates(b, t):
                pe.wait_ge(*bank_read(b, ("G", t)))
                cols = slice(G_AT + t * P, G_AT + (t + 1) * P)
                products(bank(b, ("G", t))[:, :], ([wa_h[:, m, cols] for m in range(KD)],
                                                [wa_l[:, m, cols] for m in range(KD)]),
                         ([xh[:, m, :] for m in range(KD)], [xl[:, m, :] for m in range(KD)])).then_inc(work_full, 1)

            def spread(b, t):
                pe.wait_ge(wt_done, upto(b, 1, 1))
                pe.wait_ge(*bank_read(b, ("WB", t)))
                mm(bank(b, ("WB", t))[:, :], sel16[:, t * P:(t + 1) * P], wt[:, :], start=True,
                   stop=True).then_inc(work_full, 1)

            def output(b, t):
                pe.wait_ge(a_lo, upto(b, NP_, t + 1))
                for m in range(KD):
                    mc = slice(m * P, (m + 1) * P)
                    ins = products(acc[m][:, :], ([wo_h[:, t, mc]], [wo_l[:, t, mc]]),
                                   ([ah[:, t % 2, :]], [al[:, t % 2, :]]), first=False, last=(t == NP_ - 1))
                ins.then_inc(out_mm, 1)

            def ahead(b, kind, n):
                if kind == "X":
                    turn_tokens(b, n)
                elif kind == "R":
                    router(b)
                elif kind == "QK":
                    project(b, (kind, n), n, 0, QK_W)
                else:
                    pe.wait_ge(route_step, upto(b, ROUTE_STEPS, ROUTE_STEPS))
                    turn_small(b, ("CT", 0), cst)

            for kind, n in FIRST:
                ahead(0, kind, n)

            def body(b, last):
                for kind, n in pe_order():
                    if kind == "V":
                        project(b, (kind, n), n // 2, V_AT + (n % 2) * T, T)
                    elif kind == "T":
                        turn_qk(b, n)
                    elif kind == "S":
                        scores(b, n)
                    elif kind == "AV":
                        values(b, n)
                    elif kind == "N":
                        head_sums(b, n)
                    elif kind in "cgud":
                        item(b, kind, n)
                    elif kind == "G":
                        gates(b, n)
                    elif kind == "WT":
                        pe.wait_ge(an_step, upto(b, HEAD_STEPS, HEAD_STEPS))
                        turn_small(b, ("WT", 0), wst)
                    elif kind == "WB":
                        spread(b, n)
                    elif kind == "O":
                        output(b, n)
                    elif kind in AHEAD and not last:
                        ahead(b + 1, kind, n)

            rounds(pe, body)


def split_weights(nc, x, wa, w_gate, w_up, w_down, w_out, w_router, bias, ident, ident_h, sel, tri, parts,
                  wr, bias_sb, id32, id16, sel16, pair_sel, tri_sb, eps_qkv, inv_a, inv_m, up_routed, up_shared,
                  attn_scale, out_scale):
    with ExitStack() as ctx:
        def sb(name, shape, dt=F32):
            return ctx.enter_context(nc.sbuf_tensor(name, shape, dt))

        def sem(name):
            return ctx.enter_context(nc.semaphore(name))

        raw = {"wa": sb("raw_wa", [P, KD * WA_W]), "gate": sb("raw_gate", [P, KD * EA * P]),
               "up": sb("raw_up", [P, KD * EA * P]), "down": sb("raw_down", [P, EA * D]),
               "wo": sb("raw_wo", [P, NP_ * D])}
        source = {"wa": wa.rearrange("(m p) n -> p m n", p=P), "gate": w_gate.rearrange("(m p) n -> p m n", p=P),
                  "up": w_up.rearrange("(m p) n -> p m n", p=P), "down": w_down, "wo": w_out}
        split = {"wa": KD, "gate": KD, "up": KD, "down": EA, "wo": NP_}
        groups = [("wa",), ("gate", "up"), ("down", "wo")]
        floor = [2.0 ** -40, 2.0 ** -6, 2.0 ** -20]
        flat = {k: tuple(t[:, :, :].rearrange("p a n -> p (a n)") for t in v) for k, v in parts.items()}
        order = [k for g in groups for k in g]
        big = sb("big", [P, len(order)])
        top, every = sb("top", [P, 3]), sb("every", [P, 3])
        power, scale = sb("power", [P, 3]), sb("scale", [P, 3])
        sh = sb("sh", [P, 2])
        loaded = {k: sem(f"loaded_{k}") for k in order}
        small_loaded, big_done, top_done = sem("small_loaded"), sem("big_done"), sem("top_done")
        every_done, scale_step, hi_done, lo_done = (sem("every_done"), sem("scale_step"), sem("hi_done"),
                                                    sem("lo_done"))
        set_done = sem("set_done")
        SCALE_STEPS = 4
        CUT = 2560
        cuts = {k: [(a, min(a + CUT, raw[k].shape[1])) for a in range(0, raw[k].shape[1], CUT)] for k in order}
        pieces = [(k, a, z) for k in order for a, z in cuts[k]]

        block = ctx.enter_context(nc.Block())

        @block.sync
        def _(sp):
            for k in order:
                sp.dma_start(raw[k][:, :].rearrange("p (a n) -> p a n", a=split[k]), source[k]).then_inc(loaded[k], 16)
            sp.wait_ge(small_loaded, 16 * 6)

        @block.scalar
        def _(act):
            act.dma_start(wr[:, :, :], w_router.rearrange("(m p) e -> p m e", p=P)).then_inc(small_loaded, 16)
            act.dma_start(bias_sb[:, :], bias).then_inc(small_loaded, 16)
            act.dma_start(id32[:, :], ident).then_inc(small_loaded, 16)
            act.dma_start(id16[:, :], ident_h).then_inc(small_loaded, 16)
            act.dma_start(sel16[:, :], sel).then_inc(small_loaded, 16)
            act.dma_start(tri_sb[:, :], tri).then_inc(small_loaded, 16)
            for k, a, z in pieces:
                g = next(i for i, names in enumerate(groups) if k in names)
                act.wait_ge(scale_step, SCALE_STEPS * (g + 1))
                nc.scalar.activation(flat[k][0][:, a:z], raw[k][:, a:z], ACT.Copy,
                                     scale=scale[:, g:g + 1]).then_inc(hi_done, 1)

        @block.gpsimd
        def _(pool):
            for half in range(2):
                rows = slice(64 * half, 64 * half + 64)
                pool.memset(pair_sel[rows, half:half + 1], 1.0).then_inc(set_done, 1)
                pool.memset(pair_sel[rows, 1 - half:2 - half], 0.0).then_inc(set_done, 1)
            pool.wait_ge(set_done, 4)
            for g in range(3):
                pool.wait_ge(top_done, g + 1)
                pool.partition_all_reduce(every[:, g:g + 1], top[:, g:g + 1], P,
                                          bass.bass_isa.ReduceOp.max).then_inc(every_done, 1)

        @block.vector
        def _(dve):
            v = nc.vector
            steps = [0]

            def link(ins):
                steps[0] += 1
                ins.then_inc(scale_step, 1)
                dve.wait_ge(scale_step, steps[0])

            def largest(g):
                for k in groups[g]:
                    n = order.index(k)
                    dve.wait_ge(loaded[k], 16)
                    v.tensor_reduce(big[:, n:n + 1], raw[k][:, :], AX.X, ALU.max,
                                    apply_absolute_value=True).then_inc(big_done, 1)
                ns = [order.index(k) for k in groups[g]]
                dve.wait_ge(big_done, ns[-1] + 1)
                v.tensor_reduce(top[:, g:g + 1], big[:, ns[0]:ns[-1] + 1], AX.X, ALU.max).then_inc(top_done, 1)

            def scales(g):
                dve.wait_ge(every_done, g + 1)
                c = slice(g, g + 1)
                link(v.tensor_scalar(power[:, c], every[:, c], floor[g], None, ALU.max))
                link(v.tensor_scalar(power[:, c].bitcast(I32), power[:, c].bitcast(I32), 0x7F800000, None,
                                     ALU.bitwise_and))
                link(v.reciprocal(scale[:, c], power[:, c]))
                link(v.tensor_scalar(scale[:, c], scale[:, c], 2.0 ** W_EXP, None, ALU.mult))

            def low_parts(g):
                for n, (k, a, z) in enumerate(pieces):
                    if k in groups[g]:
                        dve.wait_ge(hi_done, n + 1)
                        v.scalar_tensor_tensor(out=flat[k][1][:, a:z], in0=raw[k][:, a:z], scalar=scale[:, g:g + 1],
                                               in1=flat[k][0][:, a:z], op0=ALU.mult,
                                               op1=ALU.subtract).then_inc(lo_done, 1)

            for g in range(3):
                largest(g)
                scales(g)
                low_parts(g)
            back = 2.0 ** -W_EXP
            mult = ALU.mult
            link(v.tensor_scalar(eps_qkv[:, :], scale[:, 0:1], scale[:, 0:1], EPS_L2 ** 2, mult, mult))
            link(v.tensor_scalar(inv_a[:, :], power[:, 0:1], back, None, mult))
            link(v.tensor_scalar(inv_m[:, :], power[:, 1:2], back, None, mult))
            link(v.reciprocal(sh[:, 0:1], power[:, 1:2]))
            link(v.tensor_scalar(up_shared[:, :], sh[:, 0:1], 2.0 ** (-5 - W_EXP), None, mult))
            link(v.tensor_scalar(up_routed[:, :], up_shared[:, :], 1.0 / C_SCALE, None, mult))
            link(v.tensor_scalar(sh[:, 1:2], sh[:, 0:1], sh[:, 0:1], 2.0 ** -5, mult, mult))
            link(v.tensor_scalar(attn_scale[:, :], sh[:, 1:2], AG_UNSCALE / C_SCALE, None, mult))
            link(v.reciprocal(sh[:, 0:1], sh[:, 1:2]))
            link(v.tensor_scalar(out_scale[:, :], power[:, 2:3], sh[:, 0:1], back, mult, mult))


_OUT = (B, D, T)


def kernel(L0_attn_tokens, L0_attn_Wqg, L0_attn_Wkv, L0_attn_Wout, L0_ffn_router_weight, L0_ffn_e_bias,
           L0_ffn_gate_w, L0_ffn_up_w, L0_ffn_down_w, L0_ffn_sh_gate_w, L0_ffn_sh_up_w, L0_ffn_sh_down_w):
    import numpy as np
    import concourse.bacc as bacc
    from concourse.bass_utils import run_bass_kernel_spmd

    asc = np.ascontiguousarray
    tokens = np.asarray(L0_attn_tokens)
    wqg = np.asarray(L0_attn_Wqg).reshape(D, H, DK + DV)
    wkv = np.asarray(L0_attn_Wkv).reshape(D, H, DK + DV)
    wa = np.concatenate([wqg[:, :, :DK].reshape(D, -1), wkv[:, :, :DK].reshape(D, -1),
                         wkv[:, :, DK:].reshape(D, -1), wqg[:, :, DK:].reshape(D, -1)], axis=1)

    def rows(routed, shared):
        return asc(np.concatenate([np.asarray(routed).reshape(E * P, D), np.asarray(shared)], axis=0).T)

    down = np.concatenate([np.asarray(L0_ffn_down_w).transpose(2, 0, 1),
                           np.asarray(L0_ffn_sh_down_w).reshape(D, ES, P).transpose(2, 1, 0)], axis=1)
    sel = np.zeros((2, H, H, DV), np.float16)
    for h in range(H):
        sel[:, h, h, :] = 1.0
    tri = np.tril(np.ones((NG, NG), np.float32), -1).reshape(1, -1)
    arrays = {
        "x": tokens,
        "x_t": asc(tokens.transpose(0, 2, 1)),
        "wa": asc(wa),
        "w_gate": rows(L0_ffn_gate_w, L0_ffn_sh_gate_w),
        "w_up": rows(L0_ffn_up_w, L0_ffn_sh_up_w),
        "w_down": asc(down),
        "w_out": asc(np.asarray(L0_attn_Wout).reshape(NP_, P, D).transpose(1, 0, 2)),
        "w_router": asc(np.asarray(L0_ffn_router_weight).T),
        "bias": asc(np.broadcast_to(np.asarray(L0_ffn_e_bias), (P, E))),
        "ident": np.eye(P, dtype=np.float32),
        "ident_h": np.eye(P, dtype=np.float16),
        "sel": sel.reshape(2 * H, H * DV),
        "tri": asc(np.broadcast_to(tri, (P, NG * NG))),
    }
    nc = bacc.Bacc("TRN2", target_bir_lowering=False, num_devices=1)
    args = [nc.dram_tensor(n, a.shape, mybir.dt.from_np(a.dtype), kind="ExternalInput").ap() for n, a in arrays.items()]
    out = nc.dram_tensor("out_t", _OUT, F32, kind="ExternalOutput").ap()
    build_layer(nc, *args, out)
    r = run_bass_kernel_spmd(nc, [arrays], core_ids=[0])
    return asc(r.results[0]["out_t"].transpose(0, 2, 1))
```

```python
from contextlib import ExitStack

import concourse.bass as bass
from concourse import mybir

F32 = mybir.dt.float32
F16 = mybir.dt.float16
I32 = mybir.dt.int32
ALU = mybir.AluOpType
ACT = mybir.ActivationFunctionType
AX = mybir.AxisListType

P = 128
B, T, D = 16, 512, 256
H, DK, DV = 16, 16, 64
E, NG, GE = 16, 4, 4
ES = 2
EA = E + ES
NB = T // P
KD = D // P
NP_ = H // 2
QK_W = 2 * H * DK
V_AT = QK_W
G_AT = V_AT + H * DV
WA_W = G_AT + H * DV
RSQRT_MAGIC = 0x5F3759DF

W_EXP = 9
QK_SCALE = 2.0 ** 7
S_SCALE = 2.0 ** -7
P_SCALE = 2.0 ** 14
V_SCALE = 2.0 ** 8
C_SCALE = 2.0 ** 8
AG_UNSCALE = 1.0 / (P_SCALE * V_SCALE)
EPS_L2 = 1e-12
EPS_LN = 1e-5
EPS_TW = 1e-20
ROUTE_SCALE = 2.5

STEPS = NP_ * NB
LAG = 2
ORDER = list(range(E, EA)) + list(range(E))
ROUTED = [e for e in ORDER if e < E]


def expert_items():
    items = []
    for n, e in enumerate(ORDER):
        if e < E:
            items.append(("c", e))
        items += [("g", e), ("u", e)]
        if n == 1:
            items.append(("d", ORDER[0]))
        if n >= 3:
            items.append(("d", ORDER[n - 2]))
    return items + [("d", ORDER[-2]), ("d", ORDER[-1])]


G_AFTER = 6
HEAD_ITEMS = 5
TAIL_ITEMS = 8
ITEMS = expert_items()

NORM_STEPS = range(1, 9)
ROUTE_FROM = 14
NEXT_AT = {9: [("X", 0)], 11: [("X", 1)], 13: [("R", 0), ("R", 1)]}


def plan_steps():
    items = ITEMS[HEAD_ITEMS:len(ITEMS) - TAIL_ITEMS]
    firsts = [e for k, e in items if k == "c"]
    steps = [[] for _ in range(STEPS)]
    downs = [item for item in items if item[0] == "d"]
    due = []
    for n, e in enumerate(firsts):
        at = n * (STEPS - 1) // (len(firsts) - 1)
        steps[at] += [("c", e), ("g", e)]
        if ("u", e) in items:
            steps[at + 1].append(("u", e))
    taken = [bool(step) for step in steps] + [True]
    for s in range(STEPS):
        if s % NB == LAG + 1 and NB < s < STEPS - 1:
            due.append(("N", s // NB - 1))
        due += NEXT_AT.get(s, [])
        opened = any(k == "c" for k, _ in steps[s])
        ups = [ORDER.index(e) for step in steps[:s + 1] for k, e in step if k == "u"]
        if downs and not opened and taken[s + 1] and ORDER.index(downs[0][1]) + 2 <= ups[-1]:
            steps[s].append(downs.pop(0))
        if not opened:
            while due:
                steps[s].append(due.pop(0))
    assert not due
    steps[-1] = downs + steps[-1]
    return steps


HEAD = ITEMS[:HEAD_ITEMS]
PLAN = plan_steps()
LATE = ITEMS[len(ITEMS) - TAIL_ITEMS:]
TAIL = ([("AV", STEPS - 2), ("G", 0), LATE[0], ("N", NP_ - 2), ("AV", STEPS - 1), LATE[1], ("N", NP_ - 1), ("G", 1)]
        + LATE[2:4] + [("TH", 0)] + LATE[4:6] + [("WT", 0), LATE[6], ("G", 2), ("WB", 0), ("WB", 1), LATE[7]])
AHEAD = ("X", "R", "QK", "CT")


def pe_order():
    seq = [("V", n) for n in range(2 * NB)]
    seq[G_AFTER:G_AFTER] = HEAD[:1]
    for k in range(NB):
        seq += [("T", 2 * k), ("T", 2 * k + 1)] + HEAD[k + 1:k + 2]
    for s in range(STEPS):
        seq.append(("S", s))
        seq += PLAN[s]
        if s >= LAG:
            seq.append(("AV", s - LAG))
    seq += TAIL
    for t in range(NP_):
        if t + 3 < NP_:
            seq.append(("G", t + 3))
        if t + 2 < NP_:
            seq.append(("WB", t + 2))
        if t >= NP_ - 2:
            seq.append(("QK", t - (NP_ - 2)))
        seq.append(("O", t))
    return seq + [("QK", 2), ("QK", 3), ("CT", 0)]


def work_order():
    return [key for key in pe_order() if key[0] not in ("S", "AV", "d", "TH", "O")]


ORDERED = work_order()
WORK = {key: n for n, key in enumerate(ORDERED)}
FIRST = [key for key in ORDERED if key[0] in AHEAD]
LAST = [key for key in ORDERED if key[0] not in AHEAD]
NW = 3
PER = len(WORK)
assert PER % NW == 0
RSQRT_STEPS = 11
ROUTE_STEPS = 34
HEAD_STEPS = 1 + RSQRT_STEPS + 4


def build_layer(nc, x, x_t, wa, w_gate, w_up, w_down, w_out, w_router, bias, ident, ident_h, sel, tri, out_t):
    with ExitStack() as ctx:
        def sb(name, shape, dt=F32):
            return ctx.enter_context(nc.sbuf_tensor(name, shape, dt))

        def sem(name):
            return ctx.enter_context(nc.semaphore(name))

        wa_h, wa_l = sb("wa_h", [P, KD, WA_W], F16), sb("wa_l", [P, KD, WA_W], F16)
        gate_h, gate_l = sb("gate_h", [P, KD, EA * P], F16), sb("gate_l", [P, KD, EA * P], F16)
        up_h, up_l = sb("up_h", [P, KD, EA * P], F16), sb("up_l", [P, KD, EA * P], F16)
        down_h, down_l = sb("down_h", [P, EA, D], F16), sb("down_l", [P, EA, D], F16)
        wo_h, wo_l = sb("wo_h", [P, NP_, D], F16), sb("wo_l", [P, NP_, D], F16)
        wr = sb("wr", [P, KD, E])
        bias_sb = sb("bias_sb", [P, E])
        id32, id16 = sb("id32", [P, P]), sb("id16", [P, P], F16)
        sel16 = sb("sel16", [2 * H, H * DV], F16)
        pair_sel = sb("pair_sel", [P, 2])
        tri_sb = sb("tri_sb", [P, NG * NG])
        eps_qkv = sb("eps_qkv", [P, 1])
        inv_a, inv_m = sb("inv_a", [P, 1]), sb("inv_m", [P, 1])
        up_routed, up_shared = sb("up_routed", [P, 1]), sb("up_shared", [P, 1])
        attn_scale, out_scale = sb("attn_scale", [P, 1]), sb("out_scale", [P, 1])

        parts = {"wa": (wa_h, wa_l), "gate": (gate_h, gate_l), "up": (up_h, up_l), "down": (down_h, down_l),
                 "wo": (wo_h, wo_l)}
        source = {"wa": wa.rearrange("(m p) n -> p m n", p=P), "gate": w_gate.rearrange("(m p) n -> p m n", p=P),
                  "up": w_up.rearrange("(m p) n -> p m n", p=P), "down": w_down, "wo": w_out}
        groups = [("wa",), ("gate", "up"), ("down", "wo")]
        floor = [2.0 ** -40, 2.0 ** -6, 2.0 ** -20]
        order = [k for g in groups for k in g]
        flat = {k: tuple(t[:, :, :].rearrange("p a n -> p (a n)") for t in v) for k, v in parts.items()}
        big = sb("big", [P, len(order)])
        top, every = sb("top", [P, 3]), sb("every", [P, 3])
        power, scale = sb("power", [P, 3]), sb("scale", [P, 3])
        sh = sb("sh", [P, 2])

        x_sb = sb("x_sb", [P, NB, D])
        xf = sb("xf", [P, KD, T])
        xh, xl = sb("xh", [P, KD, T], F16), sb("xl", [P, KD, T], F16)
        NR_, NH_ = 4, 2 * (LAG + 1)
        ring = sb("ring", [P, NR_, T])
        qk_raw = ring[:, :, :]
        sq = sb("sq", [P, 2, T])
        ct, wt = sb("ct", [2 * E, T], F16), sb("wt", [2 * H, T], F16)
        cst, wst = sb("cst", [P, NB, 2 * E], F16), sb("wst", [P, NB, 2 * H], F16)
        stats = sb("stats", [P, NB, 6])
        ln_m, ln_mean = sb("ln_m", [P, NB]), sb("ln_mean", [P, NB])
        ln_a, ln_y, ln_t = sb("ln_a", [P, NB]), sb("ln_y", [P, NB]), sb("ln_t", [P, NB])
        qn_a, qn_y, qn_t = (sb(f"qn_{c}", [P, NB, 2 * H]) for c in "ayt")
        sc_s, sc_b, sc_m = (sb(f"sc_{c}", [P, NB, E]) for c in "sbm")
        pmax, pmin = sb("pmax", [P, NB * NG, 2]), sb("pmin", [P, NB * NG, 2])
        g_a, g_b, g_c, g_s = (sb(f"g_{c}", [P, NB * NG]) for c in "abcs")
        g_gt, g_eq = sb("g_gt", [P, NB * NG, NG]), sb("g_eq", [P, NB * NG, NG])
        top8 = sb("top8", [P, NB, 8])
        PAD = 8
        pre = [sb(f"pre{n}", [P, NB, PAD + E]) for n in range(2)]
        more, cnt = sb("more", [P, NB, E]), sb("cnt", [P, NB])

        with ExitStack() as once:
            raws = {k: once.enter_context(nc.sbuf_tensor(f"raw_{k}", [P, parts[k][0].shape[1], parts[k][0].shape[2]],
                                                         F32)) for k in order}
        raw_flat = {k: raws[k][:, :, :].rearrange("p a n -> p (a n)") for k in order}
        CUT = 2560
        width = {k: parts[k][0].shape[1] * parts[k][0].shape[2] for k in order}
        cuts = {k: [(a, min(a + CUT, width[k])) for a in range(0, width[k], CUT)] for k in order}
        pieces = [(k, a, z) for k in order for a, z in cuts[k]]

        y_sb = sb("y_sb", [P, KD, T])
        ph, pl = sb("ph", [P, NH_, T], F16), sb("pl", [P, NH_, T], F16)
        wide = sb("wide", [P, NP_, T])
        v_raw = wide[:, :, :].rearrange("p (k a) t -> p k (a t)", k=NB)
        agg = wide
        qst, kst = sb("qst", [P, 2, 2 * T], F16), sb("kst", [P, 2, 2 * T], F16)
        qt, kt = sb("qt", [P, NP_, T], F16), sb("kt", [P, NP_, T], F16)
        vh, vl = sb("vh", [P, NB, H * DV], F16), sb("vl", [P, NB, H * DV], F16)
        sg = sb("sg", [P, 2, T])
        gate_sb = sb("gate_sb", [P, 3, T])
        hf = sb("hf", [P, 2, T])
        hh, hl = sb("hh", [P, 2, T], F16), sb("hl", [P, 2, T], F16)
        ah, al = ph, pl
        vn_a, vn_y, vn_t = (sb(f"vn_{c}", [P, NB, H]) for c in "ayt")
        an_a, an_y, an_t = sb("an_a", [P, NB, H]), sb("an_y", [P, NB, H]), vn_t
        th = an_t

        sim = [ctx.enter_context(nc.psum_tensor(f"sim{n}", [P, T], F32)) for n in range(2)]
        av = ctx.enter_context(nc.psum_tensor("av", [P, T], F32))
        acc = [ctx.enter_context(nc.psum_tensor(f"acc{n}", [P, T], F32)) for n in range(KD)]
        wk = [ctx.enter_context(nc.psum_tensor(f"wk{n}", [P, T], F32)) for n in range(NW)]

        loaded = {k: sem(f"loaded_{k}") for k in order}
        small_loaded, set_done = sem("small_loaded"), sem("set_done")
        big_done, top_done, every_done = sem("big_done"), sem("top_done"), sem("every_done")
        scale_step, hi_done, lo_done = sem("scale_step"), sem("hi_done"), sem("lo_done")
        SCALE_STEPS = 4
        SMALL = 16 * 6

        x_loaded, res_loaded, stored = sem("x_loaded"), sem("res_loaded"), sem("stored")
        work_full = sem("work_full")
        sim_full, relu_done, square_done = sem("sim_full"), sem("relu_done"), sem("square_done")
        ph_done, pl_done, av_step = sem("ph_done"), sem("pl_done"), sem("av_step")
        agg_done, agg_sq_done = sem("agg_done"), sem("agg_sq_done")
        down_done, y_done = sem("down_done"), sem("y_done")
        ln_step, xn_done, xf_done = sem("ln_step"), sem("xn_done"), sem("xf_done")
        xh_done, xl_done = sem("xh_done"), sem("xl_done")
        raw_done, rawsq_done, norm_done = sem("raw_done"), sem("rawsq_done"), sem("norm_done")
        qn_step, vn_step, an_step = sem("qn_step"), sem("vn_step"), sem("an_step")
        qkn_done, vn_done = sem("qkn_done"), sem("vn_done")
        qk_hi, qk_lo, q_turned = sem("qk_hi"), sem("qk_lo"), sem("q_turned")
        k_turned = sem("k_turned")
        v_hi, v_lo = sem("v_hi"), sem("v_lo")
        score_done, route_step, ct_done = sem("score_done"), sem("route_step"), sem("ct_done")
        silu_done, sgc_done = sem("silu_done"), sem("sgc_done")
        hf_done, h_hi, h_lo = sem("hf_done"), sem("h_hi"), sem("h_lo")
        n_done, th_done, wt_done = sem("n_done"), sem("th_done"), sem("wt_done")
        gsilu_done, gate_done, gw_done = sem("gsilu_done"), sem("gate_done"), sem("gw_done")
        a_done, a_hi, a_lo = sem("a_done"), sem("a_hi"), sem("a_lo")
        out_mm = sem("out_mm")

        def upto(b, per, c):
            return max(b * per + c, 0) if isinstance(b, int) else b * per + c

        def place(b, key):
            if key[0] not in AHEAD and isinstance(b, int) and b == B - 1:
                return LAST.index(key)
            return WORK[key]

        def filled(b, key):
            if isinstance(b, int) and b < 0:
                return 0
            if key[0] in AHEAD:
                if isinstance(b, int) and b == 0:
                    return FIRST.index(key) + 1
                return upto(b - 1, PER, len(FIRST) + WORK[key] + 1)
            return upto(b, PER, len(FIRST) + place(b, key) + 1)

        def bank(b, key):
            if key[0] in AHEAD and isinstance(b, int) and b == 0:
                return wk[FIRST.index(key) % NW]
            return wk[(len(FIRST) + place(b, key)) % NW]

        def bank16(b, key):
            return bank(b, key)[:, :].bitcast(F16)

        def read(b, key):
            kind, n = key
            s, per, count = {
                "R": (score_done, 2, n + 1),
                "QK": (raw_done, 3 * NB, n + 1),
                "V": (raw_done, 3 * NB, NB + n + 1),
                "T": (k_turned if n % 2 else q_turned, NB, n // 2 + 1),
                "CT": (ct_done, 1, 1),
                "c": (sgc_done, E, ROUTED.index(n) + 1 if n in ROUTED else 0),
                "g": (silu_done, EA, ORDER.index(n) + 1),
                "u": (hf_done, EA, ORDER.index(n) + 1),
                "N": (n_done, NP_, n + 1),
                "G": (gsilu_done, NP_, n + 1),
                "WT": (wt_done, 1, 1),
                "WB": (gw_done, NP_, n + 1),
                "X": (xf_done, 2, n + 1),
            }[kind]
            return s, upto(b, per, count)

        def bank_read(b, key):
            if key[0] in AHEAD:
                b = b - 1
            if isinstance(b, int) and b < 0:
                n = FIRST.index(key) - NW
                return read(0, FIRST[n]) if n >= 0 else (xf_done, 0)
            n = place(b, key) - NW
            if n >= 0:
                before = (LAST if isinstance(b, int) and b == B - 1 else ORDERED)[n]
                return read(b + 1 if before[0] in AHEAD else b, before)
            if isinstance(b, int) and b == 0:
                return read(0, FIRST[n])
            return read(b if ORDERED[n][0] in AHEAD else b - 1, ORDERED[n])

        def rounds(eng, body):
            body(0, False)
            with eng.Fori(1, B - 1) as b:
                body(b, False)
            body(B - 1, True)

        block = ctx.enter_context(nc.Block())

        @block.sync
        def _(sp):
            def load_x(b):
                sp.wait_ge(work_full, filled(b - 1, ("X", 1)))
                sp.dma_start(x_sb[:, :, :], x[b].rearrange("(k p) d -> p k d", p=P)).then_inc(x_loaded, 16)

            load_x(0)
            sp.dma_start(id32[:, :], ident).then_inc(small_loaded, 16)
            sp.dma_start(wr[:, :, :], w_router.rearrange("(m p) e -> p m e", p=P)).then_inc(small_loaded, 16)
            sp.dma_start(bias_sb[:, :], bias).then_inc(small_loaded, 16)
            sp.dma_start(tri_sb[:, :], tri).then_inc(small_loaded, 16)
            sp.dma_start(id16[:, :], ident_h).then_inc(small_loaded, 16)
            sp.dma_start(sel16[:, :], sel).then_inc(small_loaded, 16)
            for k in order:
                sp.dma_start(raws[k][:, :, :], source[k]).then_inc(loaded[k], 16)
            sp.wait_ge(lo_done, len(pieces))

            def body(b, last):
                if not last:
                    load_x(b + 1)
                sp.wait_ge(stored, upto(b, 16, 0))
                sp.dma_start(y_sb[:, :, :], x_t[b].rearrange("(m p) t -> p m t", p=P)).then_inc(res_loaded, 16)
                sp.wait_ge(y_done, upto(b, KD, KD))
                sp.dma_start(out_t[b].rearrange("(m p) t -> p m t", p=P), y_sb[:, :, :]).then_inc(stored, 16)

            rounds(sp, body)
            sp.wait_ge(stored, 16 * B)

        @block.vector
        def _(dve):
            v = nc.vector

            class Chain:

                def __init__(self, s, b, per):
                    self.s, self.b, self.per, self.n = s, b, per, 0

                def __call__(self, ins):
                    ins.then_inc(self.s, 1)
                    self.n += 1
                    dve.wait_ge(self.s, self.b * self.per + self.n)

                def end(self):
                    assert self.n == self.per, (self.n, self.per)

            def rsqrt_guess(link, a, y):
                link(v.tensor_scalar(y.bitcast(I32), a.bitcast(I32), 1, None, ALU.logical_shift_right))
                link(v.tensor_scalar(y.bitcast(I32), y.bitcast(I32), -1.0, float(RSQRT_MAGIC), ALU.mult, ALU.add))

            def newton(link, a, y, t):
                link(v.tensor_tensor(t, y, y, ALU.mult))
                link(v.scalar_tensor_tensor(out=t, in0=a, scalar=-0.5, in1=t, op0=ALU.mult, op1=ALU.mult))
                link(v.scalar_tensor_tensor(out=y, in0=t, scalar=1.5, in1=y, op0=ALU.add, op1=ALU.mult))

            def rsqrt(link, a, y, t):
                rsqrt_guess(link, a, y)
                for _ in range(3):
                    newton(link, a, y, t)

            def layernorm(b):
                link = Chain(ln_step, b, 4 + RSQRT_STEPS)
                a, y, t = ln_a[:, :], ln_y[:, :], ln_t[:, :]
                dve.wait_ge(x_loaded, upto(b, 16, 16))
                dve.wait_ge(xn_done, upto(b, NB, 0))
                for k in range(NB):
                    ins = v.bn_stats(stats[:, k, :], x_sb[:, k, :])
                    if k < NB - 1:
                        yield
                yield link(ins)
                v.tensor_tensor(ln_m[:, :], stats[:, :, 1], stats[:, :, 4], ALU.add)
                v.tensor_tensor(a, stats[:, :, 2], stats[:, :, 5], ALU.add)
                yield link(v.tensor_tensor(t, stats[:, :, 1], stats[:, :, 4], ALU.subtract))
                v.tensor_scalar(ln_mean[:, :], ln_m[:, :], 0.5, None, ALU.mult)
                v.tensor_scalar(a, a, 1.0 / D, EPS_LN, ALU.mult, ALU.add)
                yield link(v.scalar_tensor_tensor(out=y, in0=t, scalar=0.25, in1=t, op0=ALU.mult, op1=ALU.mult))
                yield link(v.tensor_tensor(a, a, y, ALU.add))
                yield rsqrt_guess(link, a, y)
                for _ in range(3):
                    yield newton(link, a, y, t)
                link.end()
                for k in range(NB):
                    v.tensor_scalar(x_sb[:, k, :], x_sb[:, k, :], ln_mean[:, k:k + 1], ln_y[:, k:k + 1],
                                    ALU.subtract, ALU.mult).then_inc(xn_done, 1)
                    yield

            def tokens_lo(b):
                dve.wait_ge(xf_done, upto(b, 2, 2))
                dve.wait_ge(xh_done, upto(b, 1, 1))
                dve.wait_ge(work_full, filled(b - 1, ("G", NP_ - 1)))
                v.tensor_tensor(xl[:, :, :], xf[:, :, :], xh[:, :, :], ALU.subtract).then_inc(xl_done, 1)

            def sums(b, n):
                dve.wait_ge(rawsq_done, upto(b, 3 * NB, n + 1))
                if n < NB:
                    v.tensor_reduce(qn_a[:, n, :], sq[:, n % 2, :].rearrange("p (h d) -> p h d", d=DK), AX.X,
                                    ALU.add).then_inc(norm_done, 1)
                else:
                    k, half = (n - NB) // 2, (n - NB) % 2
                    v.tensor_reduce(vn_a[:, k, half * 8:half * 8 + 8],
                                    sq[:, n % 2, :].rearrange("p (h d) -> p h d", d=DV), AX.X,
                                    ALU.add).then_inc(norm_done, 1)

            def norms_begin(b, which):
                if which == "qk":
                    dve.wait_ge(qkn_done, upto(b, NB, 0))
                    dve.wait_ge(norm_done, upto(b, 3 * NB, NB))
                    link, a, y = Chain(qn_step, b, 1 + RSQRT_STEPS), qn_a, qn_y
                else:
                    dve.wait_ge(vn_done, upto(b, 2 * NB, 0))
                    dve.wait_ge(norm_done, upto(b, 3 * NB, 3 * NB))
                    link, a, y = Chain(vn_step, b, 1 + RSQRT_STEPS), vn_a, vn_y
                link(v.tensor_scalar(a[:, :, :], a[:, :, :], eps_qkv[:, 0:1], None, ALU.max))
                rsqrt_guess(link, a[:, :, :], y[:, :, :])
                return link

            def norms_round(link, which):
                a, y, t = (qn_a, qn_y, qn_t) if which == "qk" else (vn_a, vn_y, vn_t)
                newton(link, a[:, :, :], y[:, :, :], t[:, :, :])

            def unit_qk(b, k):
                dve.wait_ge(raw_done, upto(b, 3 * NB, k + 1))
                blk = qk_raw[:, k, :].rearrange("p (h d) -> p h d", d=DK)
                v.scalar_tensor_tensor(out=blk, in0=blk, scalar=QK_SCALE,
                                       in1=qn_y[:, k, :].unsqueeze(2).to_broadcast([P, 2 * H, DK]),
                                       op0=ALU.mult, op1=ALU.mult).then_inc(qkn_done, 1)

            def unit_v(b, n):
                k, half = n // 2, n % 2
                dve.wait_ge(raw_done, upto(b, 3 * NB, NB + n + 1))
                blk = v_raw[:, k, half * T:half * T + T].rearrange("p (h d) -> p h d", d=DV)
                v.scalar_tensor_tensor(out=blk, in0=blk, scalar=V_SCALE,
                                       in1=vn_y[:, k, half * 8:half * 8 + 8].unsqueeze(2).to_broadcast([P, 8, DV]),
                                       op0=ALU.mult, op1=ALU.mult).then_inc(vn_done, 1)

            def turned_q(b, k):
                dve.wait_ge(work_full, filled(b, ("T", 2 * k)))
                dve.wait_ge(sim_full, upto(b, 2 * STEPS, 0))
                v.tensor_copy(qt[:, :, k * P:(k + 1) * P],
                              bank16(b, ("T", 2 * k))[:, :].rearrange("p (m t) -> p m t", m=NP_)).then_inc(q_turned, 1)

            tt = v.tensor_tensor

            def route(b):
                link = Chain(route_step, b, ROUTE_STEPS)
                dve.wait_ge(score_done, upto(b, 2, 2))
                bias_all = bias_sb[:, :].unsqueeze(1).to_broadcast([P, NB, E])
                yield link(tt(sc_b[:, :, :], sc_s[:, :, :], bias_all, ALU.add))
                two = sc_b[:, :, :].rearrange("p k (g a c) -> p (k g) a c", a=2, c=2)
                yield link(tt(pmax[:, :, :], two[:, :, :, 0], two[:, :, :, 1], ALU.max))
                yield link(tt(pmin[:, :, :], two[:, :, :, 0], two[:, :, :, 1], ALU.min))
                yield link(tt(g_a[:, :], pmax[:, :, 0], pmax[:, :, 1], ALU.max))
                yield link(tt(g_b[:, :], pmax[:, :, 0], pmax[:, :, 1], ALU.min))
                yield link(tt(g_c[:, :], pmin[:, :, 0], pmin[:, :, 1], ALU.max))
                yield link(tt(g_b[:, :], g_b[:, :], g_c[:, :], ALU.max))
                yield link(tt(g_s[:, :], g_a[:, :], g_b[:, :], ALU.add))
                other = g_s[:, :].rearrange("p (k j) -> p k j", j=NG).unsqueeze(2).to_broadcast([P, NB, NG, NG])
                mine = g_s[:, :].rearrange("p (k g) -> p k g", g=NG).unsqueeze(3).to_broadcast([P, NB, NG, NG])
                tt(g_gt[:, :, :].rearrange("p (k g) j -> p k g j", k=NB), other, mine, ALU.is_gt)
                yield link(tt(g_eq[:, :, :].rearrange("p (k g) j -> p k g j", k=NB), other, mine, ALU.is_equal))
                eq = g_eq[:, :, :].rearrange("p (k g) j -> p k (g j)", k=NB)
                yield link(tt(eq, eq, tri_sb[:, :].unsqueeze(1).to_broadcast([P, NB, NG * NG]), ALU.mult))
                yield link(tt(g_gt[:, :, :], g_gt[:, :, :], g_eq[:, :, :], ALU.add))
                yield link(v.tensor_reduce(g_a[:, :], g_gt[:, :, :], AX.X, ALU.add))
                yield link(v.tensor_scalar(g_a[:, :], g_a[:, :], 1.5, None, ALU.is_lt))
                per_group = sc_m[:, :, :].rearrange("p k (g c) -> p (k g) c", c=GE)
                yield link(tt(per_group, sc_b[:, :, :].rearrange("p k (g c) -> p (k g) c", c=GE),
                        g_a[:, :].unsqueeze(2).to_broadcast([P, NB * NG, GE]), ALU.mult))
                yield link(v.tensor_scalar(sc_m[:, :, :], sc_m[:, :, :], 0.0, None, ALU.add))
                for n in range(2):
                    v.memset(pre[n][:, :, 0:PAD], 0.0)
                for k in range(NB):
                    ins = v.max(top8[:, k, :], sc_m[:, k, :])
                yield link(ins)
                fourth = top8[:, :, 3:4].to_broadcast([P, NB, E])
                yield link(tt(more[:, :, :], sc_m[:, :, :], fourth, ALU.is_gt))
                yield link(tt(pre[0][:, :, PAD:], sc_m[:, :, :], fourth, ALU.is_equal))
                yield link(v.tensor_copy(sc_b[:, :, :], pre[0][:, :, PAD:]))
                yield link(v.tensor_reduce(cnt[:, :], more[:, :, :], AX.X, ALU.add))
                for n, d in enumerate((1, 2, 4, 8)):
                    src, dst = pre[n % 2], pre[(n + 1) % 2]
                    yield link(tt(dst[:, :, PAD:], src[:, :, PAD:], src[:, :, PAD - d:PAD + E - d], ALU.add))
                yield link(tt(pre[0][:, :, PAD:], pre[0][:, :, PAD:], cnt[:, :].unsqueeze(2).to_broadcast([P, NB, E]),
                        ALU.add))
                yield link(v.scalar_tensor_tensor(out=sc_b[:, :, :], in0=pre[0][:, :, PAD:], scalar=4.5,
                                            in1=sc_b[:, :, :], op0=ALU.is_lt, op1=ALU.mult))
                yield link(tt(more[:, :, :], more[:, :, :], sc_b[:, :, :], ALU.add))
                yield link(tt(sc_s[:, :, :], sc_s[:, :, :], more[:, :, :], ALU.mult))
                yield link(v.tensor_reduce(cnt[:, :], sc_s[:, :, :], AX.X, ALU.add))
                yield link(v.tensor_scalar(cnt[:, :], cnt[:, :], EPS_TW, None, ALU.add))
                yield link(v.reciprocal(cnt[:, :], cnt[:, :]))
                yield link(v.scalar_tensor_tensor(out=sc_m[:, :, :], in0=sc_s[:, :, :], scalar=ROUTE_SCALE * C_SCALE,
                                            in1=cnt[:, :].unsqueeze(2).to_broadcast([P, NB, E]),
                                            op0=ALU.mult, op1=ALU.mult))
                dve.wait_ge(work_full, filled(b - 1, ("CT", 0)))
                yield link(v.tensor_copy(cst[:, :, 0:E], sc_m[:, :, :]))
                yield link(tt(cst[:, :, E:2 * E], sc_m[:, :, :], cst[:, :, 0:E], ALU.subtract))
                link.end()

            def probs(b, n):
                dve.wait_ge(square_done, upto(b, 2 * STEPS, n + 1))
                dve.wait_ge(av_step, upto(b, STEPS, n // 2 - LAG))
                if n < 4:
                    dve.wait_ge(out_mm, upto(b, NP_, 0))
                v.tensor_copy(ph[:, n % NH_, :], ring[:, n % NR_, :]).then_inc(ph_done, 1)

            def probs_lo(b, n):
                dve.wait_ge(ph_done, upto(b, 2 * STEPS, n + 1))
                v.tensor_tensor(pl[:, n % NH_, :], ring[:, n % NR_, :], ph[:, n % NH_, :],
                                ALU.subtract).then_inc(pl_done, 1)

            def weigh(b, e):
                n = ORDER.index(e)
                dve.wait_ge(silu_done, upto(b, EA, n + 1))
                dve.wait_ge(work_full, filled(b, ("c", e)))
                v.tensor_tensor(sg[:, n % 2, :], sg[:, n % 2, :], bank(b, ("c", e))[:, :],
                                ALU.mult).then_inc(sgc_done, 1)

            def hidden(b, e):
                n = ORDER.index(e)
                dve.wait_ge(silu_done, upto(b, EA, n + 1))
                if e < E:
                    dve.wait_ge(sgc_done, upto(b, E, ROUTED.index(e) + 1))
                dve.wait_ge(work_full, filled(b, ("u", e)))
                dve.wait_ge(h_lo, upto(b, EA, n - 1))
                dve.wait_ge(h_hi, upto(b, EA, n - 1))
                ins = v.scalar_tensor_tensor(out=hf[:, n % 2, :], in0=bank(b, ("u", e))[:, :],
                                             scalar=(up_routed if e < E else up_shared)[:, 0:1],
                                             in1=sg[:, n % 2, :], op0=ALU.mult, op1=ALU.mult)
                ins.then_inc(hf_done, 1)

            def head_norms(b, t):
                dve.wait_ge(work_full, filled(b, ("N", t)))
                ins = v.tensor_copy(an_a[:, :, 2 * t:2 * t + 2],
                                    bank(b, ("N", t))[:, 0:2 * NB].rearrange("p (k h) -> p k h", h=2))
                ins.then_inc(n_done, 1)

            def head_scales_begin(b):
                link = Chain(an_step, b, HEAD_STEPS)
                dve.wait_ge(n_done, upto(b, NP_, NP_))
                link(v.tensor_scalar(an_a[:, :, :], an_a[:, :, :], EPS_L2 ** 2, None, ALU.max))
                rsqrt(link, an_a[:, :, :], an_y[:, :, :], an_t[:, :, :])
                link(v.tensor_tensor(an_t[:, :, :], an_a[:, :, :], an_y[:, :, :], ALU.mult))
                return link

            def head_scales_end(b, link):
                dve.wait_ge(th_done, upto(b, 1, 1))
                link(v.scalar_tensor_tensor(out=an_a[:, :, :], in0=th[:, :, :], scalar=C_SCALE, in1=an_y[:, :, :],
                                            op0=ALU.mult, op1=ALU.mult))
                link(v.tensor_copy(wst[:, :, 0:H], an_a[:, :, :]))
                link(v.tensor_tensor(wst[:, :, H:2 * H], an_a[:, :, :], wst[:, :, 0:H], ALU.subtract))
                link.end()

            def gated(b, t):
                dve.wait_ge(work_full, filled(b, ("WB", t)))
                dve.wait_ge(gate_done, upto(b, NP_, t + 1))
                ins = v.tensor_tensor(gate_sb[:, t % 3, :], gate_sb[:, t % 3, :], bank(b, ("WB", t))[:, :], ALU.mult)
                ins.then_inc(gw_done, 1)

            def gated2(b, t):
                dve.wait_ge(gw_done, upto(b, NP_, t + 1))
                dve.wait_ge(agg_done, upto(b, NP_, t + 1))
                v.scalar_tensor_tensor(out=agg[:, t, :], in0=agg[:, t, :], scalar=attn_scale[:, 0:1],
                                       in1=gate_sb[:, t % 3, :], op0=ALU.mult, op1=ALU.mult).then_inc(a_done, 1)

            def finish(b):
                dve.wait_ge(out_mm, upto(b, NP_, NP_))
                dve.wait_ge(res_loaded, upto(b, 16, 16))
                for m in range(KD):
                    v.scalar_tensor_tensor(out=y_sb[:, m, :], in0=acc[m][:, :], scalar=out_scale[:, 0:1],
                                           in1=y_sb[:, m, :], op0=ALU.mult, op1=ALU.add).then_inc(y_done, 1)

            def expert_item(b, kind, e):
                if kind == "g" and e < E:
                    weigh(b, e)
                if kind == "u":
                    hidden(b, e)
                if kind == "N":
                    head_norms(b, e)

            def linked(ins):
                links[0] += 1
                ins.then_inc(scale_step, 1)
                dve.wait_ge(scale_step, links[0])

            links = [0]

            def largest(g):
                for k in groups[g]:
                    n = order.index(k)
                    dve.wait_ge(loaded[k], 16)
                    v.tensor_reduce(big[:, n:n + 1], raw_flat[k], AX.X, ALU.max,
                                    apply_absolute_value=True).then_inc(big_done, 1)
                ns = [order.index(k) for k in groups[g]]
                dve.wait_ge(big_done, ns[-1] + 1)
                v.tensor_reduce(top[:, g:g + 1], big[:, ns[0]:ns[-1] + 1], AX.X, ALU.max).then_inc(top_done, 1)

            def scales(g):
                dve.wait_ge(every_done, g + 1)
                c = slice(g, g + 1)
                linked(v.tensor_scalar(power[:, c], every[:, c], floor[g], None, ALU.max))
                linked(v.tensor_scalar(power[:, c].bitcast(I32), power[:, c].bitcast(I32), 0x7F800000, None,
                                       ALU.bitwise_and))
                linked(v.reciprocal(scale[:, c], power[:, c]))
                linked(v.tensor_scalar(scale[:, c], scale[:, c], 2.0 ** W_EXP, None, ALU.mult))

            def low_parts(g):
                for n, (k, a, z) in enumerate(pieces):
                    if k in groups[g]:
                        dve.wait_ge(hi_done, n + 1)
                        v.scalar_tensor_tensor(out=flat[k][1][:, a:z], in0=raw_flat[k][:, a:z],
                                               scalar=scale[:, g:g + 1], in1=flat[k][0][:, a:z], op0=ALU.mult,
                                               op1=ALU.subtract).then_inc(lo_done, 1)

            def constants():
                back = 2.0 ** -W_EXP
                mult = ALU.mult
                linked(v.tensor_scalar(eps_qkv[:, :], scale[:, 0:1], scale[:, 0:1], EPS_L2 ** 2, mult, mult))
                linked(v.tensor_scalar(inv_a[:, :], power[:, 0:1], back, None, mult))
                linked(v.tensor_scalar(inv_m[:, :], power[:, 1:2], back, None, mult))
                linked(v.reciprocal(sh[:, 0:1], power[:, 1:2]))
                linked(v.tensor_scalar(up_shared[:, :], sh[:, 0:1], 2.0 ** (-5 - W_EXP), None, mult))
                linked(v.tensor_scalar(up_routed[:, :], up_shared[:, :], 1.0 / C_SCALE, None, mult))
                linked(v.tensor_scalar(sh[:, 1:2], sh[:, 0:1], sh[:, 0:1], 2.0 ** -5, mult, mult))
                linked(v.tensor_scalar(attn_scale[:, :], sh[:, 1:2], AG_UNSCALE / C_SCALE, None, mult))
                linked(v.reciprocal(sh[:, 0:1], sh[:, 1:2]))
                linked(v.tensor_scalar(out_scale[:, :], power[:, 2:3], sh[:, 0:1], back, mult, mult))

            for _ in layernorm(0):
                pass
            largest(0)
            tokens_lo(0)
            scales(0)
            largest(1)
            low_parts(0)
            scales(1)
            dve.wait_ge(small_loaded, SMALL)
            for _ in route(0):
                pass
            largest(2)
            low_parts(1)
            scales(2)
            constants()
            sums(0, 0)
            sums(0, 1)
            low_parts(2)
            dve.wait_ge(lo_done, len(pieces))

            def body(b, last):
                for n in range(2, NB):
                    sums(b, n)
                link_qk = norms_begin(b, "qk")
                sums(b, 4)
                norms_round(link_qk, "qk")
                sums(b, 5)
                norms_round(link_qk, "qk")
                norms_round(link_qk, "qk")
                link_qk.end()
                for k in range(NB):
                    unit_qk(b, k)
                    sums(b, 6 + k)
                sums(b, 10)
                turned_q(b, 0)
                sums(b, 11)
                link_v = norms_begin(b, "v")
                for kind, e in HEAD[:2]:
                    expert_item(b, kind, e)
                turned_q(b, 1)
                for _ in range(3):
                    norms_round(link_v, "v")
                link_v.end()
                turned_q(b, 2)
                unit_v(b, 0)
                unit_v(b, 1)
                for kind, e in HEAD[2:]:
                    expert_item(b, kind, e)
                turned_q(b, 3)
                for n in range(2, 2 * NB):
                    unit_v(b, n)
                next_norm = layernorm(b + 1)
                next_route = route(b + 1)
                for s in range(STEPS):
                    lead = [item for item in PLAN[s][:1] if item[0] == "u"]
                    for kind, e in lead:
                        expert_item(b, kind, e)
                    for n in (2 * s, 2 * s + 1):
                        probs(b, n)
                    for kind, e in PLAN[s][len(lead):]:
                        expert_item(b, kind, e)
                    for n in (2 * s, 2 * s + 1):
                        probs_lo(b, n)
                    if not last:
                        for _ in range(2 if s in NORM_STEPS else 0):
                            next(next_norm, None)
                        for _ in range(2 if s >= ROUTE_FROM else 0):
                            next(next_route, None)
                for kind, n in TAIL:
                    expert_item(b, kind, n)
                    if (kind, n) == ("N", NP_ - 1):
                        link_heads = head_scales_begin(b)
                    if kind == "TH":
                        head_scales_end(b, link_heads)
                for t in range(NP_):
                    gated(b, t)
                    gated2(b, t)
                    if t == NP_ - 2 and not last:
                        tokens_lo(b + 1)
                    if t == NP_ - 1 and not last:
                        sums(b + 1, 0)
                        sums(b + 1, 1)
                finish(b)

            rounds(dve, body)

        @block.scalar
        def _(act):
            a = nc.scalar.activation

            def turn_tokens(b, n):
                act.wait_ge(work_full, filled(b, ("X", n)))
                act.wait_ge(work_full, filled(b - 1, ("R", 1)))
                act.wait_ge(xh_done, upto(b, 1, 0))
                act.wait_ge(xl_done, upto(b, 1, 0))
                ins = a(xf[:, :, 2 * n * P:(2 * n + 2) * P],
                        bank(b, ("X", n))[:, :].rearrange("p (m t) -> p m t", m=KD), ACT.Copy)
                ins.then_inc(xf_done, 1)

            def tokens_hi(b):
                act.wait_ge(xf_done, upto(b, 2, 2))
                act.wait_ge(work_full, filled(b - 1, ("G", NP_ - 1)))
                a(xh[:, :, :], xf[:, :, :], ACT.Copy).then_inc(xh_done, 1)

            def router_scores(b, n):
                act.wait_ge(work_full, filled(b, ("R", n)))
                act.wait_ge(route_step, upto(b, ROUTE_STEPS, 0))
                a(sc_s[:, 2 * n:2 * n + 2, :], bank(b, ("R", n))[:, 0:2 * E].rearrange("p (k e) -> p k e", e=E),
                  ACT.Sigmoid).then_inc(score_done, 1)

            def raw(b, n):
                key = ("QK", n) if n < NB else ("V", n - NB)
                act.wait_ge(work_full, filled(b, key))
                if n < 2:
                    act.wait_ge(work_full, filled(b - 1, ("N", NP_ - 1)))
                act.wait_ge(norm_done, upto(b, 3 * NB, n - 1))
                a(sq[:, n % 2, :], bank(b, key)[:, :], ACT.Square).then_inc(rawsq_done, 1)
                if n < NB:
                    act.wait_ge(pl_done, upto(b, 2 * STEPS, 0))
                    dst = qk_raw[:, n, :]
                else:
                    k, half = (n - NB) // 2, (n - NB) % 2
                    act.wait_ge(a_hi, upto(b - 1, NP_, n - NB + 1))
                    act.wait_ge(a_lo, upto(b - 1, NP_, n - NB + 1))
                    dst = v_raw[:, k, half * T:half * T + T]
                a(dst, bank(b, key)[:, :], ACT.Copy).then_inc(raw_done, 1)

            def high_parts(g):
                for k, lo, hi in pieces:
                    if k in groups[g]:
                        act.wait_ge(scale_step, SCALE_STEPS * (g + 1))
                        a(flat[k][0][:, lo:hi], raw_flat[k][:, lo:hi], ACT.Copy,
                          scale=scale[:, g:g + 1]).then_inc(hi_done, 1)

            turn_tokens(0, 0)
            turn_tokens(0, 1)
            tokens_hi(0)
            router_scores(0, 0)
            router_scores(0, 1)
            high_parts(0)
            high_parts(1)
            raw(0, 0)
            raw(0, 1)
            high_parts(2)
            act.wait_ge(lo_done, len(pieces))

            def split_hi_qk(b, k):
                act.wait_ge(qkn_done, upto(b, NB, k + 1))
                if k >= 2:
                    act.wait_ge(work_full, filled(b, ("T", 2 * k - 3)))
                else:
                    act.wait_ge(work_full, filled(b - 1, ("T", 2 * k + 5)))
                blk = qk_raw[:, k, :]
                for c, dst, dims in ((0, qst, 0), (1, kst, 1)):
                    src = blk[:, c * H * DK:(c + 1) * H * DK].rearrange("p (h d) -> p h d", d=DK)
                    src = src.unsqueeze(2).to_broadcast([P, H, 2, DK])
                    to = dst[:, k % 2, :].rearrange("p (h a c d) -> p h a c d", a=2, c=2, d=DK)
                    to = to[:, :, 0, :, :] if c == 0 else to[:, :, :, 0, :]
                    a(to, src, ACT.Copy).then_inc(qk_hi, 1)

            def turned_k(b, k):
                act.wait_ge(work_full, filled(b, ("T", 2 * k + 1)))
                act.wait_ge(sim_full, upto(b, 2 * STEPS, 0))
                a(kt[:, :, k * P:(k + 1) * P], bank16(b, ("T", 2 * k + 1))[:, :].rearrange("p (m t) -> p m t", m=NP_),
                  ACT.Copy).then_inc(k_turned, 1)

            def split_hi_v(b, n):
                k, half = n // 2, n % 2
                act.wait_ge(vn_done, upto(b, 2 * NB, n + 1))
                act.wait_ge(av_step, upto(b, STEPS, 0))
                a(vh[:, k, half * T:half * T + T], v_raw[:, k, half * T:half * T + T], ACT.Copy).then_inc(v_hi, 1)

            def relu(b, n):
                act.wait_ge(sim_full, upto(b, 2 * STEPS, n + 1))
                act.wait_ge(pl_done, upto(b, 2 * STEPS, n - NR_ + 1))
                if n < NR_:
                    act.wait_ge(qk_lo, upto(b, 2 * NB, 2 * NB))
                a(ring[:, n % NR_, :], sim[n % 2][:, :], ACT.Relu, scale=S_SCALE).then_inc(relu_done, 1)

            def square(b, n):
                act.wait_ge(relu_done, upto(b, 2 * STEPS, n + 1))
                a(ring[:, n % NR_, :], ring[:, n % NR_, :], ACT.Square).then_inc(square_done, 1)

            def silu(b, e):
                n = ORDER.index(e)
                act.wait_ge(work_full, filled(b, ("g", e)))
                act.wait_ge(hf_done, upto(b, EA, n - 1))
                ins = a(sg[:, n % 2, :], bank(b, ("g", e))[:, :], ACT.Silu, scale=inv_m[:, 0:1])
                ins.then_inc(silu_done, 1)

            def hidden_hi(b, n):
                act.wait_ge(hf_done, upto(b, EA, n + 1))
                act.wait_ge(down_done, upto(b, EA, n - 1))
                a(hh[:, n % 2, :], hf[:, n % 2, :], ACT.Copy).then_inc(h_hi, 1)

            def square_heads(b, t, src=None):
                if t >= 2:
                    act.wait_ge(work_full, filled(b, ("N", t - 2)))
                else:
                    act.wait_ge(norm_done, upto(b, 3 * NB, 3 * NB))
                if src is None:
                    act.wait_ge(agg_done, upto(b, NP_, t + 1))
                    a(sq[:, t % 2, :], agg[:, t, :], ACT.Square, scale=AG_UNSCALE).then_inc(agg_sq_done, 1)
                else:
                    act.wait_ge(av_step, upto(b, STEPS, NB * (t + 1)))
                    a(sq[:, t % 2, :], src, ACT.Square, scale=AG_UNSCALE).then_inc(agg_sq_done, 1)

            def take_heads(b, t):
                act.wait_ge(av_step, upto(b, STEPS, NB * (t + 1)))
                act.wait_ge(v_lo, upto(b, 2 * NB, 2 * NB))
                act.wait_ge(v_hi, upto(b, 2 * NB, 2 * NB))
                a(agg[:, t, :], av[:, :], ACT.Copy).then_inc(agg_done, 1)

            def gate(b, t):
                act.wait_ge(work_full, filled(b, ("G", t)))
                act.wait_ge(a_done, upto(b, NP_, t - 2))
                ins = a(gate_sb[:, t % 3, :], bank(b, ("G", t))[:, :], ACT.Silu, scale=inv_a[:, 0:1])
                ins.then_inc(gsilu_done, 1)
                act.wait_ge(gsilu_done, upto(b, NP_, t + 1))
                a(gate_sb[:, t % 3, :], gate_sb[:, t % 3, :], ACT.Tanh).then_inc(gate_done, 1)

            def attention_hi(b, t):
                act.wait_ge(a_done, upto(b, NP_, t + 1))
                act.wait_ge(out_mm, upto(b, NP_, t - 1))
                a(ah[:, t % 2, :], agg[:, t, :], ACT.Copy).then_inc(a_hi, 1)

            def expert_item(b, kind, e):
                if kind == "g":
                    silu(b, e)
                if kind == "u" and ORDER.index(e) >= 1:
                    hidden_hi(b, ORDER.index(e) - 1)

            def whole(b, last):
                raw(b, 2)
                raw(b, 3)
                act.wait_ge(work_full, filled(b, ("CT", 0)))
                act.wait_ge(work_full, filled(b - 1, ("c", ROUTED[-1])))
                a(ct[:, :], bank16(b, ("CT", 0))[0:2 * E, 0:T], ACT.Copy).then_inc(ct_done, 1)
                for n in range(4, 8):
                    raw(b, n)
                split_hi_qk(b, 0)
                raw(b, 8)
                split_hi_qk(b, 1)
                raw(b, 9)
                expert_item(b, *HEAD[0])
                raw(b, 10)
                raw(b, 11)
                turned_k(b, 0)
                split_hi_qk(b, 2)
                expert_item(b, *HEAD[1])
                turned_k(b, 1)
                split_hi_qk(b, 3)
                expert_item(b, *HEAD[2])
                turned_k(b, 2)
                expert_item(b, *HEAD[3])
                split_hi_v(b, 0)
                split_hi_v(b, 1)
                turned_k(b, 3)
                for s in range(STEPS):
                    if s % NB == LAG and s > NB:
                        take_heads(b, s // NB - 1)
                    for n in (2 * s, 2 * s + 1):
                        relu(b, n)
                    for n in (2 * s, 2 * s + 1):
                        square(b, n)
                    for kind, e in PLAN[s]:
                        if kind == "X" and not last:
                            turn_tokens(b + 1, e)
                        elif kind == "R" and not last:
                            router_scores(b + 1, e)
                        else:
                            expert_item(b, kind, e)
                    if s in (1, 2, 3):
                        split_hi_v(b, 2 * s)
                        split_hi_v(b, 1 + 2 * s)
                    if s % NB == LAG and s > NB:
                        square_heads(b, s // NB - 1)
                for kind, n in TAIL:
                    if kind == "G":
                        gate(b, n)
                    elif (kind, n) == ("AV", STEPS - 1):
                        square_heads(b, NP_ - 1, av[:, :])
                        take_heads(b, NP_ - 1)
                    elif kind == "TH":
                        act.wait_ge(an_step, upto(b, HEAD_STEPS, HEAD_STEPS - 3))
                        a(th[:, :, :], an_t[:, :, :], ACT.Tanh).then_inc(th_done, 1)
                    elif kind == "WT":
                        act.wait_ge(work_full, filled(b, ("WT", 0)))
                        act.wait_ge(work_full, filled(b - 1, ("WB", NP_ - 1)))
                        a(wt[:, :], bank16(b, ("WT", 0))[0:2 * H, 0:T], ACT.Copy).then_inc(wt_done, 1)
                    elif (kind, n) == ("d", ORDER[-2]):
                        hidden_hi(b, EA - 1)
                    else:
                        expert_item(b, kind, n)
                attention_hi(b, 0)
                for t in range(NP_):
                    if t + 1 < NP_:
                        attention_hi(b, t + 1)
                    if t + 3 < NP_:
                        gate(b, t + 3)
                    if t == NP_ - 4 and not last:
                        tokens_hi(b + 1)
                    if t > NP_ - 3 and not last:
                        raw(b + 1, t - (NP_ - 2))

            rounds(act, whole)

        @block.gpsimd
        def _(pool):
            tt = nc.gpsimd.tensor_tensor

            def split_lo_qk(b, k):
                for c, dst in ((0, qst), (1, kst)):
                    pool.wait_ge(qk_hi, upto(b, 2 * NB, 2 * k + c + 1))
                    src = qk_raw[:, k, c * H * DK:(c + 1) * H * DK].rearrange("p (h d) -> p h d", d=DK)
                    src = src.unsqueeze(2).to_broadcast([P, H, 2, DK])
                    to = dst[:, k % 2, :].rearrange("p (h a c d) -> p h a c d", a=2, c=2, d=DK)
                    hi, lo = ((to[:, :, 0, :, :], to[:, :, 1, :, :]) if c == 0
                              else (to[:, :, :, 0, :], to[:, :, :, 1, :]))
                    tt(lo, src, hi, ALU.subtract).then_inc(qk_lo, 1)

            def split_lo_v(b, n):
                k, half = n // 2, n % 2
                pool.wait_ge(v_hi, upto(b, 2 * NB, n + 1))
                pool.wait_ge(av_step, upto(b, STEPS, 0))
                sl = slice(half * T, half * T + T)
                tt(vl[:, k, sl], v_raw[:, k, sl], vh[:, k, sl], ALU.subtract).then_inc(v_lo, 1)

            def body(b, last):
                def hidden_lo(n):
                    pool.wait_ge(h_hi, upto(b, EA, n + 1))
                    pool.wait_ge(down_done, upto(b, EA, n - 1))
                    tt(hl[:, n % 2, :], hf[:, n % 2, :], hh[:, n % 2, :], ALU.subtract).then_inc(h_lo, 1)

                for k in range(NB):
                    split_lo_qk(b, k)
                hidden_lo(0)
                for n in range(2):
                    split_lo_v(b, n)
                for s in range(STEPS):
                    for kind, e in PLAN[s]:
                        if kind == "u":
                            hidden_lo(ORDER.index(e) - 1)
                    if s in (1, 2, 3):
                        split_lo_v(b, 2 * s)
                        split_lo_v(b, 1 + 2 * s)
                for kind, e in TAIL:
                    if kind == "u":
                        hidden_lo(ORDER.index(e) - 1)
                hidden_lo(EA - 1)
                for t in range(NP_):
                    pool.wait_ge(a_hi, upto(b, NP_, t + 1))
                    pool.wait_ge(out_mm, upto(b, NP_, t - 1))
                    tt(al[:, t % 2, :], agg[:, t, :], ah[:, t % 2, :], ALU.subtract).then_inc(a_lo, 1)

            for half in range(2):
                rows = slice(64 * half, 64 * half + 64)
                pool.memset(pair_sel[rows, half:half + 1], 1.0).then_inc(set_done, 1)
                pool.memset(pair_sel[rows, 1 - half:2 - half], 0.0).then_inc(set_done, 1)
            pool.wait_ge(set_done, 4)
            for g in range(3):
                pool.wait_ge(top_done, g + 1)
                pool.partition_all_reduce(every[:, g:g + 1], top[:, g:g + 1], P,
                                          bass.bass_isa.ReduceOp.max).then_inc(every_done, 1)
            pool.wait_ge(lo_done, len(pieces))
            rounds(pool, body)

        @block.tensor
        def _(pe):
            mm, turn = nc.tensor.matmul, nc.tensor.transpose

            def products(dst, w_parts, x_parts, first=True, last=True):
                (w_h, w_l), (x_h, x_l) = w_parts, x_parts
                terms = [(w, x_h) for w in (w_h, w_l)] + [(w_h, x_l)]
                n = len(terms) * len(w_h)
                i = 0
                for w, xx in terms:
                    for k in range(len(w_h)):
                        ins = mm(dst, w[k], xx[k], start=first and i == 0, stop=last and i == n - 1)
                        i += 1
                return ins

            def turn_tokens(b, n):
                pe.wait_ge(xn_done, upto(b, NB, 2 * n + 2))
                pe.wait_ge(*bank_read(b, ("X", n)))
                for m in range(KD):
                    for k in range(2):
                        ins = turn(bank(b, ("X", n))[:, (2 * m + k) * P:(2 * m + k + 1) * P],
                                   x_sb[:, 2 * n + k, m * P:(m + 1) * P], id32[:, :])
                ins.then_inc(work_full, 1)

            def router(b, n):
                pe.wait_ge(xf_done, upto(b, 2, 2))
                pe.wait_ge(*bank_read(b, ("R", n)))
                for k in range(2):
                    blk = slice((2 * n + k) * P, (2 * n + k + 1) * P)
                    for m in range(KD):
                        ins = mm(bank(b, ("R", n))[:, k * E:(k + 1) * E], xf[:, m, blk], wr[:, m, :],
                                 start=(m == 0), stop=(m == KD - 1))
                ins.then_inc(work_full, 1)

            def project(b, key, k, lo, width):
                if key == ("QK", 0):
                    pe.wait_ge(xh_done, upto(b, 1, 1))
                    pe.wait_ge(xl_done, upto(b, 1, 1))
                pe.wait_ge(*bank_read(b, key))
                blk, cols = slice(k * P, (k + 1) * P), slice(lo, lo + width)
                ins = products(bank(b, key)[:, 0:width], ([xh[:, m, blk] for m in range(KD)],
                                                       [xl[:, m, blk] for m in range(KD)]),
                               ([wa_h[:, m, cols] for m in range(KD)], [wa_l[:, m, cols] for m in range(KD)]))
                ins.then_inc(work_full, 1)

            def turn_qk(b, n):
                k, keys = n // 2, n % 2
                pe.wait_ge(qk_lo, upto(b, 2 * NB, n + 1))
                pe.wait_ge(*bank_read(b, ("T", n)))
                src = (kst if keys else qst)[:, k % 2, :]
                for m in range(NP_):
                    ins = turn(bank16(b, ("T", n))[:, m * P:(m + 1) * P], src[:, m * P:(m + 1) * P], id16[:, :])
                ins.then_inc(work_full, 1)

            def turn_small(b, key, src):
                pe.wait_ge(*bank_read(b, key))
                for k in range(NB):
                    ins = turn(bank16(b, key)[0:2 * E, k * P:(k + 1) * P], src[:, k, :], id16[:, :])
                ins.then_inc(work_full, 1)

            def scores(b, s):
                pair, j = s // NB, s % NB
                if s == 0:
                    pe.wait_ge(q_turned, upto(b, NB, NB))
                    pe.wait_ge(k_turned, upto(b, NB, NB))
                for half in range(2):
                    n = 2 * s + half
                    pe.wait_ge(relu_done, upto(b, 2 * STEPS, n - 1))
                    rows = slice(64 * half, 64 * half + 64)
                    mm(sim[half][:, :], kt[rows, pair, j * P:(j + 1) * P], qt[rows, pair, :], start=True,
                       stop=True).then_inc(sim_full, 1)

            def values(b, s):
                pair, j = s // NB, s % NB
                pe.wait_ge(pl_done, upto(b, 2 * STEPS, 2 * s + 2))
                if pair == 0:
                    pe.wait_ge(v_lo, upto(b, 2 * NB, 2 * (j + 1)))
                if j == 0:
                    pe.wait_ge(agg_done, upto(b, NP_, pair))
                for i, (vv, pp) in enumerate(((vh, ph), (vl, ph), (vh, pl))):
                    for half in range(2):
                        h = 2 * pair + half
                        ins = mm(av[64 * half:64 * half + 64, :], vv[:, j, h * DV:(h + 1) * DV],
                                 pp[:, (2 * s + half) % NH_, :], start=(j == 0 and i == 0),
                                 stop=(j == NB - 1 and i == 2))
                ins.then_inc(av_step, 1)

            def head_sums(b, t):
                pe.wait_ge(agg_sq_done, upto(b, NP_, t + 1))
                pe.wait_ge(*bank_read(b, ("N", t)))
                for k in range(NB):
                    ins = mm(bank(b, ("N", t))[:, 2 * k:2 * k + 2], sq[:, t % 2, k * P:(k + 1) * P], pair_sel[:, :],
                             start=True, stop=True)
                ins.then_inc(work_full, 1)

            def item(b, kind, e):
                n = ORDER.index(e)
                cols = slice(e * P, (e + 1) * P)
                if kind == "c":
                    pe.wait_ge(ct_done, upto(b, 1, 1))
                    pe.wait_ge(*bank_read(b, (kind, e)))
                    for half in range(2):
                        ins = mm(bank(b, (kind, e))[64 * half:64 * half + 64, :], sel16[:, e * DV:(e + 1) * DV],
                                 ct[:, :], start=True, stop=True)
                    ins.then_inc(work_full, 1)
                elif kind in "gu":
                    pe.wait_ge(*bank_read(b, (kind, e)))
                    wh, wl = (gate_h, gate_l) if kind == "g" else (up_h, up_l)
                    ins = products(bank(b, (kind, e))[:, :], ([wh[:, m, cols] for m in range(KD)],
                                                           [wl[:, m, cols] for m in range(KD)]),
                                   ([xh[:, m, :] for m in range(KD)], [xl[:, m, :] for m in range(KD)]))
                    ins.then_inc(work_full, 1)
                else:
                    pe.wait_ge(h_hi, upto(b, EA, n + 1))
                    pe.wait_ge(h_lo, upto(b, EA, n + 1))
                    if n == 0:
                        pe.wait_ge(y_done, upto(b, KD, 0))
                    for m in range(KD):
                        mc = slice(m * P, (m + 1) * P)
                        ins = products(acc[m][:, :], ([down_h[:, e, mc]], [down_l[:, e, mc]]),
                                       ([hh[:, n % 2, :]], [hl[:, n % 2, :]]), first=(n == 0), last=False)
                    ins.then_inc(down_done, 1)

            def gates(b, t):
                pe.wait_ge(*bank_read(b, ("G", t)))
                cols = slice(G_AT + t * P, G_AT + (t + 1) * P)
                products(bank(b, ("G", t))[:, :], ([wa_h[:, m, cols] for m in range(KD)],
                                                [wa_l[:, m, cols] for m in range(KD)]),
                         ([xh[:, m, :] for m in range(KD)], [xl[:, m, :] for m in range(KD)])).then_inc(work_full, 1)

            def spread(b, t):
                pe.wait_ge(wt_done, upto(b, 1, 1))
                pe.wait_ge(*bank_read(b, ("WB", t)))
                mm(bank(b, ("WB", t))[:, :], sel16[:, t * P:(t + 1) * P], wt[:, :], start=True,
                   stop=True).then_inc(work_full, 1)

            def output(b, t):
                pe.wait_ge(a_lo, upto(b, NP_, t + 1))
                for m in range(KD):
                    mc = slice(m * P, (m + 1) * P)
                    ins = products(acc[m][:, :], ([wo_h[:, t, mc]], [wo_l[:, t, mc]]),
                                   ([ah[:, t % 2, :]], [al[:, t % 2, :]]), first=False, last=(t == NP_ - 1))
                ins.then_inc(out_mm, 1)

            def ahead(b, kind, n):
                if kind == "X":
                    turn_tokens(b, n)
                elif kind == "R":
                    router(b, n)
                elif kind == "QK":
                    project(b, (kind, n), n, 0, QK_W)
                else:
                    pe.wait_ge(route_step, upto(b, ROUTE_STEPS, ROUTE_STEPS))
                    turn_small(b, ("CT", 0), cst)

            pe.wait_ge(small_loaded, SMALL)
            pe.wait_ge(set_done, 4)
            for kind, n in FIRST:
                if (kind, n) == ("QK", 0):
                    pe.wait_ge(lo_done, len(cuts["wa"]))
                ahead(0, kind, n)
            pe.wait_ge(lo_done, len(pieces))

            def body(b, last):
                for kind, n in pe_order():
                    if kind == "V":
                        project(b, (kind, n), n // 2, V_AT + (n % 2) * T, T)
                    elif kind == "T":
                        turn_qk(b, n)
                    elif kind == "S":
                        scores(b, n)
                    elif kind == "AV":
                        values(b, n)
                    elif kind == "N":
                        head_sums(b, n)
                    elif kind in "cgud":
                        item(b, kind, n)
                    elif kind == "G":
                        gates(b, n)
                    elif kind == "WT":
                        pe.wait_ge(an_step, upto(b, HEAD_STEPS, HEAD_STEPS))
                        turn_small(b, ("WT", 0), wst)
                    elif kind == "WB":
                        spread(b, n)
                    elif kind == "O":
                        output(b, n)
                    elif kind in AHEAD and not last:
                        ahead(b + 1, kind, n)

            rounds(pe, body)


_OUT = (B, D, T)


def kernel(L0_attn_tokens, L0_attn_Wqg, L0_attn_Wkv, L0_attn_Wout, L0_ffn_router_weight, L0_ffn_e_bias,
           L0_ffn_gate_w, L0_ffn_up_w, L0_ffn_down_w, L0_ffn_sh_gate_w, L0_ffn_sh_up_w, L0_ffn_sh_down_w):
    import numpy as np
    import concourse.bacc as bacc
    from concourse.bass_utils import run_bass_kernel_spmd

    asc = np.ascontiguousarray
    tokens = np.asarray(L0_attn_tokens)
    wqg = np.asarray(L0_attn_Wqg).reshape(D, H, DK + DV)
    wkv = np.asarray(L0_attn_Wkv).reshape(D, H, DK + DV)
    wa = np.concatenate([wqg[:, :, :DK].reshape(D, -1), wkv[:, :, :DK].reshape(D, -1),
                         wkv[:, :, DK:].reshape(D, -1), wqg[:, :, DK:].reshape(D, -1)], axis=1)

    def rows(routed, shared):
        return asc(np.concatenate([np.asarray(routed).reshape(E * P, D), np.asarray(shared)], axis=0).T)

    down = np.concatenate([np.asarray(L0_ffn_down_w).transpose(2, 0, 1),
                           np.asarray(L0_ffn_sh_down_w).reshape(D, ES, P).transpose(2, 1, 0)], axis=1)
    sel = np.zeros((2, H, H, DV), np.float16)
    for h in range(H):
        sel[:, h, h, :] = 1.0
    tri = np.tril(np.ones((NG, NG), np.float32), -1).reshape(1, -1)
    arrays = {
        "x": tokens,
        "x_t": asc(tokens.transpose(0, 2, 1)),
        "wa": asc(wa),
        "w_gate": rows(L0_ffn_gate_w, L0_ffn_sh_gate_w),
        "w_up": rows(L0_ffn_up_w, L0_ffn_sh_up_w),
        "w_down": asc(down),
        "w_out": asc(np.asarray(L0_attn_Wout).reshape(NP_, P, D).transpose(1, 0, 2)),
        "w_router": asc(np.asarray(L0_ffn_router_weight).T),
        "bias": asc(np.broadcast_to(np.asarray(L0_ffn_e_bias), (P, E))),
        "ident": np.eye(P, dtype=np.float32),
        "ident_h": np.eye(P, dtype=np.float16),
        "sel": sel.reshape(2 * H, H * DV),
        "tri": asc(np.broadcast_to(tri, (P, NG * NG))),
    }
    nc = bacc.Bacc("TRN2", target_bir_lowering=False, num_devices=1)
    args = [nc.dram_tensor(n, a.shape, mybir.dt.from_np(a.dtype), kind="ExternalInput").ap() for n, a in arrays.items()]
    out = nc.dram_tensor("out_t", _OUT, F32, kind="ExternalOutput").ap()
    build_layer(nc, *args, out)
    r = run_bass_kernel_spmd(nc, [arrays], core_ids=[0])
    return asc(r.results[0]["out_t"].transpose(0, 2, 1))
```
